# Optimizing a Trainium2 kernel written in Bass

```python
import numpy as np
import jax
import jax.numpy as jnp

def _softmax(x, axis=-1):
    return jax.nn.softmax(x, axis=axis)

def _gelu(x):
    return jax.nn.gelu(x, approximate=True)

def _silu(x):
    return jax.nn.silu(x)

def _sigmoid(x):
    return jax.nn.sigmoid(x)

def _layernorm(x, axis=-1, eps=1e-05):
    m = jnp.mean(x, axis=axis, keepdims=True)
    v = jnp.var(x, axis=axis, keepdims=True)
    return (x - m) / jnp.sqrt(v + eps)

def _scatter_add(tgt, idx, src, axis=0):
    return tgt.at[idx].add(src)

def _segment_sum(src, seg, n):
    return jax.ops.segment_sum(src, seg, n)
kernel_name = 'mk_xattn_ffn_d2_seqx_r8_2c94a7'

def setup_inputs(seed: int=0):
    np.random.seed(seed)
    _w = jnp.asarray

    def _rec_inputs():
        import jax
        import jax.numpy as jnp
        _rk = jax.random.key(seed)
        x = -0.0002928 + 1 * jax.random.normal(jax.random.fold_in(_rk, 1), (32, 128, 128), jnp.float32)
        _lenS = 128 - jax.random.randint(jax.random.fold_in(_rk, 7), (32,), 0, max(1, 128 // 4) + 1, jnp.int32)
        _lenS2 = 128 - jax.random.randint(jax.random.fold_in(_rk, 8), (32,), 0, max(1, 128 // 4) + 1, jnp.int32)
        _ctx_1024P = jax.random.normal(jax.random.fold_in(_rk, 11), (32, 16, 128), jnp.float32)
        _ctx_1024c = jax.random.dirichlet(jax.random.fold_in(_rk, 511), 0.3 * jnp.ones((16,), jnp.float32), (32, 128))
        _ctx_1024t = jnp.einsum('bsk,bkd->bsd', _ctx_1024c, _ctx_1024P)
        _ctx_1024t = _ctx_1024t * jax.lax.rsqrt(jnp.mean(jnp.square(_ctx_1024t)) + 1e-12) * 0.953939
        ctx_1024 = -1.39393e-06 + 0.999914 * (_ctx_1024t + 0.3 * jax.random.normal(jax.random.fold_in(_rk, 611), (32, 128, 128), jnp.float32))
        return (x, ctx_1024)
    x, ctx_1024 = _rec_inputs()

    def _L0_xattn_setup():
        import jax, jax.numpy as jnp
        import numpy as np
        B, S, D, H = (2, 256, 128, 16)
        DK = D // H
        key = jax.random.key(seed)
        ks = jax.random.split(key, 11)
        sc = 1.0 / np.sqrt(D)
        return {'q': jax.random.normal(ks[0], (B, S, D), jnp.float32), 'k': jax.random.normal(ks[1], (B, S, D), jnp.float32), 'v': jax.random.normal(ks[2], (B, S, D), jnp.float32), 'Wq': jax.random.normal(ks[3], (D, D), jnp.float32) * sc, 'bq': jax.random.normal(ks[4], (D,), jnp.float32) * sc, 'Wk': jax.random.normal(ks[5], (D, D), jnp.float32) * sc, 'bk': jax.random.normal(ks[6], (D,), jnp.float32) * sc, 'Wv': jax.random.normal(ks[7], (D, D), jnp.float32) * sc, 'bv': jax.random.normal(ks[8], (D,), jnp.float32) * sc, 'Wo': jax.random.normal(ks[9], (D, D), jnp.float32) * sc, 'bo': jax.random.normal(ks[10], (D,), jnp.float32) * sc}
    _L0_xattn_all = _L0_xattn_setup()
    _L0_xattn_in = {k: v for k, v in _L0_xattn_all.items() if k in ('Wq', 'bq', 'Wk', 'bk', 'Wv', 'bv', 'Wo', 'bo')}
    del _L0_xattn_all

    def _L0_ffn_setup():
        import jax, jax.numpy as jnp
        import numpy as np
        QMAX = 127.0

        def _ste_round(v):
            return v + jax.lax.stop_gradient(jnp.round(v) - v)

        def _act_fake_quant(x, clip_factor):
            scale = jax.nn.sigmoid(clip_factor) * jnp.max(jnp.abs(x)) / QMAX
            return jnp.clip(_ste_round(x / scale), -QMAX - 1.0, QMAX) * scale

        def _weight_fake_quant(w):
            scale = jnp.max(jnp.abs(w), axis=1, keepdims=True) / QMAX
            return jnp.clip(_ste_round(w / scale), -QMAX - 1.0, QMAX) * scale
        key = jax.random.key(seed)
        k1, k2, k3, k4 = jax.random.split(key, 4)
        B, S, H, I = (8, 1024, 128, 352)
        return {'x': jax.random.normal(k1, (B, S, H), dtype=jnp.float32), 'clip_x': jnp.full((1,), 4.0, dtype=jnp.float32), 'clip_down': jnp.full((1,), 4.0, dtype=jnp.float32), 'w_gate': jax.random.normal(k2, (I, H), dtype=jnp.float32) * 0.02, 'w_up': jax.random.normal(k3, (I, H), dtype=jnp.float32) * 0.02, 'w_down': jax.random.normal(k4, (H, I), dtype=jnp.float32) * 0.02}
    _L0_ffn_all = _L0_ffn_setup()
    _L0_ffn_in = {k: v for k, v in _L0_ffn_all.items() if k in ('clip_x', 'clip_down', 'w_gate', 'w_up', 'w_down')}
    del _L0_ffn_all

    def _L1_xattn_setup():
        import jax, jax.numpy as jnp
        import numpy as np
        EMBED_PHI = 128
        EMBED_F = 128
        HIDDEN_F = 128
        N_HEADS = 16
        B, S = (2, 256)
        key = jax.random.key(seed)
        ks = jax.random.split(key, 9)
        sphi = 1.0 / np.sqrt(EMBED_PHI)
        sf = 1.0 / np.sqrt(EMBED_F)
        sh = 1.0 / np.sqrt(HIDDEN_F)
        return {'q': jax.random.normal(ks[0], (B, S, EMBED_PHI), jnp.float32), 'k': jax.random.normal(ks[1], (B, S, EMBED_PHI), jnp.float32), 'v': jax.random.normal(ks[2], (B, S, EMBED_F), jnp.float32), 'Wq': jax.random.normal(ks[3], (HIDDEN_F, EMBED_PHI), jnp.float32) * sphi, 'Wk': jax.random.normal(ks[4], (HIDDEN_F, EMBED_PHI), jnp.float32) * sphi, 'Wv': jax.random.normal(ks[5], (HIDDEN_F, EMBED_F), jnp.float32) * sf, 'bv': jax.random.normal(ks[6], (HIDDEN_F,), jnp.float32) * sf, 'Wo': jax.random.normal(ks[7], (EMBED_F, HIDDEN_F), jnp.float32) * sh, 'bo': jax.random.normal(ks[8], (EMBED_F,), jnp.float32) * sh}
    _L1_xattn_all = _L1_xattn_setup()
    _L1_xattn_in = {k: v for k, v in _L1_xattn_all.items() if k in ('Wq', 'Wk', 'Wv', 'bv', 'Wo', 'bo')}
    del _L1_xattn_all

    def _L1_ffn_setup():
        import jax, jax.numpy as jnp
        import numpy as np
        from jax import lax
        H = 128
        I = 128
        E = 16
        TOP_K = 4

        def _swiglu(x, wg, wd, wu):
            return jax.nn.silu(x @ wg.T) * (x @ wu.T) @ wd.T
        key = jax.random.key(seed)
        ks = jax.random.split(key, 9)
        std_gate = 0.02 / E ** 0.5
        return {'hidden_states': jax.random.normal(ks[0], (1, 256, H), jnp.float32), 'gate_w': jax.random.normal(ks[1], (E, H), jnp.float32) * std_gate, 'expert_bias': jnp.zeros((E,), jnp.float32), 'w1': jax.random.normal(ks[2], (E, I, H), jnp.float32) * 0.02, 'w2': jax.random.normal(ks[3], (E, H, I), jnp.float32) * 0.02, 'w3': jax.random.normal(ks[4], (E, I, H), jnp.float32) * 0.02, 'sw1': jax.random.normal(ks[5], (I, H), jnp.float32) * 0.02, 'sw2': jax.random.normal(ks[6], (H, I), jnp.float32) * 0.02, 'sw3': jax.random.normal(ks[7], (I, H), jnp.float32) * 0.02}
    _L1_ffn_all = _L1_ffn_setup()
    _L1_ffn_in = {k: v for k, v in _L1_ffn_all.items() if k in ('gate_w', 'expert_bias', 'w1', 'w2', 'w3', 'sw1', 'sw2', 'sw3')}
    del _L1_ffn_all
    return {'x': x, 'ctx_1024': ctx_1024, 'L0_xattn_Wq': _L0_xattn_in['Wq'], 'L0_xattn_bq': _L0_xattn_in['bq'], 'L0_xattn_Wk': _L0_xattn_in['Wk'], 'L0_xattn_bk': _L0_xattn_in['bk'], 'L0_xattn_Wv': _L0_xattn_in['Wv'], 'L0_xattn_bv': _L0_xattn_in['bv'], 'L0_xattn_Wo': _L0_xattn_in['Wo'], 'L0_xattn_bo': _L0_xattn_in['bo'], 'L0_ffn_clip_x': _L0_ffn_in['clip_x'], 'L0_ffn_clip_down': _L0_ffn_in['clip_down'], 'L0_ffn_w_gate': _L0_ffn_in['w_gate'], 'L0_ffn_w_up': _L0_ffn_in['w_up'], 'L0_ffn_w_down': _L0_ffn_in['w_down'], 'L1_xattn_Wq': _L1_xattn_in['Wq'], 'L1_xattn_Wk': _L1_xattn_in['Wk'], 'L1_xattn_Wv': _L1_xattn_in['Wv'], 'L1_xattn_bv': _L1_xattn_in['bv'], 'L1_xattn_Wo': _L1_xattn_in['Wo'], 'L1_xattn_bo': _L1_xattn_in['bo'], 'L1_ffn_gate_w': _L1_ffn_in['gate_w'], 'L1_ffn_expert_bias': _L1_ffn_in['expert_bias'], 'L1_ffn_w1': _L1_ffn_in['w1'], 'L1_ffn_w2': _L1_ffn_in['w2'], 'L1_ffn_w3': _L1_ffn_in['w3'], 'L1_ffn_sw1': _L1_ffn_in['sw1'], 'L1_ffn_sw2': _L1_ffn_in['sw2'], 'L1_ffn_sw3': _L1_ffn_in['sw3']}

def reference(x, ctx_1024, L0_xattn_Wq, L0_xattn_bq, L0_xattn_Wk, L0_xattn_bk, L0_xattn_Wv, L0_xattn_bv, L0_xattn_Wo, L0_xattn_bo, L0_ffn_clip_x, L0_ffn_clip_down, L0_ffn_w_gate, L0_ffn_w_up, L0_ffn_w_down, L1_xattn_Wq, L1_xattn_Wk, L1_xattn_Wv, L1_xattn_bv, L1_xattn_Wo, L1_xattn_bo, L1_ffn_gate_w, L1_ffn_expert_bias, L1_ffn_w1, L1_ffn_w2, L1_ffn_w3, L1_ffn_sw1, L1_ffn_sw2, L1_ffn_sw3):
    import jax
    import jax.numpy as jnp

    def _L0_xattn_ref(q, k, v, Wq, bq, Wk, bk, Wv, bv, Wo, bo):
        import jax, jax.numpy as jnp
        import numpy as np
        B, S, D, H = (2, 256, 128, 16)
        DK = D // H
        b, s, d = q.shape
        qh = (q @ Wq.T + bq).reshape(b, s, H, DK).transpose(0, 2, 1, 3)
        kh = (k @ Wk.T + bk).reshape(b, s, H, DK).transpose(0, 2, 1, 3)
        vh = (v @ Wv.T + bv).reshape(b, s, H, DK).transpose(0, 2, 1, 3)
        scores = jnp.einsum('bhqd,bhkd->bhqk', qh, kh) / jnp.sqrt(jnp.float32(DK))
        attn = jax.nn.softmax(scores, axis=-1)
        out = jnp.einsum('bhqk,bhkd->bhqd', attn, vh)
        out = out.transpose(0, 2, 1, 3).reshape(b, s, d)
        return out @ Wo.T + bo

    def _L0_ffn_ref(x, clip_x, clip_down, w_gate, w_up, w_down):
        import jax, jax.numpy as jnp
        import numpy as np
        QMAX = 127.0

        def _ste_round(v):
            return v + jax.lax.stop_gradient(jnp.round(v) - v)

        def _act_fake_quant(x, clip_factor):
            scale = jax.nn.sigmoid(clip_factor) * jnp.max(jnp.abs(x)) / QMAX
            return jnp.clip(_ste_round(x / scale), -QMAX - 1.0, QMAX) * scale

        def _weight_fake_quant(w):
            scale = jnp.max(jnp.abs(w), axis=1, keepdims=True) / QMAX
            return jnp.clip(_ste_round(w / scale), -QMAX - 1.0, QMAX) * scale
        xq = _act_fake_quant(x, clip_x[0])
        gate = jnp.einsum('bsh,ih->bsi', xq, _weight_fake_quant(w_gate))
        up = jnp.einsum('bsh,ih->bsi', xq, _weight_fake_quant(w_up))
        h = _act_fake_quant(jax.nn.silu(gate) * up, clip_down[0])
        return jnp.einsum('bsi,hi->bsh', h, _weight_fake_quant(w_down))

    def _L1_xattn_ref(q, k, v, Wq, Wk, Wv, bv, Wo, bo):
        import jax, jax.numpy as jnp
        import numpy as np
        EMBED_PHI = 128
        EMBED_F = 128
        HIDDEN_F = 128
        N_HEADS = 16
        B, S = (2, 256)
        Bq, Sq, _ = q.shape
        hd = HIDDEN_F // N_HEADS
        scale = 1.0 / np.sqrt(hd)
        qh = (q @ Wq.T).reshape(Bq, Sq, N_HEADS, hd).transpose(0, 2, 1, 3)
        kh = (k @ Wk.T).reshape(Bq, Sq, N_HEADS, hd).transpose(0, 2, 1, 3)
        vh = (v @ Wv.T + bv).reshape(Bq, Sq, N_HEADS, hd).transpose(0, 2, 1, 3)
        scores = jnp.einsum('bhsd,bhtd->bhst', qh, kh) * scale
        mask = jnp.triu(jnp.ones((Sq, Sq), dtype=bool), k=0).at[0, 0].set(False)
        scores = jnp.where(mask, -jnp.inf, scores)
        probs = jax.nn.softmax(scores, axis=-1)
        out = jnp.einsum('bhst,bhtd->bhsd', probs, vh)
        out = out.transpose(0, 2, 1, 3).reshape(Bq, Sq, HIDDEN_F)
        return out @ Wo.T + bo

    def _L1_ffn_ref(hidden_states, gate_w, expert_bias, w1, w2, w3, sw1, sw2, sw3):
        import jax, jax.numpy as jnp
        import numpy as np
        from jax import lax
        H = 128
        I = 128
        E = 16
        TOP_K = 4

        def _swiglu(x, wg, wd, wu):
            return jax.nn.silu(x @ wg.T) * (x @ wu.T) @ wd.T
        B, S, Hd = hidden_states.shape
        x = hidden_states.reshape(-1, Hd)
        T = x.shape[0]
        router_logits = x @ gate_w.T
        biased = router_logits + expert_bias
        _, sel = lax.top_k(biased, TOP_K)
        raw = jnp.take_along_axis(router_logits, sel, axis=-1)
        rw = jax.nn.softmax(raw.astype(jnp.float32), axis=-1).astype(x.dtype)
        g = jnp.zeros((T, E), x.dtype).at[jnp.arange(T)[:, None], sel].add(rw)
        routed = jnp.zeros_like(x)
        for e in range(E):
            routed = routed + g[:, e:e + 1] * _swiglu(x, w1[e], w2[e], w3[e])
        shared = _swiglu(x, sw1, sw2, sw3)
        out = (shared + routed).reshape(B, S, Hd)
        return out
    x = x + _L0_xattn_ref(_layernorm(x, axis=-1), ctx_1024, ctx_1024, L0_xattn_Wq, L0_xattn_bq, L0_xattn_Wk, L0_xattn_bk, L0_xattn_Wv, L0_xattn_bv, L0_xattn_Wo, L0_xattn_bo)
    x = x + _L0_ffn_ref(_layernorm(x, axis=-1), L0_ffn_clip_x, L0_ffn_clip_down, L0_ffn_w_gate, L0_ffn_w_up, L0_ffn_w_down)
    x = x + _L1_xattn_ref(_layernorm(x, axis=-1), ctx_1024, ctx_1024, L1_xattn_Wq, L1_xattn_Wk, L1_xattn_Wv, L1_xattn_bv, L1_xattn_Wo, L1_xattn_bo)
    x = x + _L1_ffn_ref(_layernorm(x, axis=-1), L1_ffn_gate_w, L1_ffn_expert_bias, L1_ffn_w1, L1_ffn_w2, L1_ffn_w3, L1_ffn_sw1, L1_ffn_sw2, L1_ffn_sw3)
    return x

_drawn_inputs = setup_inputs


def setup_inputs(seed=0):
    import zlib

    import numpy as np

    out = dict(_drawn_inputs(seed))
    spreads = {'L1_ffn_expert_bias': (0.0, 0.8)}
    factors = {'L0_xattn_bq': 3.372,
     'L0_xattn_bk': 8.0,
     'L0_ffn_w_gate': 7.238,
     'L0_ffn_w_up': 7.047,
     'L0_ffn_w_down': 7.074,
     'L1_ffn_gate_w': 8.0,
     'L1_ffn_w1': 8.0,
     'L1_ffn_w2': 8.0,
     'L1_ffn_w3': 8.0,
     'L1_ffn_sw1': 8.0,
     'L1_ffn_sw2': 8.0,
     'L1_ffn_sw3': 8.0}
    for name, (base, spread) in spreads.items():
        noise = np.random.default_rng([zlib.crc32(name.encode()), seed]).standard_normal(out[name].shape)
        drawn = base * np.exp(spread * noise) if base else spread * noise
        out[name] = jnp.asarray(drawn.astype(out[name].dtype))
    for name, factor in factors.items():
        out[name] = (out[name] * factor).astype(out[name].dtype)
    return out
```

```python
from contextlib import ExitStack, contextmanager

import concourse.bass as bass
from concourse import mybir

F32 = mybir.dt.float32
F16 = mybir.dt.float16
BF16 = mybir.dt.bfloat16
ALU = mybir.AluOpType
ACT = mybir.ActivationFunctionType
AX = mybir.AxisListType
ABSMAX = bass.bass_isa.ReduceOp.absmax

P = 128
B = 32
S = 128
D = 128
H = 16
DK = D // H
HG = 4
NG = H // HG
CB = 4
CT = CB * S
NC = B // CB
NT = B * S
INNER = 352
ROWS = [128, 128, 96]
NI = len(ROWS)
E = 16
TOPK = 4
R = HG * DK
MROW = 3 * R
VW = DK + 1
SCALE = float(DK) ** -0.5
MSCALE = 1024.0
EPS = 1e-5
QMAX = 127.0
MAGIC = 12582912.0
BIG = 1e30


@contextmanager
def every(eng, first, end, step):
    with eng.Fori(0, (end - first) // step) as n:
        yield n * step + first


def span(n, size):
    return slice(n * size, (n + 1) * size) if isinstance(n, int) else bass.ds(n * size, size)


def build(nc, x, ctxT, w, consts, outT):
    ds = bass.ds
    with ExitStack() as top:
        def sb(name, shape, dt=F32):
            return top.enter_context(nc.sbuf_tensor(name, shape, dt))

        def sem(name):
            return top.enter_context(nc.semaphore(name))

        X = sb("X", [P, B, D])
        XNT = sb("XNT", [P, NT])
        STATS = sb("STATS", [P, B, 6])
        MEAN = sb("MEAN", [P, B])
        RSTD = sb("RSTD", [P, B])
        tmpB = sb("tmpB", [P, 4, B])
        identf = sb("identf", [P, P])
        identb = sb("identb", [P, P], BF16)
        maskS = sb("maskS", [P, HG, P], BF16)
        maskT = sb("maskT", [P, HG, P], BF16)
        onesf = sb("onesf", [P, P])
        WQ = sb("WQ", [P, 2, D])
        WK = sb("WK", [P, 2, D])
        WV = sb("WV", [P, 2, D])
        WO = sb("WO", [P, 2, D])
        bqk = sb("bqk", [P, 2, 2])
        bvc = sb("bvc", [P, 2])
        bor = sb("bor", [1, 2, D])
        BVW = sb("BVW", [P, 2, D])
        BO = sb("BO", [P, 2, D])

        ARENA = sb("ARENA", [P, 20480])
        HBUF = sb("HBUF", [P, NI, NT])
        half = ARENA[:, :].bitcast(F16)
        QD = [half[:, n * 8192:(n + 1) * 8192].rearrange("p (g h t) -> p g h t", g=NG, h=HG) for n in (0, 1)]
        KD = [half[:, n * 8192:(n + 1) * 8192].rearrange("p (g h t) -> p g h t", g=NG, h=HG) for n in (2, 3)]
        QP = [half[:, 32768 + n * 2048:32768 + (n + 1) * 2048].rearrange("p (g t) -> p g t", g=NG) for n in (0, 1)]
        KP = [half[:, 36864 + n * 2048:36864 + (n + 1) * 2048].rearrange("p (g t) -> p g t", g=NG) for n in (0, 1)]

        bank = [top.enter_context(nc.psum_tensor(f"bank{n}", [P, 512], F32)) for n in range(8)]

        s_w = sem("weights_loaded")
        n_w = 0
        s_z = sem("arena_zeroed")
        zeroed = [0]

        def ln_stats(tag):
            step = sem(f"ln_step_{tag}")
            with nc.Block() as block:
                @block.vector
                def _(dve):
                    me, mo = STATS[:, :, 1], STATS[:, :, 4]
                    ve, vo = STATS[:, :, 2], STATS[:, :, 5]
                    nc.vector.tensor_tensor(tmpB[:, 0, :], me, mo, ALU.add)
                    nc.vector.tensor_tensor(tmpB[:, 1, :], me, mo, ALU.subtract)
                    nc.vector.tensor_tensor(tmpB[:, 2, :], ve, vo, ALU.add).then_inc(step, 1)
                    dve.wait_ge(step, 1)
                    nc.vector.tensor_scalar(MEAN[:, :], tmpB[:, 0, :], 0.5, None, ALU.mult)
                    nc.vector.tensor_scalar(tmpB[:, 2, :], tmpB[:, 2, :], 1.0 / D, EPS, ALU.mult, ALU.add)
                    nc.vector.tensor_tensor(tmpB[:, 1, :], tmpB[:, 1, :], tmpB[:, 1, :], ALU.mult).then_inc(step, 1)
                    dve.wait_ge(step, 2)
                    nc.vector.scalar_tensor_tensor(tmpB[:, 3, :], tmpB[:, 1, :], 0.25, tmpB[:, 2, :],
                                                   ALU.mult, ALU.add).then_inc(step, 1)
                    dve.wait_ge(step, 3)
                    dve.wait_ge(step, 4)
                    nc.vector.reciprocal(RSTD[:, :], tmpB[:, 0, :]).then_inc(step, 1)
                    dve.wait_ge(step, 5)
                    nc.vector.tensor_tensor(tmpB[:, 1, :], RSTD[:, :], RSTD[:, :], ALU.mult).then_inc(step, 1)
                    dve.wait_ge(step, 6)
                    nc.vector.tensor_tensor(tmpB[:, 1, :], tmpB[:, 1, :], tmpB[:, 3, :], ALU.mult).then_inc(step, 1)
                    dve.wait_ge(step, 7)
                    nc.vector.tensor_scalar(tmpB[:, 1, :], tmpB[:, 1, :], -0.5, 1.5, ALU.mult, ALU.add).then_inc(step, 1)
                    dve.wait_ge(step, 8)
                    nc.vector.tensor_tensor(RSTD[:, :], tmpB[:, 1, :], RSTD[:, :], ALU.mult).then_inc(step, 1)
                    dve.wait_ge(step, 9)

                @block.scalar
                def _(act):
                    act.wait_ge(step, 3)
                    nc.scalar.activation(tmpB[:, 0, :], tmpB[:, 3, :], ACT.Sqrt).then_inc(step, 1)

        def ln_transpose(tag, XN):
            normed, turned, kept = sem(f"normed_{tag}"), sem(f"turned_{tag}"), sem(f"xnt_kept_{tag}")
            FREE = 2
            with nc.Block() as block:
                @block.vector
                def _(dve):
                    with every(dve, 0, NC, 2) as c:
                        for u in range(2):
                            dve.wait_ge(turned, c + u + 1)
                            for j in range(CB):
                                b = c * CB + (u * CB + j)
                                ins = nc.vector.tensor_scalar(XN[:, u, j, :], X[:, ds(b, 1), :], MEAN[:, ds(b, 1)],
                                                              RSTD[:, ds(b, 1)], ALU.subtract, ALU.mult)
                            ins.then_inc(normed, 1)

                @block.tensor
                def _(pe):
                    pe.sem_inc(turned, FREE)
                    with every(pe, 0, NC, 2) as c:
                        for u in range(2):
                            pe.wait_ge(normed, c + u + 1)
                            pe.wait_ge(kept, c + u + 1)
                            for j in range(CB):
                                ins = nc.tensor.transpose(bank[u][:, j * S:(j + 1) * S], XN[:, u, j, :], identf[:, :])
                            ins.then_inc(turned, 1)

                @block.scalar
                def _(act):
                    act.sem_inc(kept, FREE)
                    with every(act, 0, NC, 2) as c:
                        for u in range(2):
                            act.wait_ge(turned, c + u + 1 + FREE)
                            nc.scalar.copy(XNT[:, ds((c + u) * CT, CT)], bank[u][:, :]).then_inc(kept, 1)

        def projections(L, qk, vs):
            t = f"L{L}"
            with ExitStack() as own:
                CX = own.enter_context(nc.sbuf_tensor(f"CX{L}", [P, 2, CT], F32))
                HL = own.enter_context(nc.sbuf_tensor(f"HL{L}", [P, 2, 4, CT], F16))
                VS = own.enter_context(nc.sbuf_tensor(f"VS{L}", [P, 2, CB * H, VW], F32))
                cx_in = [sem(f"ctx_loaded{u}_{t}") for u in range(2)]
                q_mm, k_mm, v_mm = sem(f"q_mm_{t}"), sem(f"k_mm_{t}"), sem(f"v_mm_{t}")
                hi, lo, vc = sem(f"hi_made_{t}"), sem(f"lo_made_{t}"), sem(f"v_copied_{t}")
                stored = [sem(f"qkv_stored{u}_{t}") for u in range(2)]
                ones, xb = sem(f"ones_set_{t}"), sem(f"bias_added_{t}")
                FREE = 2
                with nc.Block() as block:
                    @block.gpsimd
                    def _(pool):
                        nc.gpsimd.memset(VS[:, :, :, :], 1.0).then_inc(ones, 1)
                        nc.gpsimd.tensor_tensor(X[:, :, :], X[:, :, :],
                                                BO[:, L, :].unsqueeze(1).to_broadcast([P, B, D]),
                                                ALU.add).then_inc(xb, 1)
                        pool.wait_ge(xb, 1)

                    def store(sp, c, u):
                        sp.wait_ge(lo, (c + u) * 2 + (2 + 2 * FREE))
                        for n in range(4):
                            sp.dma_start(qk[n, :, ds((c + u) * CT, CT)], HL[:, u, n, :]).then_inc(stored[u], 16)
                        sp.wait_ge(vc, c + (u + 1 + FREE))
                        sp.dma_start(vs[:, ds((c + u) * (CB * H * VW), CB * H * VW)],
                                     VS[:, u, :, :]).then_inc(stored[u], 16)

                    @block.sync
                    def _(sp):
                        for u in range(2):
                            sp.dma_start(CX[:, u, :], ctxT[:, u * CT:(u + 1) * CT]).then_inc(cx_in[u], 16)
                        with every(sp, 0, NC - 2, 2) as c:
                            for u in range(2):
                                sp.wait_ge(v_mm, c + (u + 1))
                                sp.dma_start(CX[:, u, :], ctxT[:, ds((c + (u + 2)) * CT, CT)]).then_inc(cx_in[u], 16)
                                store(sp, c, u)
                        for u in range(2):
                            store(sp, NC - 2, u)
                        for u in range(2):
                            sp.wait_ge(stored[u], 16 * 5 * (NC // 2 + 1))

                    @block.tensor
                    def _(pe):
                        with every(pe, 0, NC, 2) as c:
                            for u in range(2):
                                pe.wait_ge(lo, (c + u) * 2 + 2)
                                nc.tensor.matmul(bank[4 * u][:, :], WQ[:, L, :], XNT[:, ds((c + u) * CT, CT)],
                                                 start=True, stop=True).then_inc(q_mm, 1)
                                pe.wait_ge(cx_in[u], c * 8 + 16)
                                nc.tensor.matmul(bank[4 * u + 1][:, :], WK[:, L, :], CX[:, u, :],
                                                 start=True, stop=True).then_inc(k_mm, 1)
                                pe.wait_ge(vc, c + (u + 1))
                                for j in range(CB):
                                    ins = nc.tensor.matmul(bank[4 * u + 2][:, j * D:(j + 1) * D],
                                                           CX[:, u, j * S:(j + 1) * S], WV[:, L, :],
                                                           start=True, stop=True)
                                ins.then_inc(v_mm, 1)

                    @block.scalar
                    def _(act):
                        act.sem_inc(vc, FREE)
                        for u in range(2):
                            act.sem_inc(stored[u], 16 * 5)
                        act.wait_ge(ones, 1)
                        with every(act, 0, NC, 2) as c:
                            for u in range(2):
                                act.wait_ge(stored[u], c * (16 * 5 // 2) + 16 * 5)
                                act.wait_ge(q_mm, c + (u + 1))
                                nc.scalar.activation(HL[:, u, 0, :], bank[4 * u][:, :], ACT.Identity,
                                                     bias=bqk[:, L, 0:1]).then_inc(hi, 1)
                                act.wait_ge(k_mm, c + (u + 1))
                                nc.scalar.activation(HL[:, u, 2, :], bank[4 * u + 1][:, :], ACT.Identity,
                                                     bias=bqk[:, L, 1:2]).then_inc(hi, 1)
                                act.wait_ge(v_mm, c + (u + 1))
                                nc.scalar.copy(VS[:, u, :, 0:DK],
                                               bank[4 * u + 2][:, :].rearrange("p (m d) -> p m d", d=DK)).then_inc(vc, 1)

                    @block.vector
                    def _(dve):
                        dve.sem_inc(lo, 2 * FREE)
                        with every(dve, 0, NC, 2) as c:
                            for u in range(2):
                                for n in range(2):
                                    dve.wait_ge(hi, (c + u) * 2 + (n + 1))
                                    nc.vector.scalar_tensor_tensor(
                                        HL[:, u, 2 * n + 1, :], bank[4 * u + n][:, :], bqk[:, L, n:n + 1],
                                        HL[:, u, 2 * n, :], ALU.add, ALU.subtract).then_inc(lo, 1)

        def attention(L, qk, vs):
            t = f"L{L}"
            causal = L == 1
            with ExitStack() as own:
                def osb(name, shape, dt=F32):
                    return own.enter_context(nc.sbuf_tensor(f"{name}{L}", shape, dt))
                VR = osb("VR", [P, 2, CB, H, VW])
                M = osb("M", [P, 2, H])
                MT = osb("MT", [H, 2, S], F16)
                PT = osb("PT", [P, 4, HG * S])
                OT = osb("OT", [P, 2, HG * S])
                REC = osb("REC", [P, 2, H])
                OQ = osb("OQ", [P, 2, D])
                OF = osb("OF", [P, 2, S])
                max_in = [sem(f"maxima_operands_loaded{u}_{t}") for u in range(2)]
                prob_in = [sem(f"probs_operands_loaded{u}_{t}") for u in range(2)]
                s_mm, maxed = sem(f"scores_ready_{t}"), sem(f"maxima_taken_{t}")
                m_turned, m_kept = sem(f"maxima_turned_{t}"), sem(f"maxima_kept_{t}")
                m_in = [sem(f"maxima_row_loaded{u}_{t}") for u in range(2)]
                st_mm, exped = sem(f"scores_T_ready_{t}"), sem(f"probs_ready_{t}")
                pv = sem(f"pv_done_{t}")
                ot_kept, turned = sem(f"out_T_kept_{t}"), sem(f"out_turned_{t}")
                recd, normed = sem(f"denominators_inverted_{t}"), sem(f"out_normalised_{t}")
                of_turned, of_kept = sem(f"out_F_turned_{t}"), sem(f"out_F_kept_{t}")
                proj, added = sem(f"out_projected_{t}"), sem(f"residual_added_{t}")
                otz = sem(f"out_banks_zeroed_{t}")
                NMAX = 1 + HG
                NPROB = 3 + 3 * HG + 1
                STEPS = B + 5
                LO, HI = 6, 30

                def steps(eng, step):
                    for s in range(LO):
                        step(s, s, False)
                    with every(eng, LO, HI, 8) as s0:
                        for u in range(8):
                            step(s0 + u if u else s0, (LO + u) % 8, True)
                    for s in range(HI, STEPS):
                        step(s, s % 8, False)

                def alive(s, loop, lag):
                    return loop or 0 <= s - lag < B

                def wait(eng, semaphore, s, loop, scale, offset):
                    if loop or scale * s + offset > 0:
                        eng.wait_ge(semaphore, s * scale + offset)

                with nc.Block() as block:
                    @block.sync
                    def _(sp):
                        q_hi, q_lo, k_hi, k_lo = range(4)

                        def part_rows(n, c):
                            return qk[n].rearrange("(g r) t -> r g t", g=NG)[:, :, span(c, CT)]

                        def part_heads(n, c):
                            return qk[n].rearrange("(g h d) t -> h d g t", g=NG, h=HG)[:, :, :, span(c, CT)]

                        def load_maxima(c, u):
                            sp.dma_start(QP[u][0:R, :, :], part_rows(q_hi, c)).then_inc(max_in[u], 16)
                            for h in range(HG):
                                sp.dma_start(KD[u][DK * h:DK * (h + 1), :, h, :],
                                             part_heads(k_hi, c)[h]).then_inc(max_in[u], 16)

                        def load_probs(c, u):
                            for n, part in enumerate((k_hi, k_lo, k_hi)):
                                sp.dma_start(KP[u][R * n:R * (n + 1), :, :], part_rows(part, c)).then_inc(prob_in[u], 16)
                            for n, part in enumerate((q_hi, q_hi, q_lo)):
                                for h in range(HG):
                                    a = R * n + DK * h
                                    sp.dma_start(QD[u][a:a + DK, :, h, :], part_heads(part, c)[h]).then_inc(prob_in[u], 16)

                        def load_v(c, u):
                            sp.dma_start(VR[:, u].rearrange("p b h v -> p (b h v)"),
                                         vs[:, span(c, CB * H * VW)]).then_inc(prob_in[u], 16)

                        sp.wait_ge(s_z, 2)
                        for u in range(2):
                            load_maxima(u, u)
                            load_probs(u, u)
                            load_v(u, u)
                        with every(sp, 2, NC, 2) as c:
                            for u in range(2):
                                sp.wait_ge(s_mm, (c + (u - 1)) * (CB * NG))
                                load_maxima(c + u if u else c, u)
                                sp.wait_ge(st_mm, (c + (u - 1)) * (CB * NG))
                                load_probs(c + u if u else c, u)
                                sp.wait_ge(pv, (c + (u - 1)) * (CB * NG))
                                load_v(c + u if u else c, u)

                    @block.tensor
                    def _(pe):
                        def scores(s, r, loop, g):
                            u, tok = r // CB, slice(r % CB * S, (r % CB + 1) * S)
                            if g == 0 and r % CB == 0:
                                wait(pe, max_in[u], s, loop, 2 * NMAX, 16 * NMAX - 2 * NMAX * r)
                            wait(pe, maxed, s, loop, NG, g - 1)
                            out = bank[g % 2][:, :]
                            if causal:
                                nc.tensor.matmul(out, identb[:, :], maskS[:, :, :], start=True, stop=False)
                            nc.tensor.matmul(out, QP[u][0:MROW, g, tok], KD[u][0:MROW, g, :, tok],
                                             start=not causal, stop=True).then_inc(s_mm, 1)

                        def scores_T(s, r, loop, g):
                            u, tok = r // CB, slice(r % CB * S, (r % CB + 1) * S)
                            if g == 0:
                                if r % CB == 0:
                                    wait(pe, prob_in[u], s, loop, 2 * NPROB, 16 * NPROB - 2 * NPROB * r)
                                wait(pe, m_in[r % 2], s, loop, 8, 16 - 8 * (r % 2))
                            wait(pe, exped, s, loop, NG, g - 1)
                            out = bank[2 + g % 2][:, :]
                            if causal:
                                nc.tensor.matmul(out, identb[:, :], maskT[:, :, :], start=True, stop=False)
                            nc.tensor.matmul(out, KP[u][0:MROW + 1, g, tok], QD[u][0:MROW + 1, g, :, tok],
                                             start=not causal, stop=True).then_inc(st_mm, 1)

                        def turn_maxima(s, r, loop):
                            wait(pe, maxed, s, loop, NG, NG)
                            wait(pe, normed, s, loop, 1, -2)
                            nc.tensor.transpose(bank[6][0:H, 0:S], M[:, r % 2, :], identf[:, :]).then_inc(m_turned, 1)

                        def product_v(s, r, loop, g):
                            wait(pe, exped, s, loop, NG, g + 1)
                            if g == 0:
                                wait(pe, ot_kept, s, loop, 1, -1)
                            for h in range(HG):
                                ins = nc.tensor.matmul(bank[4 + r % 2][32 * h:32 * h + VW, g * S:(g + 1) * S],
                                                       VR[:, r // CB, r % CB, HG * g + h, :],
                                                       PT[:, g, h * S:(h + 1) * S], start=True, stop=True,
                                                       tile_position=(0, 32 * h))
                            ins.then_inc(pv, 1)

                        def turn_out(s, r, loop):
                            wait(pe, ot_kept, s, loop, 1, 1)
                            if loop or s + 2 < B:
                                pe.wait_ge(m_kept, s + 3)
                            wait(pe, normed, s, loop, 1, 0)
                            for g in range(NG):
                                ins = nc.tensor.transpose(bank[6][:, g * S:(g + 1) * S],
                                                          OT[:, r % 2, g * S:(g + 1) * S], identf[:, :])
                            ins.then_inc(turned, 1)

                        def turn_normed(s, r, loop):
                            wait(pe, normed, s, loop, 1, 1)
                            wait(pe, added, s, loop, 1, 0)
                            nc.tensor.transpose(bank[7][:, 0:S], OQ[:, r % 2, :], identf[:, :]).then_inc(of_turned, 1)

                        def project_out(s, r, loop):
                            wait(pe, of_kept, s, loop, 1, 1)
                            nc.tensor.matmul(bank[7][:, S:S + D], OF[:, r % 2, :], WO[:, L, :],
                                             start=True, stop=True).then_inc(proj, 1)

                        def step(s, r, loop):
                            def at(lag):
                                return s - lag if lag else s, (r - lag) % 8, loop
                            for g in range(NG):
                                if alive(s, loop, 0):
                                    scores(*at(0), g)
                                if alive(s, loop, 2):
                                    scores_T(*at(2), g)
                                if g == 1 and alive(s, loop, 1):
                                    turn_maxima(*at(1))
                                if g == 1 and alive(s, loop, 5):
                                    project_out(*at(5))
                                if g == 3 and alive(s, loop, 4):
                                    turn_normed(*at(4))
                                lag = 3 if g < 2 else 2
                                if alive(s, loop, lag):
                                    product_v(*at(lag), (g + 2) % NG)
                            if alive(s, loop, 3):
                                turn_out(*at(3))

                        pe.wait_ge(otz, 2)
                        steps(pe, step)

                    @block.vector
                    def _(dve):
                        def normalise(s, r, loop):
                            wait(dve, turned, s, loop, 1, 1)
                            wait(dve, of_turned, s, loop, 1, -1)
                            out = bank[6][:, :].rearrange("p (h v) -> p h v", v=32)
                            nc.vector.reciprocal(REC[:, r % 2, :].unsqueeze(2), out[:, :, DK:DK + 1]).then_inc(recd, 1)
                            wait(dve, recd, s, loop, 1, 1)
                            nc.vector.tensor_tensor(OQ[:, r % 2, :].rearrange("p (h d) -> p h d", d=DK), out[:, :, 0:DK],
                                                    REC[:, r % 2, :].unsqueeze(2).to_broadcast([P, H, DK]),
                                                    ALU.mult).then_inc(normed, 1)

                        def maxima(s, r, loop, g):
                            if g == 0:
                                wait(dve, m_turned, s, loop, 1, -1)
                            wait(dve, s_mm, s, loop, NG, g + 1)
                            nc.vector.tensor_reduce(M[:, r % 2, HG * g:HG * (g + 1)],
                                                    bank[g % 2][:, :].rearrange("p (h t) -> p h t", t=S),
                                                    AX.X, ALU.max).then_inc(maxed, 1)

                        def residual(s, r, loop):
                            wait(dve, proj, s, loop, 1, 1)
                            xs = X[:, ds(s, 1), :].rearrange("p o d -> p (o d)") if loop else X[:, s, :]
                            st = STATS[:, ds(s, 1), :].rearrange("p o d -> p (o d)") if loop else STATS[:, s, :]
                            nc.vector.tensor_tensor(xs, bank[7][:, S:S + D], xs, ALU.add).then_inc(added, 1)
                            wait(dve, added, s, loop, 1, 1)
                            nc.vector.bn_stats(st, xs)

                        def step(s, r, loop):
                            for g in range(NG):
                                if alive(s, loop, 0):
                                    maxima(s, r, loop, g)
                                if g == 0 and alive(s, loop, 4):
                                    normalise(s - 4, (r - 4) % 8, loop)
                                if g == 2 and alive(s, loop, 5):
                                    residual(s - 5, (r - 5) % 8, loop)

                        for n in (4, 5):
                            nc.vector.memset(bank[n][:, :], 0.0).then_inc(otz, 1)
                        steps(dve, step)

                    @block.scalar
                    def _(act):
                        def probs(s, r, loop, g):
                            wait(act, st_mm, s, loop, NG, g + 1)
                            wait(act, pv, s, loop, NG, g - 3)
                            nc.scalar.activation(PT[:, g, :], bank[2 + g % 2][:, :], ACT.Exp,
                                                 scale=SCALE).then_inc(exped, 1)

                        def keep_maxima(s, r, loop):
                            u, tok = r // CB, slice(r % CB * S, (r % CB + 1) * S)
                            wait(act, m_turned, s, loop, 1, 1)
                            wait(act, m_in[r % 2], s, loop, 8, -8 * (r % 2))
                            nc.scalar.mul(MT[:, r % 2, :], bank[6][0:H, 0:S], -1.0 / MSCALE).then_inc(m_kept, 1)
                            wait(act, m_kept, s, loop, 1, 1)
                            act.dma_start(QD[u][MROW:MROW + 1, :, :, tok].rearrange("p g h t -> p (g h) t"),
                                          MT[:, r % 2, :]).then_inc(m_in[r % 2], 16)

                        def keep_out_T(s, r, loop):
                            wait(act, pv, s, loop, NG, NG)
                            wait(act, turned, s, loop, 1, -1)
                            nc.scalar.copy(OT[:, r % 2, :], bank[4 + r % 2][:, :]).then_inc(ot_kept, 1)

                        def keep_out_F(s, r, loop):
                            wait(act, of_turned, s, loop, 1, 1)
                            wait(act, proj, s, loop, 1, -1)
                            nc.scalar.copy(OF[:, r % 2, :], bank[7][:, 0:S]).then_inc(of_kept, 1)

                        def step(s, r, loop):
                            def at(lag):
                                return s - lag if lag else s, (r - lag) % 8, loop
                            for g in range(NG):
                                if alive(s, loop, 2):
                                    probs(*at(2), g)
                                if g == 1:
                                    if alive(s, loop, 1):
                                        keep_maxima(*at(1))
                                    if alive(s, loop, 3):
                                        keep_out_T(*at(3))
                            if alive(s, loop, 4):
                                keep_out_F(*at(4))

                        steps(act, step)

        SIG = sb("SIG", [P, 2])
        SW = sb("SW", [P, 2 * NI + 1])
        SWX = sb("SWX", [P, 2 * NI])
        SACT = sb("SACT", [P, 2])
        INV = sb("INV", [P, 2])
        AMX = sb("AMX", [P, 2, 2])
        WGT = sb("WGT", [P, 2, INNER], BF16)
        WDT = sb("WDT", [P, NI, D], BF16)
        SDB = sb("SDB", [P, D])

        def ffn_weights():
            with ExitStack() as own:
                WR = own.enter_context(nc.sbuf_tensor("WR", [P, 2 * NI, D], F32))
                WDR = own.enter_context(nc.sbuf_tensor("WDR", [P, INNER], F32))
                clips = own.enter_context(nc.sbuf_tensor("clips", [P, 2], F32))
                ISW = own.enter_context(nc.sbuf_tensor("ISW", [P, 2 * NI + 1], F32))
                sd_diag = own.enter_context(nc.sbuf_tensor("sd_diag", [P, D], F32))
                ffn_in, small_in, x_in = sem("ffn_weights_loaded"), sem("small_loaded"), sem("x_loaded")
                expd, chain, quantised = sem("clips_exped"), sem("prep_chain"), sem("weights_quantised")
                turned, made = sem("weights_turned"), sem("biases_made")
                done = sem("prep_copied")
                small = [(identf[:, :], consts["identf"]), (identb[:, :], consts["identb"]),
                         (maskS[:, :, :], consts["maskS"]), (maskT[:, :, :], consts["maskT"]),
                         (clips[:, 0:1], w["clip_x"].partition_broadcast(P)),
                         (clips[:, 1:2], w["clip_down"].partition_broadcast(P))]
                for L in range(2):
                    small += [(WQ[:, L, :], w[f"Wq{L}"]), (WK[:, L, :], w[f"Wk{L}"]),
                              (WV[:, L, :], w[f"Wv{L}"]), (WO[:, L, :], w[f"Wo{L}"]),
                              (bvc[:, L:L + 1], w[f"bv{L}"]), (bor[:, L, :], w[f"bo{L}"])]
                small += [(bqk[:, 0, 0:1], w["bq0"]), (bqk[:, 0, 1:2], w["bk0"])]
                ffn = []
                for k, name in enumerate(("w_gate", "w_up")):
                    for i, rows in enumerate(ROWS):
                        ffn.append((WR[0:rows, NI * k + i, :], w[name][P * i:P * i + rows, :]))
                ffn.append((WDR[:, :], w["w_down"]))
                with nc.Block() as block:
                    @block.sync
                    def _(sp):
                        for n in range(NC):
                            sp.dma_start(X[:, CB * n:CB * (n + 1), :],
                                         x[CB * n:CB * (n + 1)].rearrange("b s d -> s b d")).then_inc(x_in, 16)
                        for dst, src in ffn:
                            sp.dma_start(dst, src).then_inc(ffn_in, 16)

                    @block.gpsimd
                    def _(pool):
                        nc.gpsimd.memset(HBUF[96:P, NI - 1, :], 0.0).then_inc(done, 1)
                        pool.wait_ge(done, 1)
                        nc.gpsimd.memset(ARENA[:, 0:10240], 0.0).then_inc(s_z, 1)
                        pool.wait_ge(s_z, 2)
                        for u in range(2):
                            if u:
                                pool.wait_ge(made, 5)
                            nc.gpsimd.memset(KP[u][MROW:MROW + 1, :, :], MSCALE).then_inc(made, 1)

                    @block.vector
                    def _(dve):
                        count = [0]

                        def link(ins):
                            count[0] += 1
                            ins.then_inc(chain, 1)
                            dve.wait_ge(chain, count[0])

                        nc.vector.memset(onesf[:, :], 1.0).then_inc(made, 1)
                        nc.vector.memset(bqk[:, 1, :], 0.0).then_inc(made, 1)
                        dve.wait_ge(small_in, 16 * len(small))
                        for L in range(2):
                            nc.vector.tensor_scalar(BVW[:, L, :], identf[:, :], 0.0, bvc[:, L:L + 1],
                                                    ALU.mult, ALU.add).then_inc(made, 1)
                        dve.wait_ge(expd, 1)
                        link(nc.vector.tensor_scalar(SIG[:, :], SIG[:, :], 1.0, None, ALU.add))
                        link(nc.vector.reciprocal(SIG[:, :], SIG[:, :]))
                        dve.wait_ge(ffn_in, 16 * len(ffn))
                        mats = [(WR[0:ROWS[k % NI], k, :], SW[0:ROWS[k % NI], k:k + 1]) for k in range(2 * NI)]
                        mats.append((WDR[:, :], SW[:, 2 * NI:2 * NI + 1]))
                        for k, (m, scale) in enumerate(mats):
                            link(nc.vector.tensor_reduce(scale, m, AX.X, ALU.max, apply_absolute_value=True))
                            link(nc.vector.tensor_scalar(scale, scale, 1.0 / QMAX, None, ALU.mult))
                            inv = ISW[0:m.shape[0], k:k + 1]
                            link(nc.vector.reciprocal(inv, scale))
                            link(nc.vector.tensor_scalar(m, m, inv, MAGIC, ALU.mult, ALU.add))
                            link(nc.vector.tensor_scalar(m, m, MAGIC, QMAX, ALU.subtract, ALU.min))
                        nc.vector.tensor_scalar(sd_diag[:, :], identf[:, :], SW[:, 2 * NI:2 * NI + 1], None,
                                                ALU.mult).then_inc(quantised, 1)
                        for n in range(NC):
                            pass
                        dve.wait_ge(x_in, 16 * NC)
                        for b in range(B):
                            ins = nc.vector.bn_stats(STATS[:, b, :], X[:, b, :])
                        ins.then_inc(chain, 1)
                        nc.vector.memset(ARENA[:, 10240:20480], 0.0).then_inc(s_z, 1)

                    @block.scalar
                    def _(act):
                        for dst, src in small:
                            act.dma_start(dst, src).then_inc(small_in, 16)
                        act.wait_ge(small_in, 16 * len(small))
                        nc.scalar.activation(SIG[:, :], clips[:, :], ACT.Exp, scale=-1.0).then_inc(expd, 1)
                        act.wait_ge(turned, 1)
                        for k in range(2):
                            nc.scalar.copy(WGT[:, k, :], bank[k][:, 0:INNER]).then_inc(done, 1)
                        nc.scalar.copy(WDT[:, 0:NI - 1, :], bank[2][:, 0:(NI - 1) * D]).then_inc(done, 1)
                        nc.scalar.copy(WDT[0:ROWS[-1], NI - 1, :], bank[3][0:ROWS[-1], 0:D]).then_inc(done, 1)
                        nc.scalar.copy(SDB[:, :], bank[4][:, 0:D]).then_inc(done, 1)
                        for L in range(2):
                            nc.scalar.copy(BO[:, L, :], bank[5 + L][:, 0:D]).then_inc(done, 1)

                    @block.tensor
                    def _(pe):
                        pe.wait_ge(quantised, 1)
                        pe.wait_ge(small_in, 16 * len(small))
                        for k in range(2):
                            for i, rows in enumerate(ROWS):
                                nc.tensor.transpose(bank[k][:, P * i:P * i + rows], WR[0:rows, NI * k + i, :],
                                                    identf[0:rows, 0:rows])
                        for i, rows in enumerate(ROWS):
                            out = bank[2][:, P * i:P * (i + 1)] if i < NI - 1 else bank[3][0:rows, 0:D]
                            nc.tensor.transpose(out, WDR[:, P * i:P * i + rows], identf[:, :])
                        pe.wait_ge(made, 6)
                        nc.tensor.matmul(bank[4][:, 0:D], onesf[:, :], sd_diag[:, :], start=True, stop=True)
                        for L in range(2):
                            nc.tensor.matmul(bank[5 + L][:, 0:D], BVW[:, L, :], WO[:, L, :], start=True, stop=False)
                            ins = nc.tensor.matmul(bank[5 + L][:, 0:D], onesf[0:1, :], bor[:, L, :],
                                                   start=False, stop=True)
                        ins.then_inc(turned, 1)

        def ffn():
            XN = XNT[:, :].rearrange("p (b d) -> p b d", d=D)
            with ExitStack() as own:
                def osb(name, shape, dt=F32):
                    return own.enter_context(nc.sbuf_tensor(name, shape, dt))
                QX = osb("QX", [P, 2, CB, D])
                XQ = osb("XQ", [P, 2, CT], BF16)
                SL = osb("SL", [P, 2, CT])
                HQ = osb("HQ", [P, 2, NI, CT], BF16)
                YB = osb("YB", [P, 2, CT])
                for which in range(2):
                    chain, maxed, reduced = sem(f"amax_chain{which}"), sem(f"amax_part{which}"), sem(f"amax_all{which}")
                    with nc.Block() as block:
                        @block.vector
                        def _(dve):
                            if which == 0:
                                with every(dve, 0, B, CB) as b0:
                                    for j in range(CB):
                                        b = b0 + j if j else b0
                                        ins = nc.vector.tensor_scalar(XN[:, ds(b, 1), :], X[:, ds(b, 1), :],
                                                                      MEAN[:, ds(b, 1)], RSTD[:, ds(b, 1)],
                                                                      ALU.subtract, ALU.mult)
                                    ins.then_inc(chain, 1)
                                dve.wait_ge(chain, NC)
                                nc.vector.tensor_reduce(AMX[:, 0, 0:1], XNT[:, :], AX.X, ALU.max,
                                                        apply_absolute_value=True).then_inc(maxed, 1)
                            else:
                                nc.vector.tensor_reduce(AMX[:, 1, 0:1], HBUF[:, :, :], AX.XY, ALU.max,
                                                        apply_absolute_value=True).then_inc(maxed, 1)
                            dve.wait_ge(reduced, 1)
                            base = NC if which == 0 else 0
                            nc.vector.tensor_scalar(SACT[:, which:which + 1], AMX[:, which, 1:2],
                                                    SIG[:, which:which + 1], 1.0 / QMAX, ALU.mult,
                                                    ALU.mult).then_inc(chain, 1)
                            dve.wait_ge(chain, base + 1)
                            nc.vector.reciprocal(INV[:, which:which + 1], SACT[:, which:which + 1]).then_inc(chain, 1)
                            if which == 0:
                                for k in range(2 * NI):
                                    rows = ROWS[k % NI]
                                    nc.vector.tensor_scalar(SWX[0:rows, k:k + 1], SW[0:rows, k:k + 1],
                                                            SACT[0:rows, 0:1], None, ALU.mult).then_inc(chain, 1)

                        @block.gpsimd
                        def _(pool):
                            pool.wait_ge(maxed, 1)
                            nc.gpsimd.partition_all_reduce(AMX[:, which, 1:2], AMX[:, which, 0:1], P,
                                                           ABSMAX).then_inc(reduced, 1)
                    if which == 0:
                        ffn_up(XN, QX, XQ, SL)
                ffn_down(HQ, YB)

        def ffn_up(XN, QX, XQ, SL):
            FREE = 2
            rounded, quant, turned, xq = sem("x_rounded"), sem("x_quantised"), sem("x_turned"), sem("x_integers")
            gate_mm, up_mm, silu, hid = sem("gate_mm"), sem("up_mm"), sem("silu_done"), sem("hidden_done")
            with nc.Block() as block:
                @block.vector
                def _(dve):
                    dve.sem_inc(hid, FREE)

                    def quantise(c, u):
                        dve.wait_ge(turned, c + (u + 1))
                        nc.vector.tensor_scalar(QX[:, u], XN[:, ds((c + u) * CB, CB), :], INV[:, 0:1], MAGIC,
                                                ALU.mult, ALU.add).then_inc(rounded, 1)
                        dve.wait_ge(rounded, c + (u + 1))
                        nc.vector.tensor_scalar(QX[:, u], QX[:, u], MAGIC + QMAX, MAGIC - QMAX - 1.0,
                                                ALU.min, ALU.max).then_inc(quant, 1)

                    with every(dve, 0, NC, 2) as c:
                        for u in range(2):
                            quantise(c, u)
                            for i, rows in enumerate(ROWS):
                                k = (u + i) % 2
                                dve.wait_ge(up_mm, (c + u) * NI + (i + 1 + NI * FREE))
                                dve.wait_ge(silu, (c + u) * NI + (i + 1 + FREE))
                                nc.vector.scalar_tensor_tensor(HBUF[0:rows, i, ds((c + u) * CT, CT)],
                                                               bank[2 + k][0:rows, :], SWX[0:rows, NI + i:NI + i + 1],
                                                               SL[0:rows, k, :], ALU.mult, ALU.mult).then_inc(hid, 1)

                @block.tensor
                def _(pe):
                    pe.sem_inc(turned, FREE)
                    pe.sem_inc(up_mm, NI * FREE)
                    with every(pe, 0, NC, 2) as c:
                        for u in range(2):
                            pe.wait_ge(quant, c + (u + 1))
                            pe.wait_ge(xq, c + (u + 1))
                            for j in range(CB):
                                ins = nc.tensor.transpose(bank[6 + u][:, j * S:(j + 1) * S], QX[:, u, j, :],
                                                          identf[:, :])
                            ins.then_inc(turned, 1)
                            pe.wait_ge(xq, c + (u + 1 + FREE))
                            for i, rows in enumerate(ROWS):
                                k = (u + i) % 2
                                pe.wait_ge(silu, (c + u) * NI + (i + 1))
                                nc.tensor.matmul(bank[k][0:rows, :], WGT[:, 0, P * i:P * i + rows], XQ[:, u, :],
                                                 start=True, stop=True).then_inc(gate_mm, 1)
                                pe.wait_ge(hid, (c + u) * NI + (i + 1))
                                nc.tensor.matmul(bank[2 + k][0:rows, :], WGT[:, 1, P * i:P * i + rows], XQ[:, u, :],
                                                 start=True, stop=True).then_inc(up_mm, 1)

                @block.scalar
                def _(act):
                    act.sem_inc(xq, FREE)
                    act.sem_inc(silu, FREE)
                    with every(act, 0, NC, 2) as c:
                        for u in range(2):
                            act.wait_ge(turned, c + (u + 1 + FREE))
                            act.wait_ge(up_mm, (c + u) * NI + NI)
                            nc.scalar.activation(XQ[:, u, :], bank[6 + u][:, :], ACT.Copy,
                                                 bias=-MAGIC).then_inc(xq, 1)
                            for i, rows in enumerate(ROWS):
                                k = (u + i) % 2
                                act.wait_ge(gate_mm, (c + u) * NI + (i + 1))
                                act.wait_ge(hid, (c + u) * NI + (i + 1))
                                nc.scalar.activation(SL[0:rows, k, :], bank[k][0:rows, :], ACT.Silu,
                                                     scale=SWX[0:rows, i:i + 1]).then_inc(silu, 1)

        def ffn_down(HQ, YB):
            FREE = 2
            clipped, rounded, ints = sem("h_clipped"), sem("h_rounded"), sem("h_integers")
            down, scaled, added = sem("down_mm"), sem("down_scaled"), sem("ffn_added")
            with nc.Block() as block:
                @block.vector
                def _(dve):
                    dve.sem_inc(scaled, FREE)
                    with every(dve, 0, NC, 2) as c:
                        for u in range(2):
                            h = HBUF[:, :, ds((c + u) * CT, CT)]
                            nc.vector.tensor_scalar(h, h, INV[:, 1:2], QMAX, ALU.mult, ALU.min).then_inc(clipped, 1)
                            dve.wait_ge(clipped, c + (u + 1))
                            nc.vector.tensor_scalar(h, h, -QMAX - 1.0, MAGIC, ALU.max, ALU.add).then_inc(rounded, 1)
                            dve.wait_ge(down, c + (u + 1 + FREE))
                            nc.vector.scalar_tensor_tensor(YB[:, u, :].rearrange("p (b d) -> p b d", d=D),
                                                           bank[u][:, :].rearrange("p (b d) -> p b d", d=D),
                                                           SACT[:, 1:2], SDB[:, :].unsqueeze(1).to_broadcast([P, CB, D]),
                                                           ALU.mult, ALU.mult).then_inc(scaled, 1)
                            dve.wait_ge(scaled, c + (u + 1 + FREE))
                            xs = X[:, ds((c + u) * CB, CB), :]
                            nc.vector.tensor_tensor(xs, YB[:, u, :].rearrange("p (b d) -> p b d", d=D), xs,
                                                    ALU.add).then_inc(added, 1)
                            dve.wait_ge(added, c + (u + 1))
                            for j in range(CB):
                                b = (c + u) * CB + j
                                nc.vector.bn_stats(STATS[:, ds(b, 1), :], X[:, ds(b, 1), :])

                @block.scalar
                def _(act):
                    with every(act, 0, NC, 2) as c:
                        for u in range(2):
                            act.wait_ge(rounded, c + (u + 1))
                            act.wait_ge(down, c + (u + 1))
                            nc.scalar.activation(HQ[:, u], HBUF[:, :, ds((c + u) * CT, CT)], ACT.Copy,
                                                 bias=-MAGIC).then_inc(ints, 1)

                @block.tensor
                def _(pe):
                    pe.sem_inc(down, FREE)
                    with every(pe, 0, NC, 2) as c:
                        for u in range(2):
                            pe.wait_ge(ints, c + (u + 1))
                            pe.wait_ge(scaled, c + (u + 1))
                            for j in range(CB):
                                for i, rows in enumerate(ROWS):
                                    ins = nc.tensor.matmul(bank[u][:, j * D:(j + 1) * D],
                                                           HQ[0:rows, u, i, j * S:(j + 1) * S], WDT[0:rows, i, :],
                                                           start=(i == 0), stop=(i == NI - 1))
                            ins.then_inc(down, 1)

        moe_w = HBUF[:, :, :].rearrange("p i t -> p (i t)")
        n_w = (E + 1) * D
        W1 = moe_w[:, 0:n_w].rearrange("p (e i) -> p e i", i=D)
        W3 = moe_w[:, n_w:2 * n_w].rearrange("p (e i) -> p e i", i=D)
        W2 = moe_w[:, 2 * n_w:3 * n_w].rearrange("p (e i) -> p e i", i=D)

        def router(gscr):
            with ExitStack() as own:
                def osb(name, shape, dt=F32):
                    return own.enter_context(nc.sbuf_tensor(name, shape, dt))
                GW = osb("GW", [P, E])
                EB = osb("EB", [P, E])
                T8 = osb("T8", [P, B, 8])
                RAW, BI, GT_, EQ, SC, SC2 = (osb(n, [P, B, E]) for n in ("RAW", "BI", "GTR", "EQ", "SC", "SC2"))
                CNT = osb("CNT", [P, B])
                GTT = osb("GTT", [P, 4, P])
                LT = moe_w[0:E, 3 * n_w:3 * n_w + NT]
                w_in, gw_in = sem("experts_loaded"), sem("router_loaded")
                lg, lk, lt = sem("logits_T"), sem("logits_T_kept"), sem("logits")
                chain, topped, ex = sem("router_chain"), sem("top8"), sem("router_exp")
                g_ready, g_turned, g_kept, g_out = sem("gates"), sem("gates_turned"), sem("gates_kept"), sem("gates_stored")
                with nc.Block() as block:
                    @block.sync
                    def _(sp):
                        sp.dma_start(GW[:, :], w["gate_w"]).then_inc(gw_in, 16)
                        sp.dma_start(EB[:, :], w["expert_bias"].partition_broadcast(P)).then_inc(gw_in, 16)
                        for dst, a, b in ((W1, "w1", "sw1"), (W3, "w3", "sw3"), (W2, "w2", "sw2")):
                            sp.dma_start(dst[:, 0:E, :], w[a]).then_inc(w_in, 16)
                            sp.dma_start(dst[:, E, :], w[b]).then_inc(w_in, 16)
                        sp.wait_ge(g_kept, 1)
                        to = gscr.rearrange("e (T n k) -> n e T k", T=4, n=8)
                        for n in range(8):
                            sp.dma_start(to[n], GTT[E * n:E * (n + 1), :, :]).then_inc(g_out, 16)
                        sp.wait_ge(g_out, 16 * 8)
                        sp.wait_ge(w_in, 16 * 6)

                    @block.tensor
                    def _(pe):
                        pe.wait_ge(gw_in, 32)
                        for n in range(NC):
                            nc.tensor.matmul(bank[n][0:E, :], GW[:, :], XNT[:, n * CT:(n + 1) * CT],
                                             start=True, stop=True).then_inc(lg, 1)
                        pe.wait_ge(lk, NC)
                        for b in range(B):
                            ins = nc.tensor.transpose(bank[0][:, b * E:(b + 1) * E], LT[:, b * S:(b + 1) * S],
                                                      identf[0:E, 0:E])
                        ins.then_inc(lt, 1)
                        pe.wait_ge(g_ready, 1)
                        flat = RAW[:, :, :].rearrange("p b e -> p (b e)")
                        for n in range(4):
                            ins = nc.tensor.transpose(bank[1][:, n * P:(n + 1) * P], flat[:, n * P:(n + 1) * P],
                                                      identf[:, :])
                        ins.then_inc(g_turned, 1)

                    @block.scalar
                    def _(act):
                        for n in range(NC):
                            act.wait_ge(lg, n + 1)
                            nc.scalar.copy(LT[:, n * CT:(n + 1) * CT], bank[n][0:E, :]).then_inc(lk, 1)
                        act.wait_ge(ex, 1)
                        nc.scalar.activation(EQ[:, :, :], SC[:, :, :], ACT.Exp).then_inc(ex, 1)
                        act.wait_ge(g_turned, 1)
                        nc.scalar.copy(GTT[:, :, :], bank[1][:, :]).then_inc(g_kept, 1)

                    @block.vector
                    def _(dve):
                        count = [0]

                        def link(ins):
                            count[0] += 1
                            ins.then_inc(chain, 1)
                            dve.wait_ge(chain, count[0])

                        full = [P, B, E]
                        dve.wait_ge(lt, 1)
                        dve.wait_ge(gw_in, 32)
                        link(nc.vector.tensor_copy(RAW[:, :, :], bank[0][:, :]))
                        link(nc.vector.tensor_tensor(BI[:, :, :], RAW[:, :, :],
                                                     EB[:, :].unsqueeze(1).to_broadcast(full), ALU.add))
                        for b in range(B):
                            ins = nc.vector.max(T8[:, b, :], BI[:, b, :])
                        link(ins)
                        fourth = T8[:, :, TOPK - 1:TOPK].to_broadcast(full)
                        nc.vector.tensor_tensor(GT_[:, :, :], BI[:, :, :], fourth, ALU.is_gt)
                        link(nc.vector.tensor_tensor(EQ[:, :, :], BI[:, :, :], fourth, ALU.is_equal))
                        link(nc.vector.tensor_reduce(CNT[:, :], GT_[:, :, :], AX.X, ALU.add))
                        link(nc.vector.tensor_scalar(CNT[:, :], CNT[:, :], -1.0, float(TOPK), ALU.mult, ALU.add))
                        a, b_ = EQ, SC
                        for k in (1, 2, 4, 8):
                            nc.vector.tensor_copy(b_[:, :, 0:k], a[:, :, 0:k])
                            link(nc.vector.tensor_tensor(b_[:, :, k:E], a[:, :, k:E], a[:, :, 0:E - k], ALU.add))
                            a, b_ = b_, (SC2 if b_ is SC else SC)
                        link(nc.vector.tensor_tensor(b_[:, :, :], a[:, :, :], CNT[:, :].unsqueeze(2).to_broadcast(full),
                                                     ALU.is_le))
                        link(nc.vector.tensor_tensor(EQ[:, :, :], EQ[:, :, :], b_[:, :, :], ALU.mult))
                        link(nc.vector.tensor_tensor(GT_[:, :, :], GT_[:, :, :], EQ[:, :, :], ALU.add))
                        link(nc.vector.tensor_scalar(SC[:, :, :], GT_[:, :, :], -1.0, BIG, ALU.add, ALU.mult))
                        link(nc.vector.tensor_tensor(SC[:, :, :], SC[:, :, :], RAW[:, :, :], ALU.add))
                        link(nc.vector.tensor_reduce(CNT[:, :], SC[:, :, :], AX.X, ALU.max))
                        nc.vector.tensor_tensor(SC[:, :, :], SC[:, :, :], CNT[:, :].unsqueeze(2).to_broadcast(full),
                                                ALU.subtract).then_inc(ex, 1)
                        dve.wait_ge(ex, 2)
                        link(nc.vector.tensor_reduce(CNT[:, :], EQ[:, :, :], AX.X, ALU.add))
                        link(nc.vector.reciprocal(CNT[:, :], CNT[:, :]))
                        nc.vector.tensor_tensor(RAW[:, :, :], EQ[:, :, :], CNT[:, :].unsqueeze(2).to_broadcast(full),
                                                ALU.mult).then_inc(g_ready, 1)

        def experts(gscr):
            FREE = 2
            EN = E + 1
            with ExitStack() as own:
                def osb(name, shape, dt=F32):
                    return own.enter_context(nc.sbuf_tensor(name, shape, dt))
                G = [ARENA[:, n * E * CT:(n + 1) * E * CT].rearrange("p (e t) -> p e t", t=CT) for n in range(2)]
                SL = osb("SLE", [P, 2, CT])
                UG = osb("UG", [P, 2, CT])
                HE = osb("HE", [P, 2, CT])
                XR = osb("XR", [P, 2, CB, D])
                YT = osb("YT", [P, 2, CT])
                g_in = [sem(f"gates_loaded{u}") for u in range(2)]
                gate_mm, up_mm, down, y_mm = sem("e_gate_mm"), sem("e_up_mm"), sem("e_down_mm"), sem("y_mm")
                silu, gated, hid = sem("e_silu"), sem("e_gated"), sem("e_hidden")
                xr, yk = sem("x_ringed"), sem("y_kept")
                stored = [sem(f"out_stored{u}") for u in range(2)]
                with nc.Block() as block:
                    @block.sync
                    def _(sp):
                        def load(c, u):
                            tok = slice((c + u) * CT, (c + u + 1) * CT) if isinstance(c, int) else ds((c + u) * CT, CT)
                            sp.dma_start(G[u], gscr[:, tok].partition_broadcast(P)).then_inc(g_in[u], 16)

                        for u in range(2):
                            load(0, u)
                        with every(sp, 2, NC, 2) as c:
                            for u in range(2):
                                sp.wait_ge(hid, (c + (u - 1)) * EN + FREE)
                                load(c, u)

                    @block.gpsimd
                    def _(pool):
                        with every(pool, 0, NC, 2) as c:
                            for u in range(2):
                                pool.wait_ge(y_mm, c + (u + 1))
                                nc.gpsimd.tensor_copy(XR[:, u], X[:, ds((c + u) * CB, CB), :]).then_inc(xr, 1)

                    @block.tensor
                    def _(pe):
                        pe.sem_inc(down, FREE)
                        pe.sem_inc(y_mm, FREE)
                        with every(pe, 0, NC, 2) as c:
                            def down_mm(u, e):
                                m = (c + u) * EN
                                pe.wait_ge(hid, m + (e + 1 + FREE))
                                if e == 0:
                                    pe.wait_ge(yk, c + (u + 1))
                                nc.tensor.matmul(bank[4 + u][:, :], W2[:, e, :], HE[:, (u + e) % 2, :],
                                                 start=(e == 0), stop=False, skip_group_check=True).then_inc(down, 1)
                                if e == EN - 1:
                                    pe.wait_ge(xr, c + (u + 1))
                                    for j in range(CB):
                                        ins = nc.tensor.matmul(bank[4 + u][:, j * S:(j + 1) * S], XR[:, u, j, :],
                                                               identf[:, :], start=False, stop=(j == CB - 1),
                                                               skip_group_check=True)
                                    ins.then_inc(y_mm, 1)

                            last = None
                            for u in range(2):
                                for e in range(EN):
                                    k = (u + e) % 2
                                    m = (c + u) * EN
                                    pe.wait_ge(silu, m + (e + 1))
                                    nc.tensor.matmul(bank[k][:, :], W1[:, e, :], XNT[:, ds((c + u) * CT, CT)],
                                                     start=True, stop=True).then_inc(gate_mm, 1)
                                    pe.wait_ge(hid, m + (e + 1))
                                    nc.tensor.matmul(bank[2 + k][:, :], W3[:, e, :], XNT[:, ds((c + u) * CT, CT)],
                                                     start=True, stop=True).then_inc(up_mm, 1)
                                    if last is not None:
                                        down_mm(*last)
                                    last = (u, e)
                            down_mm(*last)

                    @block.scalar
                    def _(act):
                        act.sem_inc(silu, FREE)
                        act.sem_inc(yk, FREE)
                        for u in range(2):
                            act.sem_inc(stored[u], 16)
                        with every(act, 0, NC, 2) as c:
                            def keep_y(u):
                                act.wait_ge(y_mm, c + (u + 1 + FREE))
                                act.wait_ge(stored[u], c * 8 + 16)
                                nc.scalar.copy(YT[:, u, :], bank[4 + u][:, :]).then_inc(yk, 1)
                                act.wait_ge(yk, c + (u + 1 + FREE))
                                act.dma_start(outT[:, ds((c + u) * CT, CT)], YT[:, u, :]).then_inc(stored[u], 16)

                            for u in range(2):
                                for e in range(EN):
                                    k = (u + e) % 2
                                    m = (c + u) * EN
                                    act.wait_ge(gate_mm, m + (e + 1))
                                    act.wait_ge(hid, m + (e + 1))
                                    nc.scalar.activation(SL[:, k, :], bank[k][:, :], ACT.Silu).then_inc(silu, 1)
                                    if u == 1 and e == 3:
                                        keep_y(0)
                            keep_y(1)
                        for u in range(2):
                            act.wait_ge(stored[u], 16 * (NC // 2 + 1))

                    @block.vector
                    def _(dve):
                        dve.sem_inc(hid, FREE)
                        with every(dve, 0, NC, 2) as c:
                            for u in range(2):
                                dve.wait_ge(g_in[u], c * 8 + 16)
                                for e in range(EN):
                                    k = (u + e) % 2
                                    m = (c + u) * EN
                                    dve.wait_ge(up_mm, m + (e + 1))
                                    up = bank[2 + k][:, :]
                                    if e < E:
                                        nc.vector.tensor_tensor(UG[:, k, :], up, G[u][:, e, :], ALU.mult).then_inc(gated, 1)
                                        up = UG[:, k, :]
                                        dve.wait_ge(gated, (c + u) * E + (e + 1))
                                    dve.wait_ge(silu, m + (e + 1 + FREE))
                                    dve.wait_ge(down, m + (e + 1))
                                    nc.vector.tensor_tensor(HE[:, k, :], up, SL[:, k, :], ALU.mult).then_inc(hid, 1)

        qk = [nc.dram_tensor(f"qk_scratch{L}", [4, P, NT], F16, kind="Internal").ap() for L in range(2)]
        vs = [nc.dram_tensor(f"v_scratch{L}", [P, B * H * VW], F32, kind="Internal").ap() for L in range(2)]
        gscr = nc.dram_tensor("gates_scratch", [E, NT], F32, kind="Internal").ap()

        def turn(tag):
            with nc.sbuf_tensor(f"XN_{tag}", [P, 2, CB, D], F32) as XN:
                ln_transpose(tag, XN)

        ffn_weights()
        ln_stats("a0")
        turn("a0")
        projections(0, qk[0], vs[0])
        attention(0, qk[0], vs[0])
        ln_stats("f0")
        ffn()
        ln_stats("a1")
        turn("a1")
        projections(1, qk[1], vs[1])
        attention(1, qk[1], vs[1])
        ln_stats("f1")
        turn("f1")
        router(gscr)
        experts(gscr)


def kernel(**inputs):
    import ml_dtypes
    import numpy as np
    import concourse.bacc as bacc
    from concourse.bass_utils import run_bass_kernel_spmd

    a = {k: np.asarray(v) for k, v in inputs.items()}
    i = np.arange(S)
    hidden = i[:, None] <= i[None, :]
    hidden[0, 0] = False
    neg = np.where(hidden, -BIG, 0.0).astype(ml_dtypes.bfloat16)
    arrays = {
        "x": a["x"],
        "ctxT": a["ctx_1024"].reshape(NT, D).T,
        "identf": np.eye(P, dtype=np.float32),
        "identb": np.eye(P).astype(ml_dtypes.bfloat16),
        "maskS": np.repeat(neg[:, None, :], HG, 1),
        "maskT": np.repeat(neg.T[:, None, :], HG, 1),
        "clip_x": a["L0_ffn_clip_x"], "clip_down": a["L0_ffn_clip_down"],
        "w_gate": a["L0_ffn_w_gate"], "w_up": a["L0_ffn_w_up"], "w_down": a["L0_ffn_w_down"],
        "bq0": a["L0_xattn_bq"].reshape(D, 1), "bk0": a["L0_xattn_bk"].reshape(D, 1),
        "gate_w": a["L1_ffn_gate_w"].T, "expert_bias": a["L1_ffn_expert_bias"],
        "w1": a["L1_ffn_w1"].transpose(2, 0, 1), "w3": a["L1_ffn_w3"].transpose(2, 0, 1),
        "w2": a["L1_ffn_w2"].transpose(2, 0, 1),
        "sw1": a["L1_ffn_sw1"].T, "sw3": a["L1_ffn_sw3"].T, "sw2": a["L1_ffn_sw2"].T,
    }
    for L in range(2):
        for n in "qkvo":
            arrays[f"W{n}{L}"] = a[f"L{L}_xattn_W{n}"].T
        arrays[f"bv{L}"] = a[f"L{L}_xattn_bv"].reshape(D, 1)
        arrays[f"bo{L}"] = a[f"L{L}_xattn_bo"].reshape(1, D)
    nc = bacc.Bacc("TRN2", target_bir_lowering=False, num_devices=1)
    fed, aps = {}, {}
    for name, array in arrays.items():
        array = np.ascontiguousarray(array)
        fed[f"in_{name}"] = array
        aps[name] = nc.dram_tensor(f"in_{name}", array.shape, mybir.dt.from_np(array.dtype), kind="ExternalInput").ap()
    outT = nc.dram_tensor("outT", (D, NT), F32, kind="ExternalOutput").ap()
    consts = {k: aps.pop(k) for k in ("identf", "identb", "maskS", "maskT")}
    build(nc, aps.pop("x"), aps.pop("ctxT"), aps, consts, outT)
    r = run_bass_kernel_spmd(nc, [fed], core_ids=[0])
    return np.ascontiguousarray(r.results[0]["outT"].T).reshape(B, S, D)
```

```python
from contextlib import ExitStack, contextmanager

import concourse.bass as bass
from concourse import mybir

F32 = mybir.dt.float32
F16 = mybir.dt.float16
BF16 = mybir.dt.bfloat16
ALU = mybir.AluOpType
ACT = mybir.ActivationFunctionType
AX = mybir.AxisListType
ABSMAX = bass.bass_isa.ReduceOp.absmax

P = 128
B = 32
S = 128
D = 128
H = 16
DK = D // H
HG = 4
NG = H // HG
CB = 4
CT = CB * S
NC = B // CB
NT = B * S
INNER = 352
ROWS = [128, 128, 96]
NI = len(ROWS)
E = 16
TOPK = 4
R = HG * DK
MROW = 3 * R
VW = DK + 1
SCALE = float(DK) ** -0.5
MSCALE = 1024.0
EPS = 1e-5
QMAX = 127.0
MAGIC = 12582912.0
BIG = 1e30


@contextmanager
def every(eng, first, end, step):
    with eng.Fori(0, (end - first) // step) as n:
        yield n * step + first


def span(n, size):
    return slice(n * size, (n + 1) * size) if isinstance(n, int) else bass.ds(n * size, size)


def build(nc, x, ctxT, w, consts, outT):
    ds = bass.ds
    with ExitStack() as top:
        def sb(name, shape, dt=F32):
            return top.enter_context(nc.sbuf_tensor(name, shape, dt))

        def sem(name):
            return top.enter_context(nc.semaphore(name))

        X = sb("X", [P, B, D])
        XNT = sb("XNT", [P, NT])
        STATS = sb("STATS", [P, B, 6])
        MEAN = sb("MEAN", [P, B])
        RSTD = sb("RSTD", [P, B])
        tmpB = sb("tmpB", [P, 4, B])
        identf = sb("identf", [P, P])
        identb = sb("identb", [P, P], BF16)
        maskS = sb("maskS", [P, HG, P], BF16)
        maskT = sb("maskT", [P, HG, P], BF16)
        onesf = sb("onesf", [P, P])
        WQ = sb("WQ", [P, 2, D])
        WK = sb("WK", [P, 2, D])
        WV = sb("WV", [P, 2, D])
        WO = sb("WO", [P, 2, D])
        bqk = sb("bqk", [P, 2, 2])
        bvc = sb("bvc", [P, 2])
        bor = sb("bor", [1, 2, D])
        BVW = sb("BVW", [P, 2, D])
        BO = sb("BO", [P, 2, D])

        ARENA = sb("ARENA", [P, 20480])
        HBUF = sb("HBUF", [P, NI, NT])
        half = ARENA[:, :].bitcast(F16)
        QD = [half[:, n * 8192:(n + 1) * 8192].rearrange("p (g h t) -> p g h t", g=NG, h=HG) for n in (0, 1)]
        KD = [half[:, n * 8192:(n + 1) * 8192].rearrange("p (g h t) -> p g h t", g=NG, h=HG) for n in (2, 3)]
        QP = [half[:, 32768 + n * 2048:32768 + (n + 1) * 2048].rearrange("p (g t) -> p g t", g=NG) for n in (0, 1)]
        KP = [half[:, 36864 + n * 2048:36864 + (n + 1) * 2048].rearrange("p (g t) -> p g t", g=NG) for n in (0, 1)]

        bank = [top.enter_context(nc.psum_tensor(f"bank{n}", [P, 512], F32)) for n in range(8)]

        s_w = sem("weights_loaded")
        n_w = 0
        s_z = sem("arena_zeroed")
        zeroed = [0]

        def ln_stats(tag):
            step = sem(f"ln_step_{tag}")
            with nc.Block() as block:
                @block.vector
                def _(dve):
                    me, mo = STATS[:, :, 1], STATS[:, :, 4]
                    ve, vo = STATS[:, :, 2], STATS[:, :, 5]
                    nc.vector.tensor_tensor(tmpB[:, 0, :], me, mo, ALU.add)
                    nc.vector.tensor_tensor(tmpB[:, 1, :], me, mo, ALU.subtract)
                    nc.vector.tensor_tensor(tmpB[:, 2, :], ve, vo, ALU.add).then_inc(step, 1)
                    dve.wait_ge(step, 1)
                    nc.vector.tensor_scalar(MEAN[:, :], tmpB[:, 0, :], 0.5, None, ALU.mult)
                    nc.vector.tensor_scalar(tmpB[:, 2, :], tmpB[:, 2, :], 1.0 / D, EPS, ALU.mult, ALU.add)
                    nc.vector.tensor_tensor(tmpB[:, 1, :], tmpB[:, 1, :], tmpB[:, 1, :], ALU.mult).then_inc(step, 1)
                    dve.wait_ge(step, 2)
                    nc.vector.scalar_tensor_tensor(tmpB[:, 3, :], tmpB[:, 1, :], 0.25, tmpB[:, 2, :],
                                                   ALU.mult, ALU.add).then_inc(step, 1)
                    dve.wait_ge(step, 3)
                    dve.wait_ge(step, 4)
                    nc.vector.reciprocal(RSTD[:, :], tmpB[:, 0, :]).then_inc(step, 1)
                    dve.wait_ge(step, 5)
                    nc.vector.tensor_tensor(tmpB[:, 1, :], RSTD[:, :], RSTD[:, :], ALU.mult).then_inc(step, 1)
                    dve.wait_ge(step, 6)
                    nc.vector.tensor_tensor(tmpB[:, 1, :], tmpB[:, 1, :], tmpB[:, 3, :], ALU.mult).then_inc(step, 1)
                    dve.wait_ge(step, 7)
                    nc.vector.tensor_scalar(tmpB[:, 1, :], tmpB[:, 1, :], -0.5, 1.5, ALU.mult, ALU.add).then_inc(step, 1)
                    dve.wait_ge(step, 8)
                    nc.vector.tensor_tensor(RSTD[:, :], tmpB[:, 1, :], RSTD[:, :], ALU.mult).then_inc(step, 1)
                    dve.wait_ge(step, 9)

                @block.scalar
                def _(act):
                    act.wait_ge(step, 3)
                    nc.scalar.activation(tmpB[:, 0, :], tmpB[:, 3, :], ACT.Sqrt).then_inc(step, 1)

        def ln_transpose(tag, XN):
            normed, turned, kept = sem(f"normed_{tag}"), sem(f"turned_{tag}"), sem(f"xnt_kept_{tag}")
            FREE = 2
            with nc.Block() as block:
                @block.vector
                def _(dve):
                    with every(dve, 0, NC, 2) as c:
                        for u in range(2):
                            dve.wait_ge(turned, c + u + 1)
                            for j in range(CB):
                                b = c * CB + (u * CB + j)
                                ins = nc.vector.tensor_scalar(XN[:, u, j, :], X[:, ds(b, 1), :], MEAN[:, ds(b, 1)],
                                                              RSTD[:, ds(b, 1)], ALU.subtract, ALU.mult)
                            ins.then_inc(normed, 1)

                @block.tensor
                def _(pe):
                    pe.sem_inc(turned, FREE)
                    with every(pe, 0, NC, 2) as c:
                        for u in range(2):
                            pe.wait_ge(normed, c + u + 1)
                            pe.wait_ge(kept, c + u + 1)
                            for j in range(CB):
                                ins = nc.tensor.transpose(bank[u][:, j * S:(j + 1) * S], XN[:, u, j, :], identf[:, :])
                            ins.then_inc(turned, 1)

                @block.scalar
                def _(act):
                    act.sem_inc(kept, FREE)
                    with every(act, 0, NC, 2) as c:
                        for u in range(2):
                            act.wait_ge(turned, c + u + 1 + FREE)
                            nc.scalar.copy(XNT[:, ds((c + u) * CT, CT)], bank[u][:, :]).then_inc(kept, 1)

        def projections(L, qk, vs):
            t = f"L{L}"
            with ExitStack() as own:
                CX = own.enter_context(nc.sbuf_tensor(f"CX{L}", [P, 2, CT], F32))
                HL = own.enter_context(nc.sbuf_tensor(f"HL{L}", [P, 2, 4, CT], F16))
                VS = own.enter_context(nc.sbuf_tensor(f"VS{L}", [P, 2, CB * H, VW], F32))
                cx_in = [sem(f"ctx_loaded{u}_{t}") for u in range(2)]
                q_mm, k_mm, v_mm = sem(f"q_mm_{t}"), sem(f"k_mm_{t}"), sem(f"v_mm_{t}")
                hi, lo, vc = sem(f"hi_made_{t}"), sem(f"lo_made_{t}"), sem(f"v_copied_{t}")
                stored = [sem(f"qkv_stored{u}_{t}") for u in range(2)]
                ones, xb = sem(f"ones_set_{t}"), sem(f"bias_added_{t}")
                FREE = 2
                with nc.Block() as block:
                    @block.gpsimd
                    def _(pool):
                        nc.gpsimd.memset(VS[:, :, :, :], 1.0).then_inc(ones, 1)
                        nc.gpsimd.tensor_tensor(X[:, :, :], X[:, :, :],
                                                BO[:, L, :].unsqueeze(1).to_broadcast([P, B, D]),
                                                ALU.add).then_inc(xb, 1)
                        pool.wait_ge(xb, 1)

                    def store(sp, c, u):
                        sp.wait_ge(lo, (c + u) * 2 + (2 + 2 * FREE))
                        for n in range(4):
                            sp.dma_start(qk[n, :, ds((c + u) * CT, CT)], HL[:, u, n, :]).then_inc(stored[u], 16)
                        sp.wait_ge(vc, c + (u + 1 + FREE))
                        sp.dma_start(vs[:, ds((c + u) * (CB * H * VW), CB * H * VW)],
                                     VS[:, u, :, :]).then_inc(stored[u], 16)

                    @block.sync
                    def _(sp):
                        for u in range(2):
                            sp.dma_start(CX[:, u, :], ctxT[:, u * CT:(u + 1) * CT]).then_inc(cx_in[u], 16)
                        with every(sp, 0, NC - 2, 2) as c:
                            for u in range(2):
                                sp.wait_ge(v_mm, c + (u + 1))
                                sp.dma_start(CX[:, u, :], ctxT[:, ds((c + (u + 2)) * CT, CT)]).then_inc(cx_in[u], 16)
                                store(sp, c, u)
                        for u in range(2):
                            store(sp, NC - 2, u)
                        for u in range(2):
                            sp.wait_ge(stored[u], 16 * 5 * (NC // 2 + 1))

                    @block.tensor
                    def _(pe):
                        with every(pe, 0, NC, 2) as c:
                            for u in range(2):
                                pe.wait_ge(lo, (c + u) * 2 + 2)
                                nc.tensor.matmul(bank[4 * u][:, :], WQ[:, L, :], XNT[:, ds((c + u) * CT, CT)],
                                                 start=True, stop=True).then_inc(q_mm, 1)
                                pe.wait_ge(cx_in[u], c * 8 + 16)
                                nc.tensor.matmul(bank[4 * u + 1][:, :], WK[:, L, :], CX[:, u, :],
                                                 start=True, stop=True).then_inc(k_mm, 1)
                                pe.wait_ge(vc, c + (u + 1))
                                for j in range(CB):
                                    ins = nc.tensor.matmul(bank[4 * u + 2][:, j * D:(j + 1) * D],
                                                           CX[:, u, j * S:(j + 1) * S], WV[:, L, :],
                                                           start=True, stop=True)
                                ins.then_inc(v_mm, 1)

                    @block.scalar
                    def _(act):
                        act.sem_inc(vc, FREE)
                        for u in range(2):
                            act.sem_inc(stored[u], 16 * 5)
                        act.wait_ge(ones, 1)
                        with every(act, 0, NC, 2) as c:
                            for u in range(2):
                                act.wait_ge(stored[u], c * (16 * 5 // 2) + 16 * 5)
                                act.wait_ge(q_mm, c + (u + 1))
                                nc.scalar.activation(HL[:, u, 0, :], bank[4 * u][:, :], ACT.Identity,
                                                     bias=bqk[:, L, 0:1]).then_inc(hi, 1)
                                act.wait_ge(k_mm, c + (u + 1))
                                nc.scalar.activation(HL[:, u, 2, :], bank[4 * u + 1][:, :], ACT.Identity,
                                                     bias=bqk[:, L, 1:2]).then_inc(hi, 1)
                                act.wait_ge(v_mm, c + (u + 1))
                                nc.scalar.copy(VS[:, u, :, 0:DK],
                                               bank[4 * u + 2][:, :].rearrange("p (m d) -> p m d", d=DK)).then_inc(vc, 1)

                    @block.vector
                    def _(dve):
                        dve.sem_inc(lo, 2 * FREE)
                        with every(dve, 0, NC, 2) as c:
                            for u in range(2):
                                for n in range(2):
                                    dve.wait_ge(hi, (c + u) * 2 + (n + 1))
                                    nc.vector.scalar_tensor_tensor(
                                        HL[:, u, 2 * n + 1, :], bank[4 * u + n][:, :], bqk[:, L, n:n + 1],
                                        HL[:, u, 2 * n, :], ALU.add, ALU.subtract).then_inc(lo, 1)

        def attention(L, qk, vs):
            t = f"L{L}"
            causal = L == 1
            with ExitStack() as own:
                def osb(name, shape, dt=F32):
                    return own.enter_context(nc.sbuf_tensor(f"{name}{L}", shape, dt))
                VR = osb("VR", [P, 2, CB, H, VW])
                M = osb("M", [P, 2, H])
                MT = osb("MT", [H, 2, S], F16)
                PT = osb("PT", [P, 4, HG * S])
                OT = osb("OT", [P, 2, HG * S])
                REC = osb("REC", [P, 2, H])
                OQ = osb("OQ", [P, 2, D])
                OF = osb("OF", [P, 2, S])
                max_in = [sem(f"maxima_operands_loaded{u}_{t}") for u in range(2)]
                prob_in = [sem(f"probs_operands_loaded{u}_{t}") for u in range(2)]
                s_mm, maxed = sem(f"scores_ready_{t}"), sem(f"maxima_taken_{t}")
                m_turned, m_kept = sem(f"maxima_turned_{t}"), sem(f"maxima_kept_{t}")
                m_in = [sem(f"maxima_row_loaded{u}_{t}") for u in range(2)]
                st_mm, exped = sem(f"scores_T_ready_{t}"), sem(f"probs_ready_{t}")
                pv = sem(f"pv_done_{t}")
                ot_kept, turned = sem(f"out_T_kept_{t}"), sem(f"out_turned_{t}")
                recd, normed = sem(f"denominators_inverted_{t}"), sem(f"out_normalised_{t}")
                of_turned, of_kept = sem(f"out_F_turned_{t}"), sem(f"out_F_kept_{t}")
                proj, added = sem(f"out_projected_{t}"), sem(f"residual_added_{t}")
                otz = sem(f"out_banks_zeroed_{t}")
                NMAX = 1 + HG
                NPROB = 3 + 3 * HG + 1
                STEPS = B + 5
                LO, HI = 6, 30

                def steps(eng, step):
                    for s in range(LO):
                        step(s, s, False)
                    with every(eng, LO, HI, 8) as s0:
                        for u in range(8):
                            step(s0 + u if u else s0, (LO + u) % 8, True)
                    for s in range(HI, STEPS):
                        step(s, s % 8, False)

                def alive(s, loop, lag):
                    return loop or 0 <= s - lag < B

                def wait(eng, semaphore, s, loop, scale, offset):
                    if loop or scale * s + offset > 0:
                        eng.wait_ge(semaphore, s * scale + offset)

                with nc.Block() as block:
                    @block.sync
                    def _(sp):
                        q_hi, q_lo, k_hi, k_lo = range(4)

                        def part_rows(n, c):
                            return qk[n].rearrange("(g r) t -> r g t", g=NG)[:, :, span(c, CT)]

                        def part_heads(n, c):
                            return qk[n].rearrange("(g h d) t -> h d g t", g=NG, h=HG)[:, :, :, span(c, CT)]

                        def load_maxima(c, u):
                            sp.dma_start(QP[u][0:R, :, :], part_rows(q_hi, c)).then_inc(max_in[u], 16)
                            for h in range(HG):
                                sp.dma_start(KD[u][DK * h:DK * (h + 1), :, h, :],
                                             part_heads(k_hi, c)[h]).then_inc(max_in[u], 16)

                        def load_probs(c, u):
                            for n, part in enumerate((k_hi, k_lo, k_hi)):
                                sp.dma_start(KP[u][R * n:R * (n + 1), :, :], part_rows(part, c)).then_inc(prob_in[u], 16)
                            for n, part in enumerate((q_hi, q_hi, q_lo)):
                                for h in range(HG):
                                    a = R * n + DK * h
                                    sp.dma_start(QD[u][a:a + DK, :, h, :], part_heads(part, c)[h]).then_inc(prob_in[u], 16)

                        def load_v(c, u):
                            sp.dma_start(VR[:, u].rearrange("p b h v -> p (b h v)"),
                                         vs[:, span(c, CB * H * VW)]).then_inc(prob_in[u], 16)

                        sp.wait_ge(s_z, 2)
                        for u in range(2):
                            load_maxima(u, u)
                            load_probs(u, u)
                            load_v(u, u)
                        with every(sp, 2, NC, 2) as c:
                            for u in range(2):
                                sp.wait_ge(s_mm, (c + (u - 1)) * (CB * NG))
                                load_maxima(c + u if u else c, u)
                                sp.wait_ge(st_mm, (c + (u - 1)) * (CB * NG))
                                load_probs(c + u if u else c, u)
                                sp.wait_ge(pv, (c + (u - 1)) * (CB * NG))
                                load_v(c + u if u else c, u)

                    @block.tensor
                    def _(pe):
                        def scores(s, r, loop, g):
                            u, tok = r // CB, slice(r % CB * S, (r % CB + 1) * S)
                            if g == 0 and r % CB == 0:
                                wait(pe, max_in[u], s, loop, 2 * NMAX, 16 * NMAX - 2 * NMAX * r)
                            wait(pe, maxed, s, loop, NG, g - 1)
                            out = bank[g % 2][:, :]
                            if causal:
                                nc.tensor.matmul(out, identb[:, :], maskS[:, :, :], start=True, stop=False)
                            nc.tensor.matmul(out, QP[u][0:MROW, g, tok], KD[u][0:MROW, g, :, tok],
                                             start=not causal, stop=True).then_inc(s_mm, 1)

                        def scores_T(s, r, loop, g):
                            u, tok = r // CB, slice(r % CB * S, (r % CB + 1) * S)
                            if g == 0:
                                if r % CB == 0:
                                    wait(pe, prob_in[u], s, loop, 2 * NPROB, 16 * NPROB - 2 * NPROB * r)
                                wait(pe, m_in[r % 2], s, loop, 8, 16 - 8 * (r % 2))
                            wait(pe, exped, s, loop, NG, g - 1)
                            out = bank[2 + g % 2][:, :]
                            if causal:
                                nc.tensor.matmul(out, identb[:, :], maskT[:, :, :], start=True, stop=False)
                            nc.tensor.matmul(out, KP[u][0:MROW + 1, g, tok], QD[u][0:MROW + 1, g, :, tok],
                                             start=not causal, stop=True).then_inc(st_mm, 1)

                        def turn_maxima(s, r, loop):
                            wait(pe, maxed, s, loop, NG, NG)
                            wait(pe, normed, s, loop, 1, -2)
                            nc.tensor.transpose(bank[6][0:H, 0:S], M[:, r % 2, :], identf[:, :]).then_inc(m_turned, 1)

                        def product_v(s, r, loop, g):
                            wait(pe, exped, s, loop, NG, g + 1)
                            if g == 0:
                                wait(pe, ot_kept, s, loop, 1, -1)
                            for h in range(HG):
                                ins = nc.tensor.matmul(bank[4 + r % 2][32 * h:32 * h + VW, g * S:(g + 1) * S],
                                                       VR[:, r // CB, r % CB, HG * g + h, :],
                                                       PT[:, g, h * S:(h + 1) * S], start=True, stop=True,
                                                       tile_position=(0, 32 * h))
                            ins.then_inc(pv, 1)

                        def turn_out(s, r, loop):
                            wait(pe, ot_kept, s, loop, 1, 1)
                            if loop or s + 2 < B:
                                pe.wait_ge(m_kept, s + 3)
                            wait(pe, normed, s, loop, 1, 0)
                            for g in range(NG):
                                ins = nc.tensor.transpose(bank[6][:, g * S:(g + 1) * S],
                                                          OT[:, r % 2, g * S:(g + 1) * S], identf[:, :])
                            ins.then_inc(turned, 1)

                        def turn_normed(s, r, loop):
                            wait(pe, normed, s, loop, 1, 1)
                            wait(pe, added, s, loop, 1, 0)
                            nc.tensor.transpose(bank[7][:, 0:S], OQ[:, r % 2, :], identf[:, :]).then_inc(of_turned, 1)

                        def project_out(s, r, loop):
                            wait(pe, of_kept, s, loop, 1, 1)
                            nc.tensor.matmul(bank[7][:, S:S + D], OF[:, r % 2, :], WO[:, L, :],
                                             start=True, stop=True).then_inc(proj, 1)

                        def step(s, r, loop):
                            def at(lag):
                                return s - lag if lag else s, (r - lag) % 8, loop
                            for g in range(NG):
                                if alive(s, loop, 0):
                                    scores(*at(0), g)
                                if alive(s, loop, 2):
                                    scores_T(*at(2), g)
                                if g == 1 and alive(s, loop, 1):
                                    turn_maxima(*at(1))
                                if g == 1 and alive(s, loop, 5):
                                    project_out(*at(5))
                                if g == 3 and alive(s, loop, 4):
                                    turn_normed(*at(4))
                                lag = 3 if g < 2 else 2
                                if alive(s, loop, lag):
                                    product_v(*at(lag), (g + 2) % NG)
                            if alive(s, loop, 3):
                                turn_out(*at(3))

                        pe.wait_ge(otz, 2)
                        steps(pe, step)

                    @block.vector
                    def _(dve):
                        def normalise(s, r, loop):
                            wait(dve, turned, s, loop, 1, 1)
                            wait(dve, of_turned, s, loop, 1, -1)
                            out = bank[6][:, :].rearrange("p (h v) -> p h v", v=32)
                            nc.vector.reciprocal(REC[:, r % 2, :].unsqueeze(2), out[:, :, DK:DK + 1]).then_inc(recd, 1)
                            wait(dve, recd, s, loop, 1, 1)
                            nc.vector.tensor_tensor(OQ[:, r % 2, :].rearrange("p (h d) -> p h d", d=DK), out[:, :, 0:DK],
                                                    REC[:, r % 2, :].unsqueeze(2).to_broadcast([P, H, DK]),
                                                    ALU.mult).then_inc(normed, 1)

                        def maxima(s, r, loop, g):
                            if g == 0:
                                wait(dve, m_turned, s, loop, 1, -1)
                            wait(dve, s_mm, s, loop, NG, g + 1)
                            nc.vector.tensor_reduce(M[:, r % 2, HG * g:HG * (g + 1)],
                                                    bank[g % 2][:, :].rearrange("p (h t) -> p h t", t=S),
                                                    AX.X, ALU.max).then_inc(maxed, 1)

                        def residual(s, r, loop):
                            wait(dve, proj, s, loop, 1, 1)
                            xs = X[:, ds(s, 1), :].rearrange("p o d -> p (o d)") if loop else X[:, s, :]
                            st = STATS[:, ds(s, 1), :].rearrange("p o d -> p (o d)") if loop else STATS[:, s, :]
                            nc.vector.tensor_tensor(xs, bank[7][:, S:S + D], xs, ALU.add).then_inc(added, 1)
                            wait(dve, added, s, loop, 1, 1)
                            nc.vector.bn_stats(st, xs)

                        def step(s, r, loop):
                            for g in range(NG):
                                if alive(s, loop, 0):
                                    maxima(s, r, loop, g)
                                if g == 0 and alive(s, loop, 4):
                                    normalise(s - 4, (r - 4) % 8, loop)
                                if g == 2 and alive(s, loop, 5):
                                    residual(s - 5, (r - 5) % 8, loop)

                        for n in (4, 5):
                            nc.vector.memset(bank[n][:, :], 0.0).then_inc(otz, 1)
                        steps(dve, step)

                    @block.scalar
                    def _(act):
                        def probs(s, r, loop, g):
                            wait(act, st_mm, s, loop, NG, g + 1)
                            wait(act, pv, s, loop, NG, g - 3)
                            nc.scalar.activation(PT[:, g, :], bank[2 + g % 2][:, :], ACT.Exp,
                                                 scale=SCALE).then_inc(exped, 1)

                        def keep_maxima(s, r, loop):
                            u, tok = r // CB, slice(r % CB * S, (r % CB + 1) * S)
                            wait(act, m_turned, s, loop, 1, 1)
                            wait(act, m_in[r % 2], s, loop, 8, -8 * (r % 2))
                            nc.scalar.mul(MT[:, r % 2, :], bank[6][0:H, 0:S], -1.0 / MSCALE).then_inc(m_kept, 1)
                            wait(act, m_kept, s, loop, 1, 1)
                            act.dma_start(QD[u][MROW:MROW + 1, :, :, tok].rearrange("p g h t -> p (g h) t"),
                                          MT[:, r % 2, :]).then_inc(m_in[r % 2], 16)

                        def keep_out_T(s, r, loop):
                            wait(act, pv, s, loop, NG, NG)
                            wait(act, turned, s, loop, 1, -1)
                            nc.scalar.copy(OT[:, r % 2, :], bank[4 + r % 2][:, :]).then_inc(ot_kept, 1)

                        def keep_out_F(s, r, loop):
                            wait(act, of_turned, s, loop, 1, 1)
                            wait(act, proj, s, loop, 1, -1)
                            nc.scalar.copy(OF[:, r % 2, :], bank[7][:, 0:S]).then_inc(of_kept, 1)

                        def step(s, r, loop):
                            def at(lag):
                                return s - lag if lag else s, (r - lag) % 8, loop
                            for g in range(NG):
                                if alive(s, loop, 2):
                                    probs(*at(2), g)
                                if g == 1:
                                    if alive(s, loop, 1):
                                        keep_maxima(*at(1))
                                    if alive(s, loop, 3):
                                        keep_out_T(*at(3))
                            if alive(s, loop, 4):
                                keep_out_F(*at(4))

                        steps(act, step)

        SIG = sb("SIG", [P, 2])
        SW = sb("SW", [P, 2 * NI + 1])
        SWX = sb("SWX", [P, 2 * NI])
        SACT = sb("SACT", [P, 2])
        INV = sb("INV", [P, 2])
        AMX = sb("AMX", [P, 2, 2])
        WGT = sb("WGT", [P, 2, INNER], BF16)
        WDT = sb("WDT", [P, NI, D], BF16)
        SDB = sb("SDB", [P, D])

        def ffn_weights():
            with ExitStack() as own:
                WR = own.enter_context(nc.sbuf_tensor("WR", [P, 2 * NI, D], F32))
                WDR = own.enter_context(nc.sbuf_tensor("WDR", [P, INNER], F32))
                clips = own.enter_context(nc.sbuf_tensor("clips", [P, 2], F32))
                ISW = own.enter_context(nc.sbuf_tensor("ISW", [P, 2 * NI + 1], F32))
                sd_diag = own.enter_context(nc.sbuf_tensor("sd_diag", [P, D], F32))
                ffn_in, small_in, x_in = sem("ffn_weights_loaded"), sem("small_loaded"), sem("x_loaded")
                expd, chain, quantised = sem("clips_exped"), sem("prep_chain"), sem("weights_quantised")
                turned, made = sem("weights_turned"), sem("biases_made")
                done = sem("prep_copied")
                small = [(identf[:, :], consts["identf"]), (identb[:, :], consts["identb"]),
                         (maskS[:, :, :], consts["maskS"]), (maskT[:, :, :], consts["maskT"]),
                         (clips[:, 0:1], w["clip_x"].partition_broadcast(P)),
                         (clips[:, 1:2], w["clip_down"].partition_broadcast(P))]
                for L in range(2):
                    small += [(WQ[:, L, :], w[f"Wq{L}"]), (WK[:, L, :], w[f"Wk{L}"]),
                              (WV[:, L, :], w[f"Wv{L}"]), (WO[:, L, :], w[f"Wo{L}"]),
                              (bvc[:, L:L + 1], w[f"bv{L}"]), (bor[:, L, :], w[f"bo{L}"])]
                small += [(bqk[:, 0, 0:1], w["bq0"]), (bqk[:, 0, 1:2], w["bk0"])]
                ffn = []
                for k, name in enumerate(("w_gate", "w_up")):
                    for i, rows in enumerate(ROWS):
                        ffn.append((WR[0:rows, NI * k + i, :], w[name][P * i:P * i + rows, :]))
                ffn.append((WDR[:, :], w["w_down"]))
                with nc.Block() as block:
                    @block.sync
                    def _(sp):
                        for n in range(NC):
                            sp.dma_start(X[:, CB * n:CB * (n + 1), :],
                                         x[CB * n:CB * (n + 1)].rearrange("b s d -> s b d")).then_inc(x_in, 16)
                        for dst, src in ffn:
                            sp.dma_start(dst, src).then_inc(ffn_in, 16)

                    @block.gpsimd
                    def _(pool):
                        nc.gpsimd.memset(HBUF[96:P, NI - 1, :], 0.0).then_inc(done, 1)
                        pool.wait_ge(done, 1)
                        nc.gpsimd.memset(ARENA[:, 0:10240], 0.0).then_inc(s_z, 1)
                        pool.wait_ge(s_z, 2)
                        for u in range(2):
                            if u:
                                pool.wait_ge(made, 5)
                            nc.gpsimd.memset(KP[u][MROW:MROW + 1, :, :], MSCALE).then_inc(made, 1)

                    @block.vector
                    def _(dve):
                        count = [0]

                        def link(ins):
                            count[0] += 1
                            ins.then_inc(chain, 1)
                            dve.wait_ge(chain, count[0])

                        nc.vector.memset(onesf[:, :], 1.0).then_inc(made, 1)
                        nc.vector.memset(bqk[:, 1, :], 0.0).then_inc(made, 1)
                        dve.wait_ge(small_in, 16 * len(small))
                        for L in range(2):
                            nc.vector.tensor_scalar(BVW[:, L, :], identf[:, :], 0.0, bvc[:, L:L + 1],
                                                    ALU.mult, ALU.add).then_inc(made, 1)
                        dve.wait_ge(expd, 1)
                        link(nc.vector.tensor_scalar(SIG[:, :], SIG[:, :], 1.0, None, ALU.add))
                        link(nc.vector.reciprocal(SIG[:, :], SIG[:, :]))
                        dve.wait_ge(ffn_in, 16 * len(ffn))
                        mats = [(WR[0:ROWS[k % NI], k, :], SW[0:ROWS[k % NI], k:k + 1]) for k in range(2 * NI)]
                        mats.append((WDR[:, :], SW[:, 2 * NI:2 * NI + 1]))
                        for k, (m, scale) in enumerate(mats):
                            link(nc.vector.tensor_reduce(scale, m, AX.X, ALU.max, apply_absolute_value=True))
                            link(nc.vector.tensor_scalar(scale, scale, 1.0 / QMAX, None, ALU.mult))
                            inv = ISW[0:m.shape[0], k:k + 1]
                            link(nc.vector.reciprocal(inv, scale))
                            link(nc.vector.tensor_scalar(m, m, inv, MAGIC, ALU.mult, ALU.add))
                            link(nc.vector.tensor_scalar(m, m, MAGIC, QMAX, ALU.subtract, ALU.min))
                        nc.vector.tensor_scalar(sd_diag[:, :], identf[:, :], SW[:, 2 * NI:2 * NI + 1], None,
                                                ALU.mult).then_inc(quantised, 1)
                        for n in range(NC):
                            pass
                        dve.wait_ge(x_in, 16 * NC)
                        for b in range(B):
                            ins = nc.vector.bn_stats(STATS[:, b, :], X[:, b, :])
                        ins.then_inc(chain, 1)
                        nc.vector.memset(ARENA[:, 10240:20480], 0.0).then_inc(s_z, 1)

                    @block.scalar
                    def _(act):
                        for dst, src in small:
                            act.dma_start(dst, src).then_inc(small_in, 16)
                        act.wait_ge(small_in, 16 * len(small))
                        nc.scalar.activation(SIG[:, :], clips[:, :], ACT.Exp, scale=-1.0).then_inc(expd, 1)
                        act.wait_ge(turned, 1)
                        for k in range(2):
                            nc.scalar.copy(WGT[:, k, :], bank[k][:, 0:INNER]).then_inc(done, 1)
                        nc.scalar.copy(WDT[:, 0:NI - 1, :], bank[2][:, 0:(NI - 1) * D]).then_inc(done, 1)
                        nc.scalar.copy(WDT[0:ROWS[-1], NI - 1, :], bank[3][0:ROWS[-1], 0:D]).then_inc(done, 1)
                        nc.scalar.copy(SDB[:, :], bank[4][:, 0:D]).then_inc(done, 1)
                        for L in range(2):
                            nc.scalar.copy(BO[:, L, :], bank[5 + L][:, 0:D]).then_inc(done, 1)

                    @block.tensor
                    def _(pe):
                        pe.wait_ge(quantised, 1)
                        pe.wait_ge(small_in, 16 * len(small))
                        for k in range(2):
                            for i, rows in enumerate(ROWS):
                                nc.tensor.transpose(bank[k][:, P * i:P * i + rows], WR[0:rows, NI * k + i, :],
                                                    identf[0:rows, 0:rows])
                        for i, rows in enumerate(ROWS):
                            out = bank[2][:, P * i:P * (i + 1)] if i < NI - 1 else bank[3][0:rows, 0:D]
                            nc.tensor.transpose(out, WDR[:, P * i:P * i + rows], identf[:, :])
                        pe.wait_ge(made, 6)
                        nc.tensor.matmul(bank[4][:, 0:D], onesf[:, :], sd_diag[:, :], start=True, stop=True)
                        for L in range(2):
                            nc.tensor.matmul(bank[5 + L][:, 0:D], BVW[:, L, :], WO[:, L, :], start=True, stop=False)
                            ins = nc.tensor.matmul(bank[5 + L][:, 0:D], onesf[0:1, :], bor[:, L, :],
                                                   start=False, stop=True)
                        ins.then_inc(turned, 1)

        def pipeline(eng, stages, peel=2):
            deepest = max(lag for lag, _ in stages)
            assert deepest <= peel and peel % 2 == 0
            for n in range(peel):
                for lag, stage in stages:
                    if n >= lag:
                        stage(n - lag, (n - lag) % 2)
            with every(eng, peel, NC, 2) as c:
                for u in range(2):
                    for lag, stage in stages:
                        stage(c + (u - lag) if u != lag else c, (u - lag) % 2)
            for n in range(NC, NC + deepest):
                for lag, stage in stages:
                    if n - lag < NC:
                        stage(n - lag, (n - lag) % 2)

        def ffn():
            XN = XNT[:, :].rearrange("p (b d) -> p b d", d=D)
            with ExitStack() as own:
                def osb(name, shape, dt=F32):
                    return own.enter_context(nc.sbuf_tensor(name, shape, dt))
                QX = osb("QX", [P, 2, CB, D])
                XQ = osb("XQ", [P, 2, CT], BF16)
                SL = osb("SL", [P, 2, CT])
                HQ = osb("HQ", [P, 2, NI, CT], BF16)
                YB = osb("YB", [P, 2, CT])
                CM = osb("CM", [P, NC])
                normalise_and_amax(XN)
                ffn_up(XN, QX, XQ, SL, CM)
                hidden_amax(CM)
                ffn_down(HQ, YB)

        def whole_amax(which, maxed, reduced, pool):
            pool.wait_ge(maxed, 1)
            nc.gpsimd.partition_all_reduce(AMX[:, which, 1:2], AMX[:, which, 0:1], P, ABSMAX).then_inc(reduced, 1)

        def activation_scale(which, reduced, scaled, dve):
            dve.wait_ge(reduced, 1)
            nc.vector.tensor_scalar(SACT[:, which:which + 1], AMX[:, which, 1:2], SIG[:, which:which + 1],
                                    1.0 / QMAX, ALU.mult, ALU.mult).then_inc(scaled, 1)
            dve.wait_ge(scaled, 1)
            nc.vector.reciprocal(INV[:, which:which + 1], SACT[:, which:which + 1])

        def normalise_and_amax(XN):
            chain, maxed, reduced, scaled = sem("x_normed"), sem("x_amax_part"), sem("x_amax_all"), sem("x_scale")
            STEP = 16
            with nc.Block() as block:
                @block.vector
                def _(dve):
                    with every(dve, 0, B, STEP) as b0:
                        for j in range(STEP):
                            b = b0 + j if j else b0
                            ins = nc.vector.tensor_scalar(XN[:, ds(b, 1), :], X[:, ds(b, 1), :], MEAN[:, ds(b, 1)],
                                                          RSTD[:, ds(b, 1)], ALU.subtract, ALU.mult)
                        ins.then_inc(chain, 1)
                    dve.wait_ge(chain, B // STEP)
                    nc.vector.tensor_reduce(AMX[:, 0, 0:1], XNT[:, :], AX.X, ALU.max,
                                            apply_absolute_value=True).then_inc(maxed, 1)
                    activation_scale(0, reduced, scaled, dve)
                    for k in range(2 * NI):
                        rows = ROWS[k % NI]
                        nc.vector.tensor_scalar(SWX[0:rows, k:k + 1], SW[0:rows, k:k + 1], SACT[0:rows, 0:1],
                                                None, ALU.mult)

                @block.gpsimd
                def _(pool):
                    whole_amax(0, maxed, reduced, pool)

        def hidden_amax(CM):
            maxed, reduced, scaled = sem("h_amax_part"), sem("h_amax_all"), sem("h_scale")
            with nc.Block() as block:
                @block.vector
                def _(dve):
                    nc.vector.tensor_reduce(AMX[:, 1, 0:1], CM[:, :], AX.X, ALU.max).then_inc(maxed, 1)
                    activation_scale(1, reduced, scaled, dve)

                @block.gpsimd
                def _(pool):
                    whole_amax(1, maxed, reduced, pool)

        def ffn_up(XN, QX, XQ, SL, CM):
            FREE = 2
            rounded, quant, turned, xq = sem("x_rounded"), sem("x_quantised"), sem("x_turned"), sem("x_integers")
            gate_mm, up_mm, silu, hid = sem("gate_mm"), sem("up_mm"), sem("silu_done"), sem("hidden_done")
            with nc.Block() as block:
                @block.vector
                def _(dve):
                    def quantise(n, u):
                        dve.wait_ge(turned, n + 1)
                        nc.vector.tensor_scalar(QX[:, u], XN[:, span(n, CB), :], INV[:, 0:1], MAGIC,
                                                ALU.mult, ALU.add).then_inc(rounded, 1)
                        dve.wait_ge(rounded, n + 1)
                        nc.vector.tensor_scalar(QX[:, u], QX[:, u], MAGIC + QMAX, MAGIC - QMAX - 1.0,
                                                ALU.min, ALU.max).then_inc(quant, 1)

                    def hidden(n, u):
                        for i, rows in enumerate(ROWS):
                            k = (u + i) % 2
                            dve.wait_ge(up_mm, n * NI + (i + 1 + NI * FREE))
                            dve.wait_ge(silu, n * NI + (i + 1 + FREE))
                            nc.vector.scalar_tensor_tensor(HBUF[0:rows, i, span(n, CT)], bank[2 + k][0:rows, :],
                                                           SWX[0:rows, NI + i:NI + i + 1], SL[0:rows, k, :],
                                                           ALU.mult, ALU.mult).then_inc(hid, 1)

                    def chunk_max(n, u):
                        dve.wait_ge(hid, n * NI + (NI + FREE))
                        nc.vector.tensor_reduce(CM[:, span(n, 1)], HBUF[:, :, span(n, CT)], AX.XY, ALU.max,
                                                apply_absolute_value=True)

                    dve.sem_inc(hid, FREE)
                    pipeline(dve, [(0, quantise), (2, chunk_max), (1, hidden)])

                @block.tensor
                def _(pe):
                    def turn(n, u):
                        pe.wait_ge(quant, n + 1)
                        pe.wait_ge(xq, n + 1)
                        for j in range(CB):
                            ins = nc.tensor.transpose(bank[6 + u][:, j * S:(j + 1) * S], QX[:, u, j, :], identf[:, :])
                        ins.then_inc(turned, 1)

                    def gate_up(*tiles):
                        def stage(n, u):
                            for i in tiles:
                                rows, k = ROWS[i], (u + i) % 2
                                if i == 0:
                                    pe.wait_ge(xq, n + (1 + FREE))
                                pe.wait_ge(silu, n * NI + (i + 1))
                                nc.tensor.matmul(bank[k][0:rows, :], WGT[:, 0, P * i:P * i + rows], XQ[:, u, :],
                                                 start=True, stop=True).then_inc(gate_mm, 1)
                                pe.wait_ge(hid, n * NI + (i + 1))
                                nc.tensor.matmul(bank[2 + k][0:rows, :], WGT[:, 1, P * i:P * i + rows], XQ[:, u, :],
                                                 start=True, stop=True).then_inc(up_mm, 1)
                        return stage

                    pe.sem_inc(turned, FREE)
                    pe.sem_inc(up_mm, NI * FREE)
                    pipeline(pe, [(1, gate_up(0, 1)), (0, turn), (1, gate_up(2))])

                @block.scalar
                def _(act):
                    def integers(n, u):
                        act.wait_ge(turned, n + (1 + FREE))
                        act.wait_ge(up_mm, n * NI + NI)
                        nc.scalar.activation(XQ[:, u, :], bank[6 + u][:, :], ACT.Copy, bias=-MAGIC).then_inc(xq, 1)

                    def gate_silu(*tiles):
                        def stage(n, u):
                            for i in tiles:
                                rows, k = ROWS[i], (u + i) % 2
                                act.wait_ge(gate_mm, n * NI + (i + 1))
                                act.wait_ge(hid, n * NI + (i + 1))
                                nc.scalar.activation(SL[0:rows, k, :], bank[k][0:rows, :], ACT.Silu,
                                                     scale=SWX[0:rows, i:i + 1]).then_inc(silu, 1)
                        return stage

                    act.sem_inc(xq, FREE)
                    act.sem_inc(silu, FREE)
                    pipeline(act, [(1, gate_silu(0, 1)), (0, integers), (1, gate_silu(2))])

        def ffn_down(HQ, YB):
            FREE = 2
            rounded, clipped, ints = sem("h_rounded"), sem("h_clipped"), sem("h_integers")
            down, scaled, added = sem("down_mm"), sem("down_scaled"), sem("ffn_added")
            with nc.Block() as block:
                @block.scalar
                def _(act):
                    def round_hidden(n, u):
                        h = HBUF[:, :, span(n, CT)]
                        nc.scalar.activation(h, h, ACT.Copy, bias=MAGIC, scale=INV[:, 1:2]).then_inc(rounded, 1)

                    def integers(n, u):
                        act.wait_ge(down, n + 1)
                        act.wait_ge(clipped, n + 1)
                        nc.scalar.activation(HQ[:, u], HBUF[:, :, span(n, CT)], ACT.Copy,
                                             bias=-MAGIC).then_inc(ints, 1)

                    pipeline(act, [(0, round_hidden), (2, integers)])

                @block.vector
                def _(dve):
                    def clip(n, u):
                        h = HBUF[:, :, span(n, CT)]
                        dve.wait_ge(rounded, n + 1)
                        nc.vector.tensor_scalar(h, h, MAGIC + QMAX, MAGIC - QMAX - 1.0,
                                                ALU.min, ALU.max).then_inc(clipped, 1)

                    def scale_out(n, u):
                        dve.wait_ge(down, n + (1 + FREE))
                        dve.wait_ge(added, n + 1)
                        nc.vector.scalar_tensor_tensor(YB[:, u, :].rearrange("p (b d) -> p b d", d=D),
                                                       bank[u][:, :].rearrange("p (b d) -> p b d", d=D),
                                                       SACT[:, 1:2], SDB[:, :].unsqueeze(1).to_broadcast([P, CB, D]),
                                                       ALU.mult, ALU.mult).then_inc(scaled, 1)

                    def stats(n, u):
                        dve.wait_ge(added, n + (1 + FREE))
                        for j in range(CB):
                            b = n * CB + j
                            nc.vector.bn_stats(STATS[:, span(b, 1), :], X[:, span(b, 1), :])

                    dve.sem_inc(scaled, FREE)
                    pipeline(dve, [(0, clip), (3, scale_out), (4, stats)], peel=4)

                @block.gpsimd
                def _(pool):
                    def add(n, u):
                        pool.wait_ge(scaled, n + (1 + FREE))
                        xs = X[:, span(n, CB), :]
                        nc.gpsimd.tensor_tensor(xs, YB[:, u, :].rearrange("p (b d) -> p b d", d=D), xs,
                                                ALU.add).then_inc(added, 1)

                    pool.sem_inc(added, FREE)
                    pipeline(pool, [(0, add)])

                @block.tensor
                def _(pe):
                    def down_mm(n, u):
                        pe.wait_ge(ints, n + 1)
                        pe.wait_ge(scaled, n + 1)
                        for j in range(CB):
                            for i, rows in enumerate(ROWS):
                                ins = nc.tensor.matmul(bank[u][:, j * D:(j + 1) * D],
                                                       HQ[0:rows, u, i, j * S:(j + 1) * S], WDT[0:rows, i, :],
                                                       start=(i == 0), stop=(i == NI - 1))
                        ins.then_inc(down, 1)

                    pe.sem_inc(down, FREE)
                    pipeline(pe, [(0, down_mm)])

        moe_w = HBUF[:, :, :].rearrange("p i t -> p (i t)")
        n_w = (E + 1) * D
        w_raw = ARENA[:, 0:3 * n_w]
        w_hi, w_lo = (moe_w[:, 0:3 * n_w].bitcast(F16)[:, n * 3 * n_w:(n + 1) * 3 * n_w] for n in range(2))
        W1, W3, W2 = ([part[:, n * n_w:(n + 1) * n_w].rearrange("p (e i) -> p e i", i=D) for part in (w_hi, w_lo)]
                      for n in range(3))
        XH, XL = (ARENA[:, 16384:16384 + NT].bitcast(F16)[:, n * NT:(n + 1) * NT] for n in range(2))

        def router(gscr):
            with ExitStack() as own:
                def osb(name, shape, dt=F32):
                    return own.enter_context(nc.sbuf_tensor(name, shape, dt))
                GW = osb("GW", [P, E])
                EB = osb("EB", [P, E])
                T8 = osb("T8", [P, B, 8])
                RAW, BI, GT_, EQ, SC, SC2 = (osb(n, [P, B, E]) for n in ("RAW", "BI", "GTR", "EQ", "SC", "SC2"))
                CNT = osb("CNT", [P, B])
                GTT = osb("GTT", [P, 4, P])
                LT = moe_w[0:E, 3 * n_w:3 * n_w + NT]
                w_in, gw_in = sem("experts_loaded"), sem("router_loaded")
                x_hi, wt_hi = sem("tokens_hi_made"), sem("weights_hi_made")
                lg, lk, lt = sem("logits_T"), sem("logits_T_kept"), sem("logits")
                chain, topped, ex = sem("router_chain"), sem("top8"), sem("router_exp")
                g_ready, g_turned, g_kept, g_out = sem("gates"), sem("gates_turned"), sem("gates_kept"), sem("gates_stored")
                with nc.Block() as block:
                    @block.sync
                    def _(sp):
                        sp.dma_start(GW[:, :], w["gate_w"]).then_inc(gw_in, 16)
                        sp.dma_start(EB[:, :], w["expert_bias"].partition_broadcast(P)).then_inc(gw_in, 16)
                        for n, (a, b) in enumerate((("w1", "sw1"), ("w3", "sw3"), ("w2", "sw2"))):
                            dst = w_raw[:, n * n_w:(n + 1) * n_w].rearrange("p (e i) -> p e i", i=D)
                            sp.dma_start(dst[:, 0:E, :], w[a]).then_inc(w_in, 16)
                            sp.dma_start(dst[:, E, :], w[b]).then_inc(w_in, 16)
                        sp.wait_ge(g_kept, 1)
                        to = gscr.rearrange("e (T n k) -> n e T k", T=4, n=8)
                        for n in range(8):
                            sp.dma_start(to[n], GTT[E * n:E * (n + 1), :, :]).then_inc(g_out, 16)
                        sp.wait_ge(g_out, 16 * 8)

                    @block.gpsimd
                    def _(pool):
                        pool.wait_ge(x_hi, 1)
                        nc.gpsimd.tensor_tensor(XL, XNT[:, :], XH, ALU.subtract)
                        pool.wait_ge(wt_hi, 1)
                        nc.gpsimd.tensor_tensor(w_lo, w_raw, w_hi, ALU.subtract)

                    @block.tensor
                    def _(pe):
                        pe.wait_ge(gw_in, 32)
                        for n in range(NC):
                            nc.tensor.matmul(bank[n][0:E, :], GW[:, :], XNT[:, n * CT:(n + 1) * CT],
                                             start=True, stop=True).then_inc(lg, 1)
                        pe.wait_ge(lk, NC)
                        for b in range(B):
                            ins = nc.tensor.transpose(bank[0][:, b * E:(b + 1) * E], LT[:, b * S:(b + 1) * S],
                                                      identf[0:E, 0:E])
                        ins.then_inc(lt, 1)
                        pe.wait_ge(g_ready, 1)
                        flat = RAW[:, :, :].rearrange("p b e -> p (b e)")
                        for n in range(4):
                            ins = nc.tensor.transpose(bank[1][:, n * P:(n + 1) * P], flat[:, n * P:(n + 1) * P],
                                                      identf[:, :])
                        ins.then_inc(g_turned, 1)

                    @block.scalar
                    def _(act):
                        for n in range(NC):
                            act.wait_ge(lg, n + 1)
                            nc.scalar.copy(LT[:, n * CT:(n + 1) * CT], bank[n][0:E, :]).then_inc(lk, 1)
                        nc.scalar.copy(XH, XNT[:, :]).then_inc(x_hi, 1)
                        act.wait_ge(w_in, 16 * 6)
                        nc.scalar.copy(w_hi, w_raw).then_inc(wt_hi, 1)
                        act.wait_ge(ex, 1)
                        nc.scalar.activation(EQ[:, :, :], SC[:, :, :], ACT.Exp).then_inc(ex, 1)
                        act.wait_ge(g_turned, 1)
                        nc.scalar.copy(GTT[:, :, :], bank[1][:, :]).then_inc(g_kept, 1)

                    @block.vector
                    def _(dve):
                        count = [0]

                        def link(ins):
                            count[0] += 1
                            ins.then_inc(chain, 1)
                            dve.wait_ge(chain, count[0])

                        full = [P, B, E]
                        dve.wait_ge(lt, 1)
                        dve.wait_ge(gw_in, 32)
                        link(nc.vector.tensor_copy(RAW[:, :, :], bank[0][:, :]))
                        link(nc.vector.tensor_tensor(BI[:, :, :], RAW[:, :, :],
                                                     EB[:, :].unsqueeze(1).to_broadcast(full), ALU.add))
                        for b in range(B):
                            ins = nc.vector.max(T8[:, b, :], BI[:, b, :])
                        link(ins)
                        fourth = T8[:, :, TOPK - 1:TOPK].to_broadcast(full)
                        nc.vector.tensor_tensor(GT_[:, :, :], BI[:, :, :], fourth, ALU.is_gt)
                        link(nc.vector.tensor_tensor(EQ[:, :, :], BI[:, :, :], fourth, ALU.is_equal))
                        link(nc.vector.tensor_reduce(CNT[:, :], GT_[:, :, :], AX.X, ALU.add))
                        link(nc.vector.tensor_scalar(CNT[:, :], CNT[:, :], -1.0, float(TOPK), ALU.mult, ALU.add))
                        a, b_ = EQ, SC
                        for k in (1, 2, 4, 8):
                            nc.vector.tensor_copy(b_[:, :, 0:k], a[:, :, 0:k])
                            link(nc.vector.tensor_tensor(b_[:, :, k:E], a[:, :, k:E], a[:, :, 0:E - k], ALU.add))
                            a, b_ = b_, (SC2 if b_ is SC else SC)
                        link(nc.vector.tensor_tensor(b_[:, :, :], a[:, :, :], CNT[:, :].unsqueeze(2).to_broadcast(full),
                                                     ALU.is_le))
                        link(nc.vector.tensor_tensor(EQ[:, :, :], EQ[:, :, :], b_[:, :, :], ALU.mult))
                        link(nc.vector.tensor_tensor(GT_[:, :, :], GT_[:, :, :], EQ[:, :, :], ALU.add))
                        link(nc.vector.tensor_scalar(SC[:, :, :], GT_[:, :, :], -1.0, BIG, ALU.add, ALU.mult))
                        link(nc.vector.tensor_tensor(SC[:, :, :], SC[:, :, :], RAW[:, :, :], ALU.add))
                        link(nc.vector.tensor_reduce(CNT[:, :], SC[:, :, :], AX.X, ALU.max))
                        nc.vector.tensor_tensor(SC[:, :, :], SC[:, :, :], CNT[:, :].unsqueeze(2).to_broadcast(full),
                                                ALU.subtract).then_inc(ex, 1)
                        dve.wait_ge(ex, 2)
                        link(nc.vector.tensor_reduce(CNT[:, :], EQ[:, :, :], AX.X, ALU.add))
                        link(nc.vector.reciprocal(CNT[:, :], CNT[:, :]))
                        nc.vector.tensor_tensor(RAW[:, :, :], EQ[:, :, :], CNT[:, :].unsqueeze(2).to_broadcast(full),
                                                ALU.mult).then_inc(g_ready, 1)

        def experts(gscr):
            FREE = 2
            EN = E + 1
            ITEMS = 2 * EN
            with ExitStack() as own:
                def osb(name, shape, dt=F32):
                    return own.enter_context(nc.sbuf_tensor(name, shape, dt))
                G = [ARENA[:, n * E * CT:(n + 1) * E * CT].rearrange("p (e t) -> p e t", t=CT) for n in range(2)]
                SL = osb("SLE", [P, 2, CT])
                UG = osb("UG", [P, 2, CT])
                HE = osb("HE", [P, 2, CT])
                HH = osb("HH", [P, 2, CT], F16)
                HL = osb("HLE", [P, 2, CT], F16)
                XR = osb("XR", [P, 2, CB, D])
                YT = osb("YT", [P, 2, CT])
                g_in = [sem(f"gates_loaded{u}") for u in range(2)]
                gate_mm, up_mm, down, y_mm = sem("e_gate_mm"), sem("e_up_mm"), sem("e_down_mm"), sem("y_mm")
                silu, gated, hid = sem("e_silu"), sem("e_gated"), sem("e_hidden")
                hid_hi, hid_lo = sem("e_hidden_hi"), sem("e_hidden_lo")
                xr, yk = sem("x_ringed"), sem("y_kept")
                stored = [sem(f"out_stored{u}") for u in range(2)]

                def passes(eng, stages):
                    def one(c, first=False):
                        for j in range(ITEMS):
                            for lag, stage in stages:
                                if not first or j >= lag:
                                    stage(c, j - lag)
                    one(0, True)
                    with every(eng, 2, NC, 2) as c:
                        one(c)
                    for j in range(max(lag for lag, _ in stages)):
                        for lag, stage in stages:
                            if j < lag:
                                stage(NC, j - lag)

                def chunk(c, j):
                    return c + j // EN if j // EN else c

                with nc.Block() as block:
                    @block.sync
                    def _(sp):
                        def load(c, u):
                            tok = slice((c + u) * CT, (c + u + 1) * CT) if isinstance(c, int) else ds((c + u) * CT, CT)
                            sp.dma_start(G[u], gscr[:, tok].partition_broadcast(P)).then_inc(g_in[u], 16)

                        for u in range(2):
                            load(0, u)
                        with every(sp, 2, NC, 2) as c:
                            for u in range(2):
                                sp.wait_ge(hid, (c + (u - 1)) * EN + FREE)
                                load(c, u)

                    @block.gpsimd
                    def _(pool):
                        def make_lo(c, j):
                            k = j % 2
                            pool.wait_ge(hid_hi, c * EN + (j + 1))
                            nc.gpsimd.tensor_tensor(HL[:, k, :], HE[:, k, :], HH[:, k, :],
                                                    ALU.subtract).then_inc(hid_lo, 1)
                            if j % EN == 4:
                                pool.wait_ge(y_mm, chunk(c, j) + 1)
                                nc.gpsimd.tensor_copy(XR[:, j // EN], X[:, span(chunk(c, j), CB), :]).then_inc(xr, 1)

                        pool.sem_inc(hid_lo, FREE)
                        passes(pool, [(0, make_lo)])

                    @block.tensor
                    def _(pe):
                        def product(out, weights, e, hi, lo, first, last, own_group=True):
                            nc.tensor.matmul(out, weights[0][:, e, :], hi, start=first, stop=False,
                                             skip_group_check=not own_group)
                            nc.tensor.matmul(out, weights[0][:, e, :], lo, start=False, stop=False,
                                             skip_group_check=not own_group)
                            return nc.tensor.matmul(out, weights[1][:, e, :], hi, start=False, stop=last,
                                                    skip_group_check=not own_group)

                        def gate_up(c, j):
                            k, e = j % 2, j % EN
                            tok = span(chunk(c, j), CT)
                            pe.wait_ge(silu, c * EN + (j + 1))
                            product(bank[k][:, :], W1, e, XH[:, tok], XL[:, tok], True, True).then_inc(gate_mm, 1)
                            pe.wait_ge(hid, c * EN + (j + 1))
                            product(bank[2 + k][:, :], W3, e, XH[:, tok], XL[:, tok], True, True).then_inc(up_mm, 1)

                        def down_mm(c, j):
                            k, e, u = j % 2, j % EN, j // EN % 2
                            pe.wait_ge(hid_lo, c * EN + (j + 1 + FREE))
                            if e == 0:
                                pe.wait_ge(yk, chunk(c, j) + 1)
                            product(bank[4 + u][:, :], W2, e, HH[:, k, :], HL[:, k, :], e == 0, False,
                                    own_group=False).then_inc(down, 1)
                            if e == EN - 1:
                                pe.wait_ge(xr, chunk(c, j) + 1)
                                for b in range(CB):
                                    ins = nc.tensor.matmul(bank[4 + u][:, b * S:(b + 1) * S], XR[:, u, b, :],
                                                           identf[:, :], start=False, stop=(b == CB - 1),
                                                           skip_group_check=True)
                                ins.then_inc(y_mm, 1)

                        pe.sem_inc(down, FREE)
                        pe.sem_inc(y_mm, FREE)
                        passes(pe, [(0, gate_up), (2, down_mm)])

                    @block.scalar
                    def _(act):
                        def keep_y(c, j):
                            n, u = chunk(c, j), j // EN % 2
                            act.wait_ge(y_mm, n + (1 + FREE))
                            act.wait_ge(stored[u], (n - u) * 8 + 16)
                            nc.scalar.copy(YT[:, u, :], bank[4 + u][:, :]).then_inc(yk, 1)
                            act.wait_ge(yk, n + (1 + FREE))
                            act.dma_start(outT[:, span(n, CT)], YT[:, u, :]).then_inc(stored[u], 16)

                        def make_silu(c, j):
                            k = j % 2
                            act.wait_ge(gate_mm, c * EN + (j + 1))
                            act.wait_ge(hid, c * EN + (j + 1))
                            nc.scalar.activation(SL[:, k, :], bank[k][:, :], ACT.Silu).then_inc(silu, 1)

                        def make_hi(c, j):
                            k = j % 2
                            act.wait_ge(hid, c * EN + (j + 1 + FREE))
                            act.wait_ge(down, c * EN + (j + 1))
                            nc.scalar.copy(HH[:, k, :], HE[:, k, :]).then_inc(hid_hi, 1)
                            if j % EN == 4 and not (isinstance(c, int) and c == 0 and j == 4):
                                keep_y(c, j - EN)

                        act.sem_inc(silu, FREE)
                        act.sem_inc(yk, FREE)
                        for u in range(2):
                            act.sem_inc(stored[u], 16)
                        passes(act, [(0, make_silu), (1, make_hi)])
                        keep_y(NC, -1)
                        for u in range(2):
                            act.wait_ge(stored[u], 16 * (NC // 2 + 1))

                    @block.vector
                    def _(dve):
                        def hidden(c, j):
                            k, e, u = j % 2, j % EN, j // EN
                            if e == 0:
                                dve.wait_ge(g_in[u], c * 8 + 16)
                            dve.wait_ge(up_mm, c * EN + (j + 1))
                            up = bank[2 + k][:, :]
                            if e < E:
                                nc.vector.tensor_tensor(UG[:, k, :], up, G[u][:, e, :], ALU.mult).then_inc(gated, 1)
                                up = UG[:, k, :]
                                dve.wait_ge(gated, (c + u) * E + (e + 1))
                            dve.wait_ge(silu, c * EN + (j + 1 + FREE))
                            dve.wait_ge(hid_lo, c * EN + (j + 1))
                            nc.vector.tensor_tensor(HE[:, k, :], up, SL[:, k, :], ALU.mult).then_inc(hid, 1)

                        dve.sem_inc(hid, FREE)
                        passes(dve, [(0, hidden)])

        qk = [nc.dram_tensor(f"qk_scratch{L}", [4, P, NT], F16, kind="Internal").ap() for L in range(2)]
        vs = [nc.dram_tensor(f"v_scratch{L}", [P, B * H * VW], F32, kind="Internal").ap() for L in range(2)]
        gscr = nc.dram_tensor("gates_scratch", [E, NT], F32, kind="Internal").ap()

        def turn(tag):
            with nc.sbuf_tensor(f"XN_{tag}", [P, 2, CB, D], F32) as XN:
                ln_transpose(tag, XN)

        ffn_weights()
        ln_stats("a0")
        turn("a0")
        projections(0, qk[0], vs[0])
        attention(0, qk[0], vs[0])
        ln_stats("f0")
        ffn()
        ln_stats("a1")
        turn("a1")
        projections(1, qk[1], vs[1])
        attention(1, qk[1], vs[1])
        ln_stats("f1")
        turn("f1")
        router(gscr)
        experts(gscr)


def kernel(**inputs):
    import ml_dtypes
    import numpy as np
    import concourse.bacc as bacc
    from concourse.bass_utils import run_bass_kernel_spmd

    a = {k: np.asarray(v) for k, v in inputs.items()}
    i = np.arange(S)
    hidden = i[:, None] <= i[None, :]
    hidden[0, 0] = False
    neg = np.where(hidden, -BIG, 0.0).astype(ml_dtypes.bfloat16)
    arrays = {
        "x": a["x"],
        "ctxT": a["ctx_1024"].reshape(NT, D).T,
        "identf": np.eye(P, dtype=np.float32),
        "identb": np.eye(P).astype(ml_dtypes.bfloat16),
        "maskS": np.repeat(neg[:, None, :], HG, 1),
        "maskT": np.repeat(neg.T[:, None, :], HG, 1),
        "clip_x": a["L0_ffn_clip_x"], "clip_down": a["L0_ffn_clip_down"],
        "w_gate": a["L0_ffn_w_gate"], "w_up": a["L0_ffn_w_up"], "w_down": a["L0_ffn_w_down"],
        "bq0": a["L0_xattn_bq"].reshape(D, 1), "bk0": a["L0_xattn_bk"].reshape(D, 1),
        "gate_w": a["L1_ffn_gate_w"].T, "expert_bias": a["L1_ffn_expert_bias"],
        "w1": a["L1_ffn_w1"].transpose(2, 0, 1), "w3": a["L1_ffn_w3"].transpose(2, 0, 1),
        "w2": a["L1_ffn_w2"].transpose(2, 0, 1),
        "sw1": a["L1_ffn_sw1"].T, "sw3": a["L1_ffn_sw3"].T, "sw2": a["L1_ffn_sw2"].T,
    }
    for L in range(2):
        for n in "qkvo":
            arrays[f"W{n}{L}"] = a[f"L{L}_xattn_W{n}"].T
        arrays[f"bv{L}"] = a[f"L{L}_xattn_bv"].reshape(D, 1)
        arrays[f"bo{L}"] = a[f"L{L}_xattn_bo"].reshape(1, D)
    nc = bacc.Bacc("TRN2", target_bir_lowering=False, num_devices=1)
    fed, aps = {}, {}
    for name, array in arrays.items():
        array = np.ascontiguousarray(array)
        fed[f"in_{name}"] = array
        aps[name] = nc.dram_tensor(f"in_{name}", array.shape, mybir.dt.from_np(array.dtype), kind="ExternalInput").ap()
    outT = nc.dram_tensor("outT", (D, NT), F32, kind="ExternalOutput").ap()
    consts = {k: aps.pop(k) for k in ("identf", "identb", "maskS", "maskT")}
    build(nc, aps.pop("x"), aps.pop("ctxT"), aps, consts, outT)
    r = run_bass_kernel_spmd(nc, [fed], core_ids=[0])
    return np.ascontiguousarray(r.results[0]["outT"].T).reshape(B, S, D)
```

```python
from contextlib import ExitStack, contextmanager

import concourse.bass as bass
from concourse import mybir

F32 = mybir.dt.float32
F16 = mybir.dt.float16
BF16 = mybir.dt.bfloat16
ALU = mybir.AluOpType
ACT = mybir.ActivationFunctionType
AX = mybir.AxisListType
ABSMAX = bass.bass_isa.ReduceOp.absmax

P = 128
B = 32
S = 128
D = 128
H = 16
DK = D // H
HG = 4
NG = H // HG
CB = 4
CT = CB * S
NC = B // CB
NT = B * S
INNER = 352
ROWS = [128, 128, 96]
NI = len(ROWS)
E = 16
TOPK = 4
R = HG * DK
MROW = 3 * R
VW = DK + 1
SCALE = float(DK) ** -0.5
MSCALE = 1024.0
EPS = 1e-5
QMAX = 127.0
PACKED = P + 8 * D + 6
EARLY = 5
MAGIC = 12582912.0
BIG = 1e30


@contextmanager
def every(eng, first, end, step):
    with eng.Fori(0, (end - first) // step) as n:
        yield n * step + first


def span(n, size):
    return slice(n * size, (n + 1) * size) if isinstance(n, int) else bass.ds(n * size, size)


def pipeline(eng, stages, peel=2, at_tail=None):
    deepest = max(lag for lag, _ in stages)
    assert deepest <= peel and peel % 2 == 0
    for n in range(peel):
        for lag, stage in stages:
            if n >= lag:
                stage(n - lag, (n - lag) % 2)
    with every(eng, peel, NC, 2) as c:
        for u in range(2):
            for lag, stage in stages:
                stage(c + (u - lag) if u != lag else c, (u - lag) % 2)
    for n in range(NC, NC + deepest):
        if at_tail:
            at_tail(n - deepest, n % 2)
        for lag, stage in stages:
            if n - lag < NC:
                stage(n - lag, (n - lag) % 2)


def build(nc, x, ctxT, w, consts, outT):
    ds = bass.ds
    with ExitStack() as top:
        def sb(name, shape, dt=F32):
            return top.enter_context(nc.sbuf_tensor(name, shape, dt))

        def sem(name):
            return top.enter_context(nc.semaphore(name))

        X = sb("X", [P, B, D])
        XNT = sb("XNT", [P, NT])
        STATS = sb("STATS", [P, B, 6])
        MEAN = sb("MEAN", [P, B])
        RSTD = sb("RSTD", [P, B])
        XMAX = sb("XMAX", [P, B])
        XMIN = sb("XMIN", [P, B])
        tmpB = sb("tmpB", [P, 4, B])
        packed = sb("packed", [P, PACKED])
        identf = packed[:, 0:P]
        WQ, WK, WV, WO = (packed[:, P + 2 * D * n:P + 2 * D * (n + 1)].rearrange("p (l d) -> p l d", l=2)
                          for n in range(4))
        bqk = packed[:, PACKED - 6:PACKED - 2].rearrange("p (l n) -> p l n", l=2)
        bvc = packed[:, PACKED - 2:PACKED]
        packedb = sb("packedb", [P, P + HG * P], BF16)
        identb = packedb[:, 0:P]
        maskS = packedb[:, P:]
        onesf = sb("onesf", [P, P])
        bor = sb("bor", [1, 2, D])
        BVW = sb("BVW", [P, 2, D])
        BO = sb("BO", [P, 2, D])

        ARENA = sb("ARENA", [P, 20480])
        HBUF = sb("HBUF", [P, NI, NT])
        half = ARENA[:, :].bitcast(F16)
        QD = [half[:, n * 8192:(n + 1) * 8192].rearrange("p (g h t) -> p g h t", g=NG, h=HG) for n in (0, 1)]
        KD = [half[:, n * 8192:(n + 1) * 8192].rearrange("p (g h t) -> p g h t", g=NG, h=HG) for n in (2, 3)]
        QP = [half[:, 32768 + n * 2048:32768 + (n + 1) * 2048].rearrange("p (g t) -> p g t", g=NG) for n in (0, 1)]
        KP = [half[:, 36864 + n * 2048:36864 + (n + 1) * 2048].rearrange("p (g t) -> p g t", g=NG) for n in (0, 1)]

        bank = [top.enter_context(nc.psum_tensor(f"bank{n}", [P, 512], F32)) for n in range(8)]

        s_z = sem("arena_zeroed")
        ZEROED = 8192

        def ln_stats(tag):
            step = sem(f"ln_step_{tag}")
            with nc.Block() as block:
                @block.vector
                def _(dve):
                    me, mo = STATS[:, :, 1], STATS[:, :, 4]
                    ve, vo = STATS[:, :, 2], STATS[:, :, 5]
                    nc.vector.tensor_tensor(tmpB[:, 0, :], me, mo, ALU.add)
                    nc.vector.tensor_tensor(tmpB[:, 1, :], me, mo, ALU.subtract)
                    nc.vector.tensor_tensor(tmpB[:, 2, :], ve, vo, ALU.add).then_inc(step, 1)
                    dve.wait_ge(step, 1)
                    nc.vector.tensor_scalar(MEAN[:, :], tmpB[:, 0, :], 0.5, None, ALU.mult)
                    nc.vector.tensor_scalar(tmpB[:, 2, :], tmpB[:, 2, :], 1.0 / D, EPS, ALU.mult, ALU.add)
                    nc.vector.tensor_tensor(tmpB[:, 1, :], tmpB[:, 1, :], tmpB[:, 1, :], ALU.mult).then_inc(step, 1)
                    dve.wait_ge(step, 2)
                    nc.vector.scalar_tensor_tensor(tmpB[:, 3, :], tmpB[:, 1, :], 0.25, tmpB[:, 2, :],
                                                   ALU.mult, ALU.add).then_inc(step, 1)
                    dve.wait_ge(step, 3)
                    dve.wait_ge(step, 4)
                    nc.vector.reciprocal(RSTD[:, :], tmpB[:, 0, :]).then_inc(step, 1)
                    dve.wait_ge(step, 5)
                    nc.vector.tensor_tensor(tmpB[:, 1, :], RSTD[:, :], RSTD[:, :], ALU.mult).then_inc(step, 1)
                    dve.wait_ge(step, 6)
                    nc.vector.tensor_tensor(tmpB[:, 1, :], tmpB[:, 1, :], tmpB[:, 3, :], ALU.mult).then_inc(step, 1)
                    dve.wait_ge(step, 7)
                    nc.vector.tensor_scalar(tmpB[:, 1, :], tmpB[:, 1, :], -0.5, 1.5, ALU.mult, ALU.add).then_inc(step, 1)
                    dve.wait_ge(step, 8)
                    nc.vector.tensor_tensor(RSTD[:, :], tmpB[:, 1, :], RSTD[:, :], ALU.mult).then_inc(step, 1)
                    dve.wait_ge(step, 9)

                @block.scalar
                def _(act):
                    act.wait_ge(step, 3)
                    nc.scalar.activation(tmpB[:, 0, :], tmpB[:, 3, :], ACT.Sqrt).then_inc(step, 1)

        max_in = [[sem(f"maxima_operands_loaded{u}_L{L}") for u in range(2)] for L in range(2)]
        prob_in = [[sem(f"probs_operands_loaded{u}_L{L}") for u in range(2)] for L in range(2)]
        q_hi, q_lo, k_hi, k_lo = range(4)

        def part_rows(qk, n, c):
            return qk[n].rearrange("(g r) t -> r g t", g=NG)[:, :, span(c, CT)]

        def part_heads(qk, n, c):
            return qk[n].rearrange("(g h d) t -> h d g t", g=NG, h=HG)[:, :, :, span(c, CT)]

        def maxima_loads(qk, c, u):
            loads = [(QP[u][0:R, :, :], part_rows(qk, q_hi, c))]
            for h in range(HG):
                loads.append((KD[u][DK * h:DK * (h + 1), :, h, :], part_heads(qk, k_hi, c)[h]))
            return loads

        def probs_loads(qk, c, u):
            loads = [(KP[u][R * n:R * (n + 1), :, :], part_rows(qk, part, c))
                     for n, part in enumerate((k_hi, k_lo, k_hi))]
            for n, part in enumerate((q_hi, q_hi, q_lo)):
                for h in range(HG):
                    a = R * n + DK * h
                    loads.append((QD[u][a:a + DK, :, h, :], part_heads(qk, part, c)[h]))
            return loads

        def issue(sp, loads, semaphore):
            for dst, src in loads:
                sp.dma_start(dst, src).then_inc(semaphore, 16)

        def projections(L, qk, vs):
            t = f"L{L}"
            with ExitStack() as own:
                XN = own.enter_context(nc.sbuf_tensor(f"XN{L}", [P, 2, CB, D], F32))
                CX = own.enter_context(nc.sbuf_tensor(f"CX{L}", [P, 2, CT], F32))
                HL = own.enter_context(nc.sbuf_tensor(f"HL{L}", [P, 2, 4, CT], F16))
                VS = own.enter_context(nc.sbuf_tensor(f"VS{L}", [P, 2, CB * H, VW], F32))
                normed, turned, kept = sem(f"x_normed_{t}"), sem(f"x_turned_{t}"), sem(f"xnt_kept_{t}")
                cx_in = [sem(f"ctx_loaded{u}_{t}") for u in range(2)]
                q_mm, k_mm, v_mm = sem(f"q_mm_{t}"), sem(f"k_mm_{t}"), sem(f"v_mm_{t}")
                hi, lo, vc = sem(f"hi_made_{t}"), sem(f"lo_made_{t}"), sem(f"v_copied_{t}")
                stored = [sem(f"qkv_stored{u}_{t}") for u in range(2)]
                ones = sem(f"ones_set_{t}")
                NSTORE = 2
                FREE = 2
                with nc.Block() as block:
                    @block.gpsimd
                    def _(pool):
                        def add_bias(n, u):
                            pool.wait_ge(normed, n + 1)
                            xs = X[:, span(n, CB), :]
                            nc.gpsimd.tensor_tensor(xs, xs, BO[:, L, :].unsqueeze(1).to_broadcast([P, CB, D]), ALU.add)

                        nc.gpsimd.memset(VS[:, :, :, :], 1.0).then_inc(ones, 1)
                        if L == 0:
                            nc.gpsimd.memset(ARENA[:, ZEROED:], 0.0).then_inc(s_z, 1)
                            for u in range(2):
                                pool.wait_ge(s_z, 1 + u)
                                nc.gpsimd.memset(KP[u][MROW:MROW + 1, :, :], MSCALE).then_inc(s_z, 1)
                            pool.wait_ge(s_z, 3)
                        pipeline(pool, [(0, add_bias)])

                    @block.sync
                    def _(sp):
                        def load(n, u):
                            sp.wait_ge(v_mm, n + 1)
                            sp.dma_start(CX[:, u, :], ctxT[:, span(n, CT)]).then_inc(cx_in[u], 16)

                        def store(n, u):
                            sp.wait_ge(vc, n + (1 + FREE))
                            sp.dma_start(vs[:, span(n, CB * H * VW)], VS[:, u, :, :]).then_inc(stored[u], 16)
                            sp.wait_ge(lo, n * 2 + (2 + 2 * FREE))
                            sp.dma_start(qk[:, :, span(n, CT)].rearrange("n p t -> p n t"),
                                         HL[:, u, :, :]).then_inc(stored[u], 16)

                        def prefetch(n, u):
                            if n == NC - 2:
                                sp.wait_ge(stored[0], 16 * NSTORE * 2)
                                sp.wait_ge(s_z, 3)
                                issue(sp, maxima_loads(qk, 0, 0), max_in[L][0])
                                issue(sp, probs_loads(qk, 0, 0)[:EARLY], prob_in[L][0])

                        pipeline(sp, [(0, load), (2, store)], at_tail=prefetch)
                        for u in range(2):
                            sp.wait_ge(stored[u], 16 * NSTORE * (NC // 2 + 1))

                    @block.tensor
                    def _(pe):
                        def turn(n, u):
                            pe.wait_ge(normed, n + 1)
                            pe.wait_ge(kept, n + 1)
                            for j in range(CB):
                                ins = nc.tensor.transpose(bank[4 * u + 3][:, j * S:(j + 1) * S], XN[:, u, j, :],
                                                          identf[:, :])
                            ins.then_inc(turned, 1)

                        def project(n, u):
                            pe.wait_ge(lo, n * 2 + 2)
                            pe.wait_ge(cx_in[u], (n - u) * 8 + 16)
                            nc.tensor.matmul(bank[4 * u + 1][:, :], WK[:, L, :], CX[:, u, :],
                                             start=True, stop=True).then_inc(k_mm, 1)
                            pe.wait_ge(vc, n + 1)
                            for j in range(CB):
                                ins = nc.tensor.matmul(bank[4 * u + 2][:, j * D:(j + 1) * D],
                                                       CX[:, u, j * S:(j + 1) * S], WV[:, L, :],
                                                       start=True, stop=True)
                            ins.then_inc(v_mm, 1)
                            pe.wait_ge(kept, n + (1 + FREE))
                            nc.tensor.matmul(bank[4 * u][:, :], WQ[:, L, :], XNT[:, span(n, CT)],
                                             start=True, stop=True).then_inc(q_mm, 1)

                        pe.sem_inc(v_mm, FREE)
                        pe.sem_inc(turned, FREE)
                        pipeline(pe, [(1, turn), (2, project)])

                    @block.scalar
                    def _(act):
                        def keep(n, u):
                            act.wait_ge(turned, n + (1 + FREE))
                            nc.scalar.copy(XNT[:, span(n, CT)], bank[4 * u + 3][:, :]).then_inc(kept, 1)

                        def halves(n, u):
                            act.wait_ge(stored[u], (n - u) * (16 * NSTORE // 2) + 16 * NSTORE)
                            act.wait_ge(k_mm, n + 1)
                            nc.scalar.activation(HL[:, u, 2, :], bank[4 * u + 1][:, :], ACT.Identity,
                                                 bias=bqk[:, L, 1:2]).then_inc(hi, 1)
                            act.wait_ge(v_mm, n + (1 + FREE))
                            nc.scalar.copy(VS[:, u, :, 0:DK],
                                           bank[4 * u + 2][:, :].rearrange("p (m d) -> p m d", d=DK)).then_inc(vc, 1)
                            act.wait_ge(q_mm, n + 1)
                            nc.scalar.activation(HL[:, u, 0, :], bank[4 * u][:, :], ACT.Identity,
                                                 bias=bqk[:, L, 0:1]).then_inc(hi, 1)

                        act.sem_inc(vc, FREE)
                        act.sem_inc(kept, FREE)
                        for u in range(2):
                            act.sem_inc(stored[u], 16 * NSTORE)
                        act.wait_ge(ones, 1)
                        pipeline(act, [(1, keep), (2, halves)])

                    @block.vector
                    def _(dve):
                        def normalise(n, u):
                            dve.wait_ge(turned, n + 1)
                            for j in range(CB):
                                b = span(n * CB + j, 1)
                                ins = nc.vector.tensor_scalar(XN[:, u, j, :], X[:, b, :], MEAN[:, b], RSTD[:, b],
                                                              ALU.subtract, ALU.mult)
                            ins.then_inc(normed, 1)

                        def lows(n, u):
                            for k, part in enumerate((1, 0)):
                                dve.wait_ge(hi, n * 2 + (k + 1))
                                nc.vector.scalar_tensor_tensor(
                                    HL[:, u, 2 * part + 1, :], bank[4 * u + part][:, :], bqk[:, L, part:part + 1],
                                    HL[:, u, 2 * part, :], ALU.add, ALU.subtract).then_inc(lo, 1)

                        dve.sem_inc(lo, 2 * FREE)
                        pipeline(dve, [(0, normalise), (2, lows)])

        def attention(L, qk, vs):
            t = f"L{L}"
            causal = L == 1
            with ExitStack() as own:
                def osb(name, shape, dt=F32):
                    return own.enter_context(nc.sbuf_tensor(f"{name}{L}", shape, dt))
                VR = osb("VR", [P, 2, CB, H, VW])
                M = osb("M", [P, 2, H])
                MT = osb("MT", [H, 2, S], F16)
                PT = osb("PT", [P, 4, HG * S])
                OT = osb("OT", [P, 2, HG * S])
                REC = osb("REC", [P, 2, H])
                OQ = osb("OQ", [P, 2, D])
                OF = osb("OF", [P, 2, S])
                s_mm, maxed = sem(f"scores_ready_{t}"), sem(f"maxima_taken_{t}")
                m_turned, m_kept = sem(f"maxima_turned_{t}"), sem(f"maxima_kept_{t}")
                m_in = [sem(f"maxima_row_loaded{u}_{t}") for u in range(2)]
                st_mm, exped = sem(f"scores_T_ready_{t}"), sem(f"probs_ready_{t}")
                pv = sem(f"pv_done_{t}")
                ot_kept, turned = sem(f"out_T_kept_{t}"), sem(f"out_turned_{t}")
                recd, normed = sem(f"denominators_inverted_{t}"), sem(f"out_normalised_{t}")
                of_turned, of_kept = sem(f"out_F_turned_{t}"), sem(f"out_F_kept_{t}")
                proj, added = sem(f"out_projected_{t}"), sem(f"residual_added_{t}")
                otz, hidden = sem(f"out_banks_zeroed_{t}"), sem(f"probs_hidden_{t}")
                taken = sem(f"probs_taken_{t}")
                NMAX = 1 + HG
                NPROB = 3 + 3 * HG + 1
                STEPS = B + 6
                LO, HI = 6, 30

                def steps(eng, step):
                    for s in range(LO):
                        step(s, s, False)
                    with every(eng, LO, HI, 8) as s0:
                        for u in range(8):
                            step(s0 + u if u else s0, (LO + u) % 8, True)
                    for s in range(HI, STEPS):
                        step(s, s % 8, False)

                def alive(s, loop, lag):
                    return loop or 0 <= s - lag < B

                def wait(eng, semaphore, s, loop, scale, offset):
                    if loop or scale * s + offset > 0:
                        eng.wait_ge(semaphore, s * scale + offset)

                with nc.Block() as block:
                    if causal:
                        @block.gpsimd
                        def _(pool):
                            def hide(s, r, loop, g):
                                probs = PT[:, g, :].rearrange("p (h t) -> p h t", h=HG)
                                wait(pool, exped, s, loop, NG, g + 1)
                                pool.sem_inc(taken, 1)
                                nc.gpsimd.affine_select(probs[:, :, 1:], probs[:, :, 1:], [[0, HG], [1, S - 1]],
                                                        ALU.is_gt, 0.0, base=1, channel_multiplier=-1)
                                nc.gpsimd.affine_select(probs[:, :, 0:1], probs[:, :, 0:1], [[0, HG], [0, 1]],
                                                        ALU.is_ge, 0.0, base=0,
                                                        channel_multiplier=-1).then_inc(hidden, 1)

                            def step(s, r, loop):
                                for g in range(NG):
                                    if alive(s, loop, 3):
                                        hide(s - 3, (r - 3) % 8, loop, g)

                            steps(pool, step)

                    @block.sync
                    def _(sp):
                        MAXIMA_SHARE = [0, 0, 1, 5]
                        PROBS_SHARE = [0, 7, 12, 15]

                        def v_load(c, u):
                            return [(VR[:, u].rearrange("p b h v -> p (b h v)"), vs[:, span(c, CB * H * VW)])]

                        def store_maxima(s, r, loop):
                            u, tok = r // CB, slice(r % CB * S, (r % CB + 1) * S)
                            wait(sp, m_kept, s, loop, 1, 1)
                            sp.dma_start(QD[u][MROW:MROW + 1, :, :, tok].rearrange("p g h t -> p (g h) t"),
                                         MT[:, r % 2, :]).then_inc(m_in[r % 2], 16)

                        def step(k, i, u, maxima=True, start=True, finish=True):
                            later = not isinstance(k, int) or k > 0
                            if i or later:
                                s, r = k * CB + (i - 1), (u * CB + i - 1) % 8
                                store_maxima(s, r, not isinstance(k, int))
                            if maxima and i < 3:
                                if i == 0 and later:
                                    sp.wait_ge(s_mm, k * (CB * NG))
                                issue(sp, maxima_loads(qk, k + 1, 1 - u)[MAXIMA_SHARE[i]:MAXIMA_SHARE[i + 1]], max_in[L][1 - u])
                            if i < 2 and finish:
                                issue(sp, probs_loads(qk, k, u)[PROBS_SHARE[i + 1]:PROBS_SHARE[i + 2]], prob_in[L][u])
                            if i == 3 and start:
                                if later:
                                    sp.wait_ge(st_mm, k * (CB * NG))
                                issue(sp, probs_loads(qk, k + 1, 1 - u)[:PROBS_SHARE[1]], prob_in[L][1 - u])
                                if later:
                                    sp.wait_ge(pv, k * (CB * NG))
                                issue(sp, v_load(k + 1, 1 - u), prob_in[L][1 - u])

                        issue(sp, probs_loads(qk, 0, 0)[EARLY:] + v_load(0, 0), prob_in[L][0])
                        for i in range(CB):
                            step(0, i, 0, finish=False)
                        with every(sp, 1, NC - 1, 2) as k:
                            for u in (1, 0):
                                for i in range(CB):
                                    step(k if u else k + 1, i, u)
                        for i in range(CB):
                            step(NC - 1, i, 1, maxima=False, start=False)
                        store_maxima(B - 1, 7, False)

                    @block.tensor
                    def _(pe):
                        def scores(s, r, loop, g):
                            u, tok = r // CB, slice(r % CB * S, (r % CB + 1) * S)
                            if g == 0 and r % CB == 0:
                                wait(pe, max_in[L][u], s, loop, 2 * NMAX, 16 * NMAX - 2 * NMAX * r)
                            wait(pe, maxed, s, loop, NG, g - 1)
                            out = bank[g % 2][:, :]
                            if causal:
                                nc.tensor.matmul(out, identb, maskS, start=True, stop=False)
                            nc.tensor.matmul(out, QP[u][0:MROW, g, tok], KD[u][0:MROW, g, :, tok],
                                             start=not causal, stop=True).then_inc(s_mm, 1)

                        def scores_T(s, r, loop, g):
                            u, tok = r // CB, slice(r % CB * S, (r % CB + 1) * S)
                            if g == 0:
                                if r % CB == 0:
                                    wait(pe, prob_in[L][u], s, loop, 2 * NPROB, 16 * NPROB - 2 * NPROB * r)
                                wait(pe, m_in[r % 2], s, loop, 8, 16 - 8 * (r % 2))
                            wait(pe, exped, s, loop, NG, g - 1)
                            out = bank[2 + g % 2][:, :]
                            nc.tensor.matmul(out, KP[u][0:MROW + 1, g, tok], QD[u][0:MROW + 1, g, :, tok],
                                             start=True, stop=True).then_inc(st_mm, 1)

                        def turn_maxima(s, r, loop):
                            wait(pe, maxed, s, loop, NG, NG)
                            wait(pe, m_kept, s, loop, 1, 0)
                            wait(pe, normed, s, loop, 1, -3)
                            nc.tensor.transpose(bank[6][0:H, 0:S], M[:, r % 2, :], identf[:, :]).then_inc(m_turned, 1)

                        def product_v(s, r, loop, g):
                            wait(pe, hidden if causal else exped, s, loop, NG, g + 1)
                            if not loop and s == 0 and g == 0:
                                pe.wait_ge(otz, 2)
                            if g == 0:
                                wait(pe, ot_kept, s, loop, 1, -1)
                            for h in range(HG):
                                ins = nc.tensor.matmul(bank[4 + r % 2][32 * h:32 * h + VW, g * S:(g + 1) * S],
                                                       VR[:, r // CB, r % CB, HG * g + h, :],
                                                       PT[:, g, h * S:(h + 1) * S], start=True, stop=True,
                                                       tile_position=(0, 32 * h))
                            ins.then_inc(pv, 1)

                        def turn_out(s, r, loop):
                            wait(pe, ot_kept, s, loop, 1, 1)
                            if loop or s + 3 < B:
                                pe.wait_ge(m_kept, s + 4)
                            wait(pe, normed, s, loop, 1, 0)
                            for g in range(NG):
                                ins = nc.tensor.transpose(bank[6][:, g * S:(g + 1) * S],
                                                          OT[:, r % 2, g * S:(g + 1) * S], identf[:, :])
                            ins.then_inc(turned, 1)

                        def turn_normed(s, r, loop):
                            wait(pe, normed, s, loop, 1, 1)
                            wait(pe, added, s, loop, 1, 0)
                            nc.tensor.transpose(bank[7][:, 0:S], OQ[:, r % 2, :], identf[:, :]).then_inc(of_turned, 1)

                        def project_out(s, r, loop):
                            wait(pe, of_kept, s, loop, 1, 1)
                            nc.tensor.matmul(bank[7][:, S:S + D], OF[:, r % 2, :], WO[:, L, :],
                                             start=True, stop=True).then_inc(proj, 1)

                        def step(s, r, loop):
                            def at(lag):
                                return s - lag if lag else s, (r - lag) % 8, loop
                            for g in range(NG):
                                if alive(s, loop, 0):
                                    scores(*at(0), g)
                                if alive(s, loop, 3):
                                    scores_T(*at(3), g)
                                if g == 1 and alive(s, loop, 1):
                                    turn_maxima(*at(1))
                                if g == 0 and alive(s, loop, 6):
                                    project_out(*at(6))
                                if g == 3 and alive(s, loop, 5):
                                    turn_normed(*at(5))
                                lag = 4 if g < 2 else 3
                                if alive(s, loop, lag):
                                    product_v(*at(lag), (g + 2) % NG)
                            if alive(s, loop, 4):
                                turn_out(*at(4))

                        steps(pe, step)

                    @block.vector
                    def _(dve):
                        def normalise(s, r, loop):
                            wait(dve, turned, s, loop, 1, 1)
                            wait(dve, of_turned, s, loop, 1, -1)
                            out = bank[6][:, :].rearrange("p (h v) -> p h v", v=32)
                            nc.vector.reciprocal(REC[:, r % 2, :].unsqueeze(2), out[:, :, DK:DK + 1]).then_inc(recd, 1)
                            wait(dve, recd, s, loop, 1, 1)
                            nc.vector.tensor_tensor(OQ[:, r % 2, :].rearrange("p (h d) -> p h d", d=DK), out[:, :, 0:DK],
                                                    REC[:, r % 2, :].unsqueeze(2).to_broadcast([P, H, DK]),
                                                    ALU.mult).then_inc(normed, 1)

                        def maxima(s, r, loop, g):
                            if g == 0:
                                wait(dve, m_turned, s, loop, 1, -1)
                            wait(dve, s_mm, s, loop, NG, g + 1)
                            nc.vector.tensor_reduce(M[:, r % 2, HG * g:HG * (g + 1)],
                                                    bank[g % 2][:, :].rearrange("p (h t) -> p h t", t=S),
                                                    AX.X, ALU.max).then_inc(maxed, 1)

                        def tokens(s, loop):
                            return X[:, ds(s, 1), :].rearrange("p o d -> p (o d)") if loop else X[:, s, :]

                        def residual(s, r, loop):
                            wait(dve, proj, s, loop, 1, 1)
                            xs = tokens(s, loop)
                            nc.vector.tensor_tensor(xs, bank[7][:, S:S + D], xs, ALU.add).then_inc(added, 1)

                        def statistics(s, r, loop):
                            wait(dve, added, s, loop, 1, 1)
                            st = STATS[:, ds(s, 1), :].rearrange("p o d -> p (o d)") if loop else STATS[:, s, :]
                            nc.vector.bn_stats(st, tokens(s, loop))

                        def extreme(s, loop, kept, op):
                            nc.vector.tensor_reduce(kept[:, span(s, 1)], tokens(s, loop), AX.X, op)

                        def step(s, r, loop):
                            for g in range(NG):
                                if g == 0 and alive(s, loop, 5):
                                    normalise(s - 5, (r - 5) % 8, loop)
                                if alive(s, loop, 0):
                                    maxima(s, r, loop, g)
                                if g == 0 and alive(s, loop, 6):
                                    residual(s - 6, (r - 6) % 8, loop)
                                if g == 1 and alive(s, loop, 6):
                                    statistics(s - 6, (r - 6) % 8, loop)
                                if not loop and s == 1 and g < 2:
                                    nc.vector.memset(bank[4 + g][:, :], 0.0).then_inc(otz, 1)
                                if L == 0 and g >= 2 and alive(s, loop, 6):
                                    extreme(s - 6, loop, *((XMAX, ALU.max) if g == 2 else (XMIN, ALU.min)))

                        steps(dve, step)

                    @block.scalar
                    def _(act):
                        def probs(s, r, loop, g):
                            wait(act, st_mm, s, loop, NG, g + 1)
                            wait(act, pv, s, loop, NG, g - 3)
                            nc.scalar.activation(PT[:, g, :], bank[2 + g % 2][:, :], ACT.Exp,
                                                 scale=SCALE).then_inc(exped, 1)

                        def keep_maxima(s, r, loop):
                            wait(act, m_turned, s, loop, 1, 1)
                            wait(act, m_in[r % 2], s, loop, 8, -8 * (r % 2))
                            nc.scalar.mul(MT[:, r % 2, :], bank[6][0:H, 0:S], -1.0 / MSCALE).then_inc(m_kept, 1)

                        def keep_out_T(s, r, loop):
                            wait(act, pv, s, loop, NG, NG)
                            wait(act, turned, s, loop, 1, -1)
                            nc.scalar.copy(OT[:, r % 2, :], bank[4 + r % 2][:, :]).then_inc(ot_kept, 1)

                        def keep_out_F(s, r, loop):
                            wait(act, of_turned, s, loop, 1, 1)
                            wait(act, proj, s, loop, 1, -1)
                            nc.scalar.copy(OF[:, r % 2, :], bank[7][:, 0:S]).then_inc(of_kept, 1)

                        def step(s, r, loop):
                            def at(lag):
                                return s - lag if lag else s, (r - lag) % 8, loop
                            for g in range(NG):
                                if alive(s, loop, 3):
                                    probs(*at(3), g)
                                if g == 1:
                                    if alive(s, loop, 1):
                                        keep_maxima(*at(1))
                                    if alive(s, loop, 4):
                                        keep_out_T(*at(4))
                            if alive(s, loop, 5):
                                keep_out_F(*at(5))

                        steps(act, step)

        SIG = sb("SIG", [P, 2])
        SW = sb("SW", [P, 2 * NI + 1])
        SWX = sb("SWX", [P, 2 * NI])
        SACT = sb("SACT", [P, 2])
        INV = sb("INV", [P, 2])
        AMX = sb("AMX", [P, 2, 2])
        WGT = sb("WGT", [P, 2, INNER], BF16)
        WDT = sb("WDT", [P, NI, D], BF16)
        SDB = sb("SDB", [P, D])

        def ffn_weights():
            with ExitStack() as own:
                WR = own.enter_context(nc.sbuf_tensor("WR", [P, 2 * NI, D], F32))
                WDR = own.enter_context(nc.sbuf_tensor("WDR", [P, INNER], F32))
                clips = own.enter_context(nc.sbuf_tensor("clips", [P, 2], F32))
                ISW = own.enter_context(nc.sbuf_tensor("ISW", [P, 2 * NI + 1], F32))
                sd_diag = own.enter_context(nc.sbuf_tensor("sd_diag", [P, D], F32))
                ffn_in, clips_in, packed_in, x_in = (sem(f"{n}_loaded") for n in ("ffn_weights", "clips", "packed", "x"))
                expd, chain, quantised = sem("clips_exped"), sem("prep_chain"), sem("weights_quantised")
                turned, made, padded = sem("weights_turned"), sem("biases_made"), sem("short_tiles_padded")
                full = sum(rows == P for rows in ROWS)
                ffn = []
                for k, name in enumerate(("w_gate", "w_up")):
                    ffn.append((WR[:, NI * k:NI * k + full, :],
                                w[name][0:P * full, :].rearrange("(i p) d -> p i d", p=P)))
                    ffn.append((WR[0:ROWS[-1], NI * k + full, :], w[name][P * full:INNER, :]))
                ffn.append((WDR[:, :], w["w_down"]))
                packed_loads = [(packed[:, :], consts["packed"]), (packedb[:, :], consts["packedb"]),
                                (bor[:, :, :], w["bo"])]
                with nc.Block() as block:
                    @block.sync
                    def _(sp):
                        for n in range(NC):
                            sp.dma_start(X[:, CB * n:CB * (n + 1), :],
                                         x[CB * n:CB * (n + 1)].rearrange("b s d -> s b d")).then_inc(x_in, 16)

                    @block.gpsimd
                    def _(pool):
                        for k in range(2):
                            nc.gpsimd.memset(WR[ROWS[-1]:P, NI * k + NI - 1, :], 0.0).then_inc(padded, 1)
                        nc.gpsimd.memset(HBUF[ROWS[-1]:P, NI - 1, :], 0.0).then_inc(padded, 1)
                        pool.wait_ge(padded, 3)
                        nc.gpsimd.memset(ARENA[:, 0:ZEROED], 0.0)

                    @block.vector
                    def _(dve):
                        count = [0]

                        def link(ins):
                            count[0] += 1
                            ins.then_inc(chain, 1)
                            dve.wait_ge(chain, count[0])

                        nc.vector.memset(onesf[:, :], 1.0).then_inc(made, 1)
                        dve.wait_ge(ffn_in, 16 * len(ffn))
                        dve.wait_ge(padded, 2)
                        nc.vector.tensor_reduce(SW[:, 0:2 * NI], WR[:, :, :], AX.X, ALU.max, apply_absolute_value=True)
                        link(nc.vector.tensor_reduce(SW[:, 2 * NI:], WDR[:, :], AX.X, ALU.max, apply_absolute_value=True))
                        link(nc.vector.tensor_scalar(SW[:, :], SW[:, :], 1.0 / QMAX, None, ALU.mult))
                        link(nc.vector.reciprocal(ISW[:, :], SW[:, :]))
                        for k in range(2 * NI):
                            m = WR[0:ROWS[k % NI], k, :]
                            nc.vector.tensor_scalar(m, m, ISW[0:ROWS[k % NI], k:k + 1], MAGIC, ALU.mult, ALU.add)
                        link(nc.vector.tensor_scalar(WDR[:, :], WDR[:, :], ISW[:, 2 * NI:], MAGIC, ALU.mult, ALU.add))
                        nc.vector.tensor_scalar(WR[:, :, :], WR[:, :, :], MAGIC, QMAX, ALU.subtract,
                                                ALU.min).then_inc(quantised, 1)
                        nc.vector.tensor_scalar(WDR[:, :], WDR[:, :], MAGIC, QMAX, ALU.subtract,
                                                ALU.min).then_inc(quantised, 1)
                        dve.wait_ge(packed_in, 16 * len(packed_loads))
                        nc.vector.tensor_scalar(sd_diag[:, :], identf, SW[:, 2 * NI:], None, ALU.mult).then_inc(made, 1)
                        for L in range(2):
                            nc.vector.tensor_scalar(BVW[:, L, :], identf, 0.0, bvc[:, L:L + 1],
                                                    ALU.mult, ALU.add).then_inc(made, 1)
                        dve.wait_ge(x_in, 16 * NC)
                        for b in range(B):
                            nc.vector.bn_stats(STATS[:, b, :], X[:, b, :])
                        dve.wait_ge(expd, 1)
                        link(nc.vector.tensor_scalar(SIG[:, :], SIG[:, :], 1.0, None, ALU.add))
                        link(nc.vector.reciprocal(SIG[:, :], SIG[:, :]))

                    @block.scalar
                    def _(act):
                        for dst, src in ffn:
                            act.dma_start(dst, src).then_inc(ffn_in, 16)
                        for dst, src in packed_loads:
                            act.dma_start(dst, src).then_inc(packed_in, 16)
                        for n, name in enumerate(("clip_x", "clip_down")):
                            act.dma_start(clips[:, n:n + 1], w[name].partition_broadcast(P)).then_inc(clips_in, 16)
                        act.wait_ge(clips_in, 32)
                        nc.scalar.activation(SIG[:, :], clips[:, :], ACT.Exp, scale=-1.0).then_inc(expd, 1)
                        act.wait_ge(turned, 1)
                        for k in range(2):
                            nc.scalar.copy(WGT[:, k, :], bank[k][:, 0:INNER])
                        nc.scalar.copy(WDT[:, 0:NI - 1, :], bank[2][:, 0:(NI - 1) * D])
                        nc.scalar.copy(WDT[0:ROWS[-1], NI - 1, :], bank[3][0:ROWS[-1], 0:D])
                        nc.scalar.copy(SDB[:, :], bank[4][:, 0:D])
                        for L in range(2):
                            nc.scalar.copy(BO[:, L, :], bank[5 + L][:, 0:D])

                    @block.tensor
                    def _(pe):
                        pe.wait_ge(packed_in, 16 * len(packed_loads))
                        pe.wait_ge(quantised, 2)
                        for k in range(2):
                            for i, rows in enumerate(ROWS):
                                nc.tensor.transpose(bank[k][:, P * i:P * i + rows], WR[0:rows, NI * k + i, :],
                                                    identf[0:rows, 0:rows])
                        for i, rows in enumerate(ROWS):
                            out = bank[2][:, P * i:P * (i + 1)] if i < NI - 1 else bank[3][0:rows, 0:D]
                            nc.tensor.transpose(out, WDR[:, P * i:P * i + rows], identf)
                        pe.wait_ge(made, 4)
                        nc.tensor.matmul(bank[4][:, 0:D], onesf[:, :], sd_diag[:, :], start=True, stop=True)
                        for L in range(2):
                            nc.tensor.matmul(bank[5 + L][:, 0:D], BVW[:, L, :], WO[:, L, :], start=True, stop=False)
                            ins = nc.tensor.matmul(bank[5 + L][:, 0:D], onesf[0:1, :], bor[:, L, :],
                                                   start=False, stop=True)
                        ins.then_inc(turned, 1)

        def ffn():
            with ExitStack() as own:
                def osb(name, shape, dt=F32):
                    return own.enter_context(nc.sbuf_tensor(name, shape, dt))
                XN = osb("XNF", [P, 2, CB, D])
                QX = osb("QX", [P, 2, CB, D])
                XQ = osb("XQ", [P, 2, CT], BF16)
                SL = osb("SL", [P, 2, CT])
                HQ = osb("HQ", [P, 2, NI, CT], BF16)
                YB = osb("YB", [P, 2, CT])
                CM = osb("CM", [P, NC])
                input_amax()
                ffn_up(XN, QX, XQ, SL, CM)
                hidden_amax(CM)
                ffn_down(HQ, YB)

        def whole_amax(which, maxed, reduced, pool):
            pool.wait_ge(maxed, 1)
            nc.gpsimd.partition_all_reduce(AMX[:, which, 1:2], AMX[:, which, 0:1], P, ABSMAX).then_inc(reduced, 1)

        def activation_scale(which, reduced, scaled, dve):
            dve.wait_ge(reduced, 1)
            nc.vector.tensor_scalar(SACT[:, which:which + 1], AMX[:, which, 1:2], SIG[:, which:which + 1],
                                    1.0 / QMAX, ALU.mult, ALU.mult).then_inc(scaled, 1)
            dve.wait_ge(scaled, 1)
            nc.vector.reciprocal(INV[:, which:which + 1], SACT[:, which:which + 1])

        def input_amax():
            chain, maxed, reduced, scaled = sem("x_amax_step"), sem("x_amax_part"), sem("x_amax_all"), sem("x_scale")
            with nc.Block() as block:
                @block.vector
                def _(dve):
                    nc.vector.tensor_tensor(XMAX[:, :], XMAX[:, :], MEAN[:, :], ALU.subtract)
                    nc.vector.tensor_tensor(XMIN[:, :], MEAN[:, :], XMIN[:, :], ALU.subtract).then_inc(chain, 1)
                    dve.wait_ge(chain, 1)
                    nc.vector.tensor_tensor(XMAX[:, :], XMAX[:, :], XMIN[:, :], ALU.max).then_inc(chain, 1)
                    dve.wait_ge(chain, 2)
                    nc.vector.tensor_tensor(XMAX[:, :], XMAX[:, :], RSTD[:, :], ALU.mult).then_inc(chain, 1)
                    dve.wait_ge(chain, 3)
                    nc.vector.tensor_reduce(AMX[:, 0, 0:1], XMAX[:, :], AX.X, ALU.max).then_inc(maxed, 1)
                    activation_scale(0, reduced, scaled, dve)
                    for k in range(2 * NI):
                        rows = ROWS[k % NI]
                        nc.vector.tensor_scalar(SWX[0:rows, k:k + 1], SW[0:rows, k:k + 1], SACT[0:rows, 0:1],
                                                None, ALU.mult)

                @block.gpsimd
                def _(pool):
                    whole_amax(0, maxed, reduced, pool)

        def hidden_amax(CM):
            maxed, reduced, scaled = sem("h_amax_part"), sem("h_amax_all"), sem("h_scale")
            with nc.Block() as block:
                @block.vector
                def _(dve):
                    nc.vector.tensor_reduce(AMX[:, 1, 0:1], CM[:, :], AX.X, ALU.max).then_inc(maxed, 1)
                    activation_scale(1, reduced, scaled, dve)

                @block.gpsimd
                def _(pool):
                    whole_amax(1, maxed, reduced, pool)

        def ffn_up(XN, QX, XQ, SL, CM):
            FREE = 2
            centred, normed = sem("x_centred"), sem("x_normed")
            rounded, quant, turned, xq = sem("x_rounded"), sem("x_quantised"), sem("x_turned"), sem("x_integers")
            gate_mm, up_mm, silu, hid = sem("gate_mm"), sem("up_mm"), sem("silu_done"), sem("hidden_done")
            with nc.Block() as block:
                @block.vector
                def _(dve):
                    def clip(n, u):
                        dve.wait_ge(rounded, n + (1 + FREE))
                        nc.vector.tensor_scalar(QX[:, u], QX[:, u], MAGIC + QMAX, MAGIC - QMAX - 1.0,
                                                ALU.min, ALU.max).then_inc(quant, 1)

                    def hidden(n, u):
                        for i, rows in enumerate(ROWS):
                            k = (u + i) % 2
                            dve.wait_ge(up_mm, n * NI + (i + 1 + NI * FREE))
                            dve.wait_ge(silu, n * NI + (i + 1 + FREE))
                            nc.vector.scalar_tensor_tensor(HBUF[0:rows, i, span(n, CT)], bank[2 + k][0:rows, :],
                                                           SWX[0:rows, NI + i:NI + i + 1], SL[0:rows, k, :],
                                                           ALU.mult, ALU.mult).then_inc(hid, 1)

                    def chunk_max(n, u):
                        dve.wait_ge(hid, n * NI + (NI + FREE))
                        nc.vector.tensor_reduce(CM[:, span(n, 1)], HBUF[:, :, span(n, CT)], AX.XY, ALU.max,
                                                apply_absolute_value=True)

                    dve.sem_inc(hid, FREE)
                    pipeline(dve, [(1, clip), (3, chunk_max), (2, hidden)], peel=4)

                @block.gpsimd
                def _(pool):
                    def normalise(n, u):
                        pool.wait_ge(rounded, n + 1)
                        b = span(n, CB)
                        nc.gpsimd.tensor_tensor(XN[:, u], X[:, b, :], MEAN[:, b].unsqueeze(2).to_broadcast([P, CB, D]),
                                                ALU.subtract).then_inc(centred, 1)
                        pool.wait_ge(centred, n + 1)
                        nc.gpsimd.tensor_tensor(XN[:, u], XN[:, u], RSTD[:, b].unsqueeze(2).to_broadcast([P, CB, D]),
                                                ALU.mult).then_inc(normed, 1)

                    pipeline(pool, [(0, normalise)])

                @block.tensor
                def _(pe):
                    def turn(n, u):
                        pe.wait_ge(quant, n + 1)
                        pe.wait_ge(xq, n + 1)
                        for j in range(CB):
                            ins = nc.tensor.transpose(bank[6 + u][:, j * S:(j + 1) * S], QX[:, u, j, :], identf[:, :])
                        ins.then_inc(turned, 1)

                    def gate_up(*tiles):
                        def stage(n, u):
                            for i in tiles:
                                rows, k = ROWS[i], (u + i) % 2
                                if i == 0:
                                    pe.wait_ge(xq, n + (1 + FREE))
                                pe.wait_ge(silu, n * NI + (i + 1))
                                nc.tensor.matmul(bank[k][0:rows, :], WGT[:, 0, P * i:P * i + rows], XQ[:, u, :],
                                                 start=True, stop=True).then_inc(gate_mm, 1)
                                pe.wait_ge(hid, n * NI + (i + 1))
                                nc.tensor.matmul(bank[2 + k][0:rows, :], WGT[:, 1, P * i:P * i + rows], XQ[:, u, :],
                                                 start=True, stop=True).then_inc(up_mm, 1)
                        return stage

                    pe.sem_inc(turned, FREE)
                    pe.sem_inc(up_mm, NI * FREE)
                    pipeline(pe, [(2, gate_up(0, 1)), (1, turn), (2, gate_up(2))])

                @block.scalar
                def _(act):
                    def round_input(n, u):
                        act.wait_ge(normed, n + 1)
                        act.wait_ge(turned, n + 1)
                        nc.scalar.activation(QX[:, u], XN[:, u], ACT.Copy, bias=MAGIC,
                                             scale=INV[:, 0:1]).then_inc(rounded, 1)

                    def integers(n, u):
                        act.wait_ge(turned, n + (1 + FREE))
                        act.wait_ge(up_mm, n * NI + NI)
                        nc.scalar.activation(XQ[:, u, :], bank[6 + u][:, :], ACT.Copy, bias=-MAGIC).then_inc(xq, 1)

                    def gate_silu(*tiles):
                        def stage(n, u):
                            for i in tiles:
                                rows, k = ROWS[i], (u + i) % 2
                                act.wait_ge(gate_mm, n * NI + (i + 1))
                                act.wait_ge(hid, n * NI + (i + 1))
                                nc.scalar.activation(SL[0:rows, k, :], bank[k][0:rows, :], ACT.Silu,
                                                     scale=SWX[0:rows, i:i + 1]).then_inc(silu, 1)
                        return stage

                    act.sem_inc(rounded, FREE)
                    act.sem_inc(xq, FREE)
                    act.sem_inc(silu, FREE)
                    pipeline(act, [(2, gate_silu(0, 1)), (1, integers), (0, round_input), (2, gate_silu(2))])

        def ffn_down(HQ, YB):
            FREE = 2
            rounded, clipped, ints = sem("h_rounded"), sem("h_clipped"), sem("h_integers")
            down, scaled, added = sem("down_mm"), sem("down_scaled"), sem("ffn_added")
            last_ints = sem("h_last_integers")
            with nc.Block() as block:
                @block.scalar
                def _(act):
                    def round_hidden(n, u):
                        h = HBUF[:, :, span(n, CT)]
                        nc.scalar.activation(h, h, ACT.Copy, bias=MAGIC, scale=INV[:, 1:2]).then_inc(rounded, 1)

                    def integers(n, u):
                        act.wait_ge(down, n + 1)
                        act.wait_ge(clipped, n + 1)
                        nc.scalar.activation(HQ[:, u, 0:NI - 1], HBUF[:, 0:NI - 1, span(n, CT)], ACT.Copy,
                                             bias=-MAGIC).then_inc(ints, 1)

                    pipeline(act, [(0, round_hidden), (2, integers)])

                @block.vector
                def _(dve):
                    def clip(n, u):
                        h = HBUF[:, :, span(n, CT)]
                        dve.wait_ge(rounded, n + 1)
                        nc.vector.tensor_scalar(h, h, MAGIC + QMAX, MAGIC - QMAX - 1.0,
                                                ALU.min, ALU.max).then_inc(clipped, 1)

                    def last_integers(n, u):
                        dve.wait_ge(clipped, n + 1)
                        dve.wait_ge(down, n + 1)
                        nc.vector.tensor_scalar(HQ[:, u, NI - 1], HBUF[:, NI - 1, span(n, CT)], MAGIC, None,
                                                ALU.subtract).then_inc(last_ints, 1)

                    def scale_out(n, u):
                        dve.wait_ge(down, n + (1 + FREE))
                        dve.wait_ge(added, n + 1)
                        nc.vector.scalar_tensor_tensor(YB[:, u, :].rearrange("p (b d) -> p b d", d=D),
                                                       bank[u][:, :].rearrange("p (b d) -> p b d", d=D),
                                                       SACT[:, 1:2], SDB[:, :].unsqueeze(1).to_broadcast([P, CB, D]),
                                                       ALU.mult, ALU.mult).then_inc(scaled, 1)

                    def stats(n, u):
                        dve.wait_ge(added, n + (1 + FREE))
                        for j in range(CB):
                            b = n * CB + j
                            nc.vector.bn_stats(STATS[:, span(b, 1), :], X[:, span(b, 1), :])

                    dve.sem_inc(scaled, FREE)
                    pipeline(dve, [(0, clip), (2, last_integers), (3, scale_out), (4, stats)], peel=4)

                @block.gpsimd
                def _(pool):
                    def add(n, u):
                        pool.wait_ge(scaled, n + (1 + FREE))
                        xs = X[:, span(n, CB), :]
                        nc.gpsimd.tensor_tensor(xs, YB[:, u, :].rearrange("p (b d) -> p b d", d=D), xs,
                                                ALU.add).then_inc(added, 1)

                    pool.sem_inc(added, FREE)
                    pipeline(pool, [(0, add)])

                @block.tensor
                def _(pe):
                    def down_mm(n, u):
                        pe.wait_ge(ints, n + 1)
                        pe.wait_ge(last_ints, n + 1)
                        pe.wait_ge(scaled, n + 1)
                        for j in range(CB):
                            for i, rows in enumerate(ROWS):
                                ins = nc.tensor.matmul(bank[u][:, j * D:(j + 1) * D],
                                                       HQ[0:rows, u, i, j * S:(j + 1) * S], WDT[0:rows, i, :],
                                                       start=(i == 0), stop=(i == NI - 1))
                        ins.then_inc(down, 1)

                    pe.sem_inc(down, FREE)
                    pipeline(pe, [(0, down_mm)])

        moe_w = HBUF[:, :, :].rearrange("p i t -> p (i t)")
        n_w = (E + 1) * D
        w_raw = ARENA[:, 0:3 * n_w]
        w_hi, w_lo = (moe_w[:, 0:3 * n_w].bitcast(F16)[:, n * 3 * n_w:(n + 1) * 3 * n_w] for n in range(2))
        W1, W3, W2 = ([part[:, n * n_w:(n + 1) * n_w].rearrange("p (e i) -> p e i", i=D) for part in (w_hi, w_lo)]
                      for n in range(3))
        XH, XL = (ARENA[:, 16384:16384 + NT].bitcast(F16)[:, n * NT:(n + 1) * NT] for n in range(2))

        def router(gscr):
            FREE = 2
            with ExitStack() as own:
                def osb(name, shape, dt=F32):
                    return own.enter_context(nc.sbuf_tensor(name, shape, dt))
                GW = osb("GW", [P, E])
                XN = osb("XNR", [P, 2, CB, D])
                EB = osb("EB", [P, E])
                T8 = osb("T8", [P, B, 8])
                RAW, BI, GT_, EQ, SC, SC2 = (osb(n, [P, B, E]) for n in ("RAW", "BI", "GTR", "EQ", "SC", "SC2"))
                CNT = osb("CNT", [P, B])
                GO = osb("GO", [P, B * E])
                GTT = osb("GTT", [P, 4, P])
                LT = moe_w[0:E, 3 * n_w:3 * n_w + NT]
                w_in, gw_in = sem("experts_loaded"), sem("router_loaded")
                normed, turned, kept = sem("r_normed"), sem("r_turned"), sem("r_xnt_kept")
                x_hi, wt_hi = sem("tokens_hi_made"), sem("weights_hi_made")
                lg, lk, lt = sem("logits_T"), sem("logits_T_kept"), sem("logits")
                chain, ex = sem("router_chain"), sem("router_exp")
                g_ready, g_turned, g_kept, g_out = sem("gates"), sem("gates_turned"), sem("gates_kept"), sem("gates_stored")
                with nc.Block() as block:
                    @block.sync
                    def _(sp):
                        sp.dma_start(GW[:, :], w["gate_w"]).then_inc(gw_in, 16)
                        sp.dma_start(EB[:, :], w["expert_bias"].partition_broadcast(P)).then_inc(gw_in, 16)
                        for n, (a, b) in enumerate((("w1", "sw1"), ("w3", "sw3"), ("w2", "sw2"))):
                            dst = w_raw[:, n * n_w:(n + 1) * n_w].rearrange("p (e i) -> p e i", i=D)
                            sp.dma_start(dst[:, 0:E, :], w[a]).then_inc(w_in, 16)
                            sp.dma_start(dst[:, E, :], w[b]).then_inc(w_in, 16)
                        sp.wait_ge(g_kept, 1)
                        sp.dma_start(gscr.rearrange("T e k -> (T e k)").rearrange("(T p k) -> p T k", T=4, p=P),
                                     GTT[:, :, :]).then_inc(g_out, 16)
                        sp.wait_ge(g_out, 16)

                    @block.gpsimd
                    def _(pool):
                        def make_lo(n, u):
                            pool.wait_ge(x_hi, n + (1 + FREE))
                            nc.gpsimd.tensor_tensor(XL[:, span(n, CT)], XNT[:, span(n, CT)], XH[:, span(n, CT)],
                                                    ALU.subtract)

                        pipeline(pool, [(0, make_lo)])
                        for n in range(3):
                            pool.wait_ge(wt_hi, n + 1)
                            nc.gpsimd.tensor_tensor(w_lo[:, span(n, n_w)], w_raw[:, span(n, n_w)],
                                                    w_hi[:, span(n, n_w)], ALU.subtract)

                    @block.tensor
                    def _(pe):
                        def turn(n, u):
                            pe.wait_ge(normed, n + 1)
                            pe.wait_ge(x_hi, n + 1)
                            for j in range(CB):
                                ins = nc.tensor.transpose(bank[u][:, j * S:(j + 1) * S], XN[:, u, j, :], identf)
                            ins.then_inc(turned, 1)

                        def logits(n, u):
                            pe.wait_ge(kept, n + 1)
                            pe.wait_ge(lk, n + 1)
                            nc.tensor.matmul(bank[2 + u][0:E, :], GW[:, :], XNT[:, span(n, CT)],
                                             start=True, stop=True).then_inc(lg, 1)

                        pe.sem_inc(turned, FREE)
                        pe.wait_ge(gw_in, 32)
                        pipeline(pe, [(1, turn), (2, logits)])
                        pe.wait_ge(lk, NC + FREE)
                        for b in range(B):
                            ins = nc.tensor.transpose(bank[4][:, b * E:(b + 1) * E], LT[:, b * S:(b + 1) * S],
                                                      identf[0:E, 0:E])
                        ins.then_inc(lt, 1)
                        pe.wait_ge(g_ready, 1)
                        for n in range(4):
                            ins = nc.tensor.transpose(bank[5][:, n * P:(n + 1) * P], GO[:, n * P:(n + 1) * P], identf)
                        ins.then_inc(g_turned, 1)

                    @block.scalar
                    def _(act):
                        def keep(n, u):
                            act.wait_ge(turned, n + (1 + FREE))
                            nc.scalar.copy(XNT[:, span(n, CT)], bank[u][:, :]).then_inc(kept, 1)
                            nc.scalar.copy(XH[:, span(n, CT)], bank[u][:, :]).then_inc(x_hi, 1)

                        def keep_logits(n, u):
                            act.wait_ge(lg, n + 1)
                            nc.scalar.copy(LT[:, span(n, CT)], bank[2 + u][0:E, :]).then_inc(lk, 1)

                        act.sem_inc(x_hi, FREE)
                        act.sem_inc(lk, FREE)
                        pipeline(act, [(1, keep), (2, keep_logits)])
                        act.wait_ge(w_in, 16 * 6)
                        for n in range(3):
                            nc.scalar.copy(w_hi[:, span(n, n_w)], w_raw[:, span(n, n_w)]).then_inc(wt_hi, 1)
                        act.wait_ge(ex, 1)
                        nc.scalar.activation(EQ[:, :, :], SC[:, :, :], ACT.Exp).then_inc(ex, 1)
                        act.wait_ge(g_turned, 1)
                        nc.scalar.copy(GTT[:, :, :], bank[5][:, :]).then_inc(g_kept, 1)

                    @block.vector
                    def _(dve):
                        count = [0]

                        def link(ins):
                            count[0] += 1
                            ins.then_inc(chain, 1)
                            dve.wait_ge(chain, count[0])

                        def normalise(n, u):
                            dve.wait_ge(turned, n + 1)
                            for j in range(CB):
                                b = span(n * CB + j, 1)
                                ins = nc.vector.tensor_scalar(XN[:, u, j, :], X[:, b, :], MEAN[:, b], RSTD[:, b],
                                                              ALU.subtract, ALU.mult)
                            ins.then_inc(normed, 1)

                        pipeline(dve, [(0, normalise)])
                        full = [P, B, E]
                        dve.wait_ge(lt, 1)
                        dve.wait_ge(gw_in, 32)
                        link(nc.vector.tensor_copy(RAW[:, :, :], bank[4][:, :]))
                        link(nc.vector.tensor_tensor(BI[:, :, :], RAW[:, :, :],
                                                     EB[:, :].unsqueeze(1).to_broadcast(full), ALU.add))
                        for b in range(B):
                            ins = nc.vector.max(T8[:, b, :], BI[:, b, :])
                        link(ins)
                        fourth = T8[:, :, TOPK - 1:TOPK].to_broadcast(full)
                        nc.vector.tensor_tensor(GT_[:, :, :], BI[:, :, :], fourth, ALU.is_gt)
                        link(nc.vector.tensor_tensor(EQ[:, :, :], BI[:, :, :], fourth, ALU.is_equal))
                        link(nc.vector.tensor_reduce(CNT[:, :], GT_[:, :, :], AX.X, ALU.add))
                        link(nc.vector.tensor_scalar(CNT[:, :], CNT[:, :], -1.0, float(TOPK), ALU.mult, ALU.add))
                        a, b_ = EQ, SC
                        for k in (1, 2, 4, 8):
                            nc.vector.tensor_copy(b_[:, :, 0:k], a[:, :, 0:k])
                            link(nc.vector.tensor_tensor(b_[:, :, k:E], a[:, :, k:E], a[:, :, 0:E - k], ALU.add))
                            a, b_ = b_, (SC2 if b_ is SC else SC)
                        link(nc.vector.tensor_tensor(b_[:, :, :], a[:, :, :], CNT[:, :].unsqueeze(2).to_broadcast(full),
                                                     ALU.is_le))
                        link(nc.vector.tensor_tensor(EQ[:, :, :], EQ[:, :, :], b_[:, :, :], ALU.mult))
                        link(nc.vector.tensor_tensor(GT_[:, :, :], GT_[:, :, :], EQ[:, :, :], ALU.add))
                        link(nc.vector.tensor_scalar(SC[:, :, :], GT_[:, :, :], -1.0, BIG, ALU.add, ALU.mult))
                        link(nc.vector.tensor_tensor(SC[:, :, :], SC[:, :, :], RAW[:, :, :], ALU.add))
                        link(nc.vector.tensor_reduce(CNT[:, :], SC[:, :, :], AX.X, ALU.max))
                        nc.vector.tensor_tensor(SC[:, :, :], SC[:, :, :], CNT[:, :].unsqueeze(2).to_broadcast(full),
                                                ALU.subtract).then_inc(ex, 1)
                        dve.wait_ge(ex, 2)
                        link(nc.vector.tensor_reduce(CNT[:, :], EQ[:, :, :], AX.X, ALU.add))
                        link(nc.vector.reciprocal(CNT[:, :], CNT[:, :]))
                        nc.vector.tensor_tensor(GO[:, :].rearrange("p (T e n) -> p T n e", T=4, e=E),
                                                EQ[:, :, :].rearrange("p (T n) e -> p T n e", T=4),
                                                CNT[:, :].rearrange("p (T n) -> p T n", T=4).unsqueeze(3)
                                                .to_broadcast([P, 4, B // 4, E]), ALU.mult).then_inc(g_ready, 1)

        def experts(gscr):
            FREE = 2
            EN = E + 1
            ITEMS = 2 * EN
            GLOAD = 4
            with ExitStack() as own:
                def osb(name, shape, dt=F32):
                    return own.enter_context(nc.sbuf_tensor(name, shape, dt))
                G = [ARENA[:, n * E * CT:(n + 1) * E * CT].rearrange("p (e t) -> p e t", t=CT) for n in range(2)]
                SL = osb("SLE", [P, 2, CT])
                UG = osb("UG", [P, 2, CT])
                HE = osb("HE", [P, 2, CT])
                HH = osb("HH", [P, 2, CT], F16)
                HL = osb("HLE", [P, 2, CT], F16)
                XR = osb("XR", [P, 2, CB, D])
                YT = osb("YT", [P, 2, CT])
                g_in = [[sem(f"gates_loaded{u}_{q}") for q in range(E // GLOAD)] for u in range(2)]
                gate_mm, up_mm, down, y_mm = sem("e_gate_mm"), sem("e_up_mm"), sem("e_down_mm"), sem("y_mm")
                silu, gated, hid = sem("e_silu"), sem("e_gated"), sem("e_hidden")
                hid_hi, hid_lo = sem("e_hidden_hi"), sem("e_hidden_lo")
                xr, yk = sem("x_ringed"), sem("y_kept")
                stored = [sem(f"out_stored{u}") for u in range(2)]

                def passes(eng, stages):
                    def one(c, first=False):
                        for j in range(ITEMS):
                            for lag, stage in stages:
                                if not first or j >= lag:
                                    stage(c, j - lag)
                    one(0, True)
                    with every(eng, 2, NC, 2) as c:
                        one(c)
                    for j in range(max(lag for lag, _ in stages)):
                        for lag, stage in stages:
                            if j < lag:
                                stage(NC, j - lag)

                def chunk(c, j):
                    return c + j // EN if j // EN else c

                with nc.Block() as block:
                    @block.sync
                    def _(sp):
                        def load(pair, u, q):
                            es = slice(q * GLOAD, (q + 1) * GLOAD)
                            src = gscr[span(pair, 1), es, u * CT:(u + 1) * CT].rearrange("o e t -> (o e) t")
                            sp.dma_start(G[u][:, es, :], src.partition_broadcast(P)).then_inc(g_in[u][q], 16)

                        for u in range(2):
                            for q in range(E // GLOAD):
                                load(0, u, q)
                        with every(sp, 1, NC // 2, 1) as pair:
                            for u in range(2):
                                for q in range(E // GLOAD):
                                    sp.wait_ge(hid, pair * ITEMS + ((u - 2) * EN + (q + 1) * GLOAD + FREE))
                                    load(pair, u, q)

                    @block.gpsimd
                    def _(pool):
                        def make_lo(c, j):
                            k = j % 2
                            pool.wait_ge(hid_hi, c * EN + (j + 1))
                            nc.gpsimd.tensor_tensor(HL[:, k, :], HE[:, k, :], HH[:, k, :],
                                                    ALU.subtract).then_inc(hid_lo, 1)

                        pool.sem_inc(hid_lo, FREE)
                        passes(pool, [(0, make_lo)])

                    @block.tensor
                    def _(pe):
                        def product(out, weights, e, hi, lo, first, last, own_group=True):
                            nc.tensor.matmul(out, weights[0][:, e, :], hi, start=first, stop=False,
                                             skip_group_check=not own_group)
                            nc.tensor.matmul(out, weights[0][:, e, :], lo, start=False, stop=False,
                                             skip_group_check=not own_group)
                            return nc.tensor.matmul(out, weights[1][:, e, :], hi, start=False, stop=last,
                                                    skip_group_check=not own_group)

                        def gate_up(c, j):
                            k, e = j % 2, j % EN
                            tok = span(chunk(c, j), CT)
                            pe.wait_ge(silu, c * EN + (j + 1))
                            product(bank[k][:, :], W1, e, XH[:, tok], XL[:, tok], True, True).then_inc(gate_mm, 1)
                            pe.wait_ge(hid, c * EN + (j + 1))
                            product(bank[2 + k][:, :], W3, e, XH[:, tok], XL[:, tok], True, True).then_inc(up_mm, 1)

                        def down_mm(c, j):
                            k, e, u = j % 2, j % EN, j // EN % 2
                            pe.wait_ge(hid_lo, c * EN + (j + 1 + FREE))
                            if e == 0:
                                pe.wait_ge(yk, chunk(c, j) + 1)
                            product(bank[4 + u][:, :], W2, e, HH[:, k, :], HL[:, k, :], e == 0, False,
                                    own_group=False).then_inc(down, 1)
                            if e == EN - 1:
                                pe.wait_ge(xr, chunk(c, j) + 1)
                                for b in range(CB):
                                    ins = nc.tensor.matmul(bank[4 + u][:, b * S:(b + 1) * S], XR[:, u, b, :],
                                                           identf[:, :], start=False, stop=(b == CB - 1),
                                                           skip_group_check=True)
                                ins.then_inc(y_mm, 1)

                        pe.sem_inc(down, FREE)
                        pe.sem_inc(y_mm, FREE)
                        passes(pe, [(0, gate_up), (2, down_mm)])

                    @block.scalar
                    def _(act):
                        def keep_y(c, j):
                            n, u = chunk(c, j), j // EN % 2
                            act.wait_ge(y_mm, n + (1 + FREE))
                            act.wait_ge(stored[u], (n - u) * 8 + 16)
                            nc.scalar.copy(YT[:, u, :], bank[4 + u][:, :]).then_inc(yk, 1)
                            act.wait_ge(yk, n + (1 + FREE))
                            act.dma_start(outT[:, span(n, CT)], YT[:, u, :]).then_inc(stored[u], 16)

                        def make_silu(c, j):
                            k = j % 2
                            act.wait_ge(gate_mm, c * EN + (j + 1))
                            act.wait_ge(hid, c * EN + (j + 1))
                            nc.scalar.activation(SL[:, k, :], bank[k][:, :], ACT.Silu).then_inc(silu, 1)
                            if j % EN == 7:
                                act.wait_ge(y_mm, chunk(c, j) + 1)
                                nc.scalar.copy(XR[:, j // EN], X[:, span(chunk(c, j), CB), :]).then_inc(xr, 1)

                        def make_hi(c, j):
                            k = j % 2
                            act.wait_ge(hid, c * EN + (j + 1 + FREE))
                            act.wait_ge(down, c * EN + (j + 1))
                            nc.scalar.copy(HH[:, k, :], HE[:, k, :]).then_inc(hid_hi, 1)
                            if j % EN == 4 and not (isinstance(c, int) and c == 0 and j == 4):
                                keep_y(c, j - EN)

                        act.sem_inc(silu, FREE)
                        act.sem_inc(yk, FREE)
                        for u in range(2):
                            act.sem_inc(stored[u], 16)
                        passes(act, [(0, make_silu), (1, make_hi)])
                        keep_y(NC, -1)
                        for u in range(2):
                            act.wait_ge(stored[u], 16 * (NC // 2 + 1))

                    @block.vector
                    def _(dve):
                        def hidden(c, j):
                            k, e, u = j % 2, j % EN, j // EN
                            if e < E and e % GLOAD == 0:
                                dve.wait_ge(g_in[u][e // GLOAD], c * 8 + 16)
                            dve.wait_ge(up_mm, c * EN + (j + 1))
                            up = bank[2 + k][:, :]
                            if e < E:
                                nc.vector.tensor_tensor(UG[:, k, :], up, G[u][:, e, :], ALU.mult).then_inc(gated, 1)
                                up = UG[:, k, :]
                                dve.wait_ge(gated, (c + u) * E + (e + 1))
                            dve.wait_ge(silu, c * EN + (j + 1 + FREE))
                            dve.wait_ge(hid_lo, c * EN + (j + 1))
                            nc.vector.tensor_tensor(HE[:, k, :], up, SL[:, k, :], ALU.mult).then_inc(hid, 1)

                        dve.sem_inc(hid, FREE)
                        passes(dve, [(0, hidden)])

        qk = [nc.dram_tensor(f"qk_scratch{L}", [4, P, NT], F16, kind="Internal").ap() for L in range(2)]
        vs = [nc.dram_tensor(f"v_scratch{L}", [P, B * H * VW], F32, kind="Internal").ap() for L in range(2)]
        gscr = nc.dram_tensor("gates_scratch", [4, E, 2 * CT], F32, kind="Internal").ap()

        ffn_weights()
        ln_stats("a0")
        projections(0, qk[0], vs[0])
        attention(0, qk[0], vs[0])
        ln_stats("f0")
        ffn()
        ln_stats("a1")
        projections(1, qk[1], vs[1])
        attention(1, qk[1], vs[1])
        ln_stats("f1")
        router(gscr)
        experts(gscr)


def kernel(**inputs):
    import ml_dtypes
    import numpy as np
    import concourse.bacc as bacc
    from concourse.bass_utils import run_bass_kernel_spmd

    a = {k: np.asarray(v) for k, v in inputs.items()}
    i = np.arange(S)
    hidden = i[:, None] <= i[None, :]
    hidden[0, 0] = False
    neg = np.where(hidden, -BIG, 0.0)
    columns = [np.eye(P, dtype=np.float32)]
    columns += [a[f"L{L}_xattn_W{n}"].T for n in "qkvo" for L in range(2)]
    columns += [a["L0_xattn_bq"].reshape(D, 1), a["L0_xattn_bk"].reshape(D, 1), np.zeros((D, 2), np.float32)]
    columns += [a[f"L{L}_xattn_bv"].reshape(D, 1) for L in range(2)]
    arrays = {
        "x": a["x"],
        "ctxT": a["ctx_1024"].reshape(NT, D).T,
        "packed": np.concatenate(columns, 1),
        "packedb": np.concatenate([np.eye(P)] + [neg] * HG, 1).astype(ml_dtypes.bfloat16),
        "bo": np.stack([a[f"L{L}_xattn_bo"] for L in range(2)])[None],
        "clip_x": a["L0_ffn_clip_x"], "clip_down": a["L0_ffn_clip_down"],
        "w_gate": a["L0_ffn_w_gate"], "w_up": a["L0_ffn_w_up"], "w_down": a["L0_ffn_w_down"],
        "gate_w": a["L1_ffn_gate_w"].T, "expert_bias": a["L1_ffn_expert_bias"],
        "w1": a["L1_ffn_w1"].transpose(2, 0, 1), "w3": a["L1_ffn_w3"].transpose(2, 0, 1),
        "w2": a["L1_ffn_w2"].transpose(2, 0, 1),
        "sw1": a["L1_ffn_sw1"].T, "sw3": a["L1_ffn_sw3"].T, "sw2": a["L1_ffn_sw2"].T,
    }
    nc = bacc.Bacc("TRN2", target_bir_lowering=False, num_devices=1)
    fed, aps = {}, {}
    for name, array in arrays.items():
        array = np.ascontiguousarray(array)
        fed[f"in_{name}"] = array
        aps[name] = nc.dram_tensor(f"in_{name}", array.shape, mybir.dt.from_np(array.dtype), kind="ExternalInput").ap()
    outT = nc.dram_tensor("outT", (D, NT), F32, kind="ExternalOutput").ap()
    consts = {k: aps.pop(k) for k in ("packed", "packedb")}
    build(nc, aps.pop("x"), aps.pop("ctxT"), aps, consts, outT)
    r = run_bass_kernel_spmd(nc, [fed], core_ids=[0])
    return np.ascontiguousarray(r.results[0]["outT"].T).reshape(B, S, D)
```
